# Optimizing a Trainium2 kernel written in Bass

```python
import numpy as np
import jax
import jax.numpy as jnp

def _softmax(x, axis=-1):
    return jax.nn.softmax(x, axis=axis)

def _gelu(x):
    return jax.nn.gelu(x, approximate=True)

def _silu(x):
    return jax.nn.silu(x)

def _sigmoid(x):
    return jax.nn.sigmoid(x)

def _layernorm(x, axis=-1, eps=1e-05):
    m = jnp.mean(x, axis=axis, keepdims=True)
    v = jnp.var(x, axis=axis, keepdims=True)
    return (x - m) / jnp.sqrt(v + eps)

def _scatter_add(tgt, idx, src, axis=0):
    return tgt.at[idx].add(src)

def _segment_sum(src, seg, n):
    return jax.ops.segment_sum(src, seg, n)
kernel_name = 'mk_adj_resnorm_d4_adj_r2_c1952c'

def setup_inputs(seed: int=0):
    np.random.seed(seed)
    _w = jnp.asarray

    def _rec_inputs():
        import jax
        import jax.numpy as jnp
        _gk = jax.random.key(seed)
        x = 7.22e-05 + 1 * jax.random.normal(jax.random.fold_in(_gk, 1), (64, 128, 512), jnp.float32)
        _a = jax.random.bernoulli(jax.random.fold_in(_gk, 2), 0.015625, (128, 128))
        _a = jnp.logical_or(_a, jnp.swapaxes(_a, -1, -2))
        _a = jnp.logical_or(_a, jnp.eye(128, dtype=bool))
        _af = _a.astype(jnp.float32)
        _af = _af * jax.random.uniform(jax.random.fold_in(_gk, 3), (128, 128), jnp.float32, 0.05, 0.108252)
        adj = _af
        return (x, adj)
    x, adj = _rec_inputs()

    def _L0_gnn_setup():
        import jax, jax.numpy as jnp
        import numpy as np

        def _ada_gcn(xn, weight, bias):
            N, B, L = xn.shape
            x_norm = xn / jnp.maximum(jnp.linalg.norm(xn, axis=-1, keepdims=True), 1e-12)
            mean_sim = jnp.einsum('nbl,mbl->nm', x_norm, x_norm) / B
            k = max(int(N * 0.3), 1)
            _, idx = jax.lax.top_k(mean_sim, k + 1)
            rows = jnp.arange(N)[:, None]
            non_self = idx != rows
            order = jnp.cumsum(non_self.astype(jnp.int32), axis=1) - 1
            keep = non_self & (order < k)
            mask = jnp.zeros((N, N), dtype=bool).at[jnp.broadcast_to(rows, idx.shape), idx].set(keep)
            A = jnp.where(mask, mean_sim, jnp.zeros((), mean_sim.dtype))
            deg = A.sum(axis=0)
            dinv = jnp.where(deg > 0, jax.lax.rsqrt(deg), jnp.zeros((), deg.dtype))
            An = dinv[:, None] * A * dinv[None, :]
            xw = jnp.einsum('nbl,lo->nbo', xn, weight)
            out = jnp.einsum('sd,sbl->dbl', An, xw) + bias
            return out
        key = jax.random.key(seed)
        k1, k2 = jax.random.split(key)
        B, L, N = (32, 128, 512)
        x = jax.random.normal(k1, (B, L, N), dtype=jnp.float32)
        limit = float(np.sqrt(6.0 / (L + L)))
        weight = jax.random.uniform(k2, (L, L), dtype=jnp.float32, minval=-limit, maxval=limit)
        bias = jnp.zeros((L,), dtype=jnp.float32)
        return {'x': x, 'weight': weight, 'bias': bias}
    _L0_gnn_all = _L0_gnn_setup()
    _L0_gnn_in = {k: v for k, v in _L0_gnn_all.items() if k in ('bias',)}
    del _L0_gnn_all

    def _L1_gnn_setup():
        import jax, jax.numpy as jnp
        import numpy as np
        DIM = 199
        K_HOP = 3

        def _khop_support(n, k):
            A = np.eye(n, dtype=np.float64)
            idx = np.arange(n)
            A[idx, (idx + 1) % n] = 1.0
            A[(idx + 1) % n, idx] = 1.0
            S = np.linalg.matrix_power(A, k)
            return (S > 0).astype(np.float32)
        key = jax.random.key(seed)
        kx, kk = jax.random.split(key)
        batch, n, f = (128, DIM, 512)
        x = jax.random.normal(kx, (batch, n, f), dtype=jnp.float32)
        support = jnp.asarray(_khop_support(n, K_HOP))
        limit = float(np.sqrt(6.0 / (n + n)))
        kernel = jax.random.uniform(kk, (n, n), minval=-limit, maxval=limit, dtype=jnp.float32)
        bias = jnp.zeros((f,), dtype=jnp.float32)
        return {'x': x, 'support': support, 'kernel': kernel, 'bias': bias}
    _L1_gnn_all = _L1_gnn_setup()
    _L1_gnn_in = {k: v for k, v in _L1_gnn_all.items() if k in ('bias',)}
    del _L1_gnn_all

    def _L2_gnn_setup():
        import jax, jax.numpy as jnp
        import numpy as np
        DIM = 199
        K_HOP = 3

        def _khop_support(n, k):
            A = np.eye(n, dtype=np.float64)
            idx = np.arange(n)
            A[idx, (idx + 1) % n] = 1.0
            A[(idx + 1) % n, idx] = 1.0
            S = np.linalg.matrix_power(A, k)
            return (S > 0).astype(np.float32)
        key = jax.random.key(seed)
        kx, kk = jax.random.split(key)
        batch, n, f = (128, DIM, 512)
        x = jax.random.normal(kx, (batch, n, f), dtype=jnp.float32)
        support = jnp.asarray(_khop_support(n, K_HOP))
        limit = float(np.sqrt(6.0 / (n + n)))
        kernel = jax.random.uniform(kk, (n, n), minval=-limit, maxval=limit, dtype=jnp.float32)
        bias = jnp.zeros((f,), dtype=jnp.float32)
        return {'x': x, 'support': support, 'kernel': kernel, 'bias': bias}
    _L2_gnn_all = _L2_gnn_setup()
    _L2_gnn_in = {k: v for k, v in _L2_gnn_all.items() if k in ('bias',)}
    del _L2_gnn_all

    def _L3_gnn_setup():
        import jax, jax.numpy as jnp
        import numpy as np
        EPS = 1e-08

        def _row_stochastic_causal(A, causal_mask):
            A = A * causal_mask
            deg = jnp.maximum(A.sum(axis=-1, keepdims=True), EPS)
            return A / deg
        key = jax.random.key(seed)
        k = jax.random.split(key, 5)
        B, N, D = (4, 1024, 512)
        s = 1.0 / np.sqrt(D)
        h = jax.random.normal(k[0], (B, N, D), dtype=jnp.float32)
        W_lang = jax.random.normal(k[1], (D, D), dtype=jnp.float32) * s
        W_grav = jax.random.normal(k[2], (D, D), dtype=jnp.float32) * s
        W_V = jax.random.normal(k[3], (D, D), dtype=jnp.float32) * s
        W_O = jax.random.normal(k[4], (D, D), dtype=jnp.float32) * s
        causal_mask = jnp.tril(jnp.ones((N, N), dtype=jnp.float32))
        gate_logit = jnp.zeros((), jnp.float32)
        log_sigma = jnp.zeros((), jnp.float32)
        return {'h': h, 'causal_mask': causal_mask, 'W_lang': W_lang, 'W_grav': W_grav, 'W_V': W_V, 'W_O': W_O, 'gate_logit': gate_logit, 'log_sigma': log_sigma}
    _L3_gnn_all = _L3_gnn_setup()
    _L3_gnn_in = {k: v for k, v in _L3_gnn_all.items() if k in ('W_lang', 'W_grav', 'W_V', 'W_O', 'gate_logit', 'log_sigma')}
    del _L3_gnn_all
    return {'x': x, 'adj': adj, 'L0_gnn_bias': _L0_gnn_in['bias'], 'L1_gnn_bias': _L1_gnn_in['bias'], 'L2_gnn_bias': _L2_gnn_in['bias'], 'L3_gnn_W_lang': _L3_gnn_in['W_lang'], 'L3_gnn_W_grav': _L3_gnn_in['W_grav'], 'L3_gnn_W_V': _L3_gnn_in['W_V'], 'L3_gnn_W_O': _L3_gnn_in['W_O'], 'L3_gnn_gate_logit': _L3_gnn_in['gate_logit'], 'L3_gnn_log_sigma': _L3_gnn_in['log_sigma']}

def reference(x, adj, L0_gnn_bias, L1_gnn_bias, L2_gnn_bias, L3_gnn_W_lang, L3_gnn_W_grav, L3_gnn_W_V, L3_gnn_W_O, L3_gnn_gate_logit, L3_gnn_log_sigma):
    import jax
    import jax.numpy as jnp

    def _L0_gnn_ref(x, weight, bias):
        import jax, jax.numpy as jnp
        import numpy as np

        def _ada_gcn(xn, weight, bias):
            N, B, L = xn.shape
            x_norm = xn / jnp.maximum(jnp.linalg.norm(xn, axis=-1, keepdims=True), 1e-12)
            mean_sim = jnp.einsum('nbl,mbl->nm', x_norm, x_norm) / B
            k = max(int(N * 0.3), 1)
            _, idx = jax.lax.top_k(mean_sim, k + 1)
            rows = jnp.arange(N)[:, None]
            non_self = idx != rows
            order = jnp.cumsum(non_self.astype(jnp.int32), axis=1) - 1
            keep = non_self & (order < k)
            mask = jnp.zeros((N, N), dtype=bool).at[jnp.broadcast_to(rows, idx.shape), idx].set(keep)
            A = jnp.where(mask, mean_sim, jnp.zeros((), mean_sim.dtype))
            deg = A.sum(axis=0)
            dinv = jnp.where(deg > 0, jax.lax.rsqrt(deg), jnp.zeros((), deg.dtype))
            An = dinv[:, None] * A * dinv[None, :]
            xw = jnp.einsum('nbl,lo->nbo', xn, weight)
            out = jnp.einsum('sd,sbl->dbl', An, xw) + bias
            return out
        xn = jnp.transpose(x, (2, 0, 1))
        num_levels = 1
        for _ in range(num_levels):
            xn = _ada_gcn(xn, weight, bias)
        return jnp.transpose(xn, (1, 2, 0))

    def _L1_gnn_ref(x, support, kernel, bias):
        import jax, jax.numpy as jnp
        import numpy as np
        DIM = 199
        K_HOP = 3

        def _khop_support(n, k):
            A = np.eye(n, dtype=np.float64)
            idx = np.arange(n)
            A[idx, (idx + 1) % n] = 1.0
            A[(idx + 1) % n, idx] = 1.0
            S = np.linalg.matrix_power(A, k)
            return (S > 0).astype(np.float32)
        W = support * kernel
        out = jnp.einsum('bnf,nm->bmf', x, W)
        out = out + bias
        return out

    def _L2_gnn_ref(x, support, kernel, bias):
        import jax, jax.numpy as jnp
        import numpy as np
        DIM = 199
        K_HOP = 3

        def _khop_support(n, k):
            A = np.eye(n, dtype=np.float64)
            idx = np.arange(n)
            A[idx, (idx + 1) % n] = 1.0
            A[(idx + 1) % n, idx] = 1.0
            S = np.linalg.matrix_power(A, k)
            return (S > 0).astype(np.float32)
        W = support * kernel
        out = jnp.einsum('bnf,nm->bmf', x, W)
        out = out + bias
        return out

    def _L3_gnn_ref(h, causal_mask, W_lang, W_grav, W_V, W_O, gate_logit, log_sigma):
        import jax, jax.numpy as jnp
        import numpy as np
        EPS = 1e-08

        def _row_stochastic_causal(A, causal_mask):
            A = A * causal_mask
            deg = jnp.maximum(A.sum(axis=-1, keepdims=True), EPS)
            return A / deg
        z_l = jnp.einsum('bnd,ed->bne', h, W_lang)
        z_g = jnp.einsum('bnd,ed->bne', h, W_grav)
        v = jnp.einsum('bnd,ed->bne', h, W_V)
        N = h.shape[-2]
        not_eye = 1.0 - jnp.eye(N, dtype=h.dtype)
        zn = z_l / jnp.maximum(jnp.linalg.norm(z_l, axis=-1, keepdims=True), EPS)
        A_l = jnp.maximum(jnp.einsum('bnd,bmd->bnm', zn, zn), 0.0) * not_eye
        sq = jnp.sum(z_g * z_g, axis=-1, keepdims=True)
        d2 = jnp.maximum(sq + jnp.swapaxes(sq, -1, -2) - 2.0 * jnp.einsum('bnd,bmd->bnm', z_g, z_g), 0.0)
        sigma = jnp.exp(log_sigma)
        A_g = jnp.exp(-d2 / (2.0 * sigma * sigma)) * not_eye
        K_l = _row_stochastic_causal(A_l, causal_mask)
        K_g = _row_stochastic_causal(A_g, causal_mask)
        w_l = jax.nn.sigmoid(gate_logit)
        K = w_l * K_l + (1.0 - w_l) * K_g
        out = jnp.einsum('bnm,bmd->bnd', K, v)
        return jnp.einsum('bnd,ed->bne', out, W_O)
    x = _layernorm(x + _L0_gnn_ref(x, adj, L0_gnn_bias), axis=-1)
    x = _layernorm(x + _L1_gnn_ref(x, adj, adj, L1_gnn_bias), axis=-1)
    x = _layernorm(x + _L2_gnn_ref(x, adj, adj, L2_gnn_bias), axis=-1)
    x = _layernorm(x + _L3_gnn_ref(x, adj, L3_gnn_W_lang, L3_gnn_W_grav, L3_gnn_W_V, L3_gnn_W_O, L3_gnn_gate_logit, L3_gnn_log_sigma), axis=-1)
    return x

_drawn_inputs = setup_inputs


def setup_inputs(seed=0):
    import zlib

    import numpy as np

    out = dict(_drawn_inputs(seed))
    spreads = {'L0_gnn_bias': (0.0, 0.1), 'L1_gnn_bias': (0.0, 0.1), 'L2_gnn_bias': (0.0, 0.1)}
    factors = {}
    for name, (base, spread) in spreads.items():
        noise = np.random.default_rng([zlib.crc32(name.encode()), seed]).standard_normal(out[name].shape)
        drawn = base * np.exp(spread * noise) if base else spread * noise
        out[name] = jnp.asarray(drawn.astype(out[name].dtype))
    for name, factor in factors.items():
        out[name] = (out[name] * factor).astype(out[name].dtype)
    return out
```

```python
import concourse.bass as bass
from concourse import mybir
from contextlib import ExitStack

F32 = mybir.dt.float32
F16 = mybir.dt.float16
ALU = mybir.AluOpType
ACT = mybir.ActivationFunctionType
AX = mybir.AxisListType


def gnn_kernel(nc, x, adj, bias0, bias1, bias2, w_lang, w_grav, w_v, w_o, gate_logit, log_sigma, out):
    NB, L, N = x.shape
    P = 128
    assert L == P
    T = N // P
    G = 4
    NG = NB // G
    K_KEEP = max(int(N * 0.3), 1)
    TOP_ROUNDS = (K_KEEP - 1) // 8
    TOP_REST = K_KEEP - 8 * TOP_ROUNDS
    LN_EPS = 1e-05
    NORM_EPS = 1e-08
    NEG = -(2.0 ** 100)
    XN_SCALE = 2.0 ** 8
    ADJ_SCALE = 2.0 ** 10
    W1_SCALE = 2.0 ** 8
    XW_SCALE = 2.0 ** 6
    AN_SCALE = 2.0 ** 10
    P_SCALE = 2.0 ** 6
    M_SCALE = 2.0 ** 8
    K_SCALE = 2.0 ** 8

    ctx = ExitStack()
    with ctx:
        ctx.enter_context(nc.allow_non_contiguous_dma(reason="biases of one element per partition"))

        def sb(name, shape, dt):
            return ctx.enter_context(nc.sbuf_tensor(name, shape, dt))

        def sem(name):
            return ctx.enter_context(nc.semaphore(name))

        bank = [ctx.enter_context(nc.psum_tensor(f"bank{i}", [P, N], F32)) for i in range(8)]

        ident = sb("ident", [P, P], F32)
        ones = sb("ones", [P, P], F32)
        zeros = sb("zeros", [P, P], F32)
        not_eye = sb("not_eye", [P, P], F32)
        adj_sb = sb("adj_sb", [P, P], F32)
        adj_off = sb("adj_off", [P, P], F32)
        adj_s = sb("adj_s", [P, P], F32)
        adj_hi = sb("adj_hi", [P, P], F16)
        adj_lo = sb("adj_lo", [P, P], F16)
        w1_f = sb("w1_f", [P, P], F32)
        w1_hi = sb("w1_hi", [P, P], F16)
        w1_lo = sb("w1_lo", [P, P], F16)
        bias0_col = sb("bias0_col", [P, 1], F32)
        bias1_row = sb("bias1_row", [P, N], F32)
        bias2_row = sb("bias2_row", [P, N], F32)
        gate = sb("gate", [P, 8], F32)
        an_hi = sb("an_hi", [P, T, N], F16)
        an_lo = sb("an_lo", [P, T, N], F16)
        pg_hi = sb("pg_hi", [P, T, N], F16)
        pg_lo = sb("pg_lo", [P, T, N], F16)
        pl_hi = sb("pl_hi", [P, T, N], F16)
        pl_lo = sb("pl_lo", [P, T, N], F16)
        m_hi = sb("m_hi", [P, T, N], F16)
        m_lo = sb("m_lo", [P, T, N], F16)

        x_in = sb("x_in", [P, G, N], F32)
        xb = sb("xb", [P, G, N], F32)
        x_hi = sb("x_hi", [P, G, N], F16)
        x_lo = sb("x_lo", [P, G, N], F16)
        xw_hi = sb("xw_hi", [P, 2, N], F16)
        xw_lo = sb("xw_lo", [P, 2, N], F16)
        t_sb = sb("t_sb", [P, G, N], F32)
        y_f = sb("y_f", [P, G, N], F32)
        y_hi = sb("y_hi", [P, G, N], F16)
        y_lo = sb("y_lo", [P, G, N], F16)
        h_sb = sb("h_sb", [P, G, N], F32)
        ht_hi = sb("ht_hi", [P, T, N], F16)
        ht_lo = sb("ht_lo", [P, T, N], F16)
        yt_hi = sb("yt_hi", [P, 2, T, N], F16)
        yt_lo = sb("yt_lo", [P, 2, T, N], F16)
        u_hi = sb("u_hi", [P, G, N], F16)
        u_lo = sb("u_lo", [P, G, N], F16)
        t3 = sb("t3", [P, G, N], F32)
        o_sb = sb("o_sb", [P, G, N], F32)
        gram = sb("gram", [P, 2, N], F32)
        diag = sb("diag", [P, N], F32)
        dist = sb("dist", [P, N], F32)
        expo = sb("expo", [P, N], F32)
        a_g = sb("a_g", [P, N], F32)
        a_l = sb("a_l", [P, N], F32)
        k_g = sb("k_g", [P, N], F32)
        k_sb = sb("k_sb", [P, N], F32)
        kt_hi = sb("kt_hi", [P, N], F16)
        kt_lo = sb("kt_lo", [P, N], F16)
        stats = sb("stats", [P, 4, G, 6], F32)
        mv = sb("mv", [P, 4, G, 2], F32)
        half_var = sb("half_var", [P, 4, G], F32)
        ln_v = sb("ln_v", [P, 5, G], F32)
        r0 = sb("r0", [P, 5, G], F32)
        r_t = sb("r_t", [P, 5, G], F32)
        rstd = sb("rstd", [P, 5, G], F32)
        nmr = sb("nmr", [P, 4, G], F32)
        sq = sb("sq", [P, 2, G], F32)
        sq_h = sb("sq_h", [P, G], F32)
        deg = sb("deg", [P, 2, G], F32)
        deg_c = sb("deg_c", [P, 2, G], F32)
        inv_deg = sb("inv_deg", [P, 2, G], F32)
        coef = sb("coef", [P, 2, G], F32)

        xa = [x_in, xb]
        sqr = t_sb
        xn_f = y_f
        xn_hi, xn_lo = y_hi, y_lo
        ss = sb("ss", [P, G * T], F32)
        rs = sb("rs", [P, 4, G * T], F32)
        s_sb = h_sb
        work = t3
        a_sb = o_sb
        w_stage = [y_f, t_sb, xb, x_in]
        wot = yt_hi[:, :, :, :].rearrange("p a t n -> p (a t n)").bitcast(F32).rearrange(
            "p (t n) -> p t n", t=T)
        prod_f = yt_lo[:, :, :, :].rearrange("p a t n -> p (a t n)").bitcast(F32).rearrange(
            "p (t n) -> p t n", t=T)
        an_f = prod_f
        top8 = sb("top8", [P, T, 8], F32)
        held = sb("held", [P, 2], F32)
        dcol = sb("dcol", [P, 8, T], F32)

        const_set = sem("const_set")
        small_in = sem("small_in")
        xa_in = [sem("xa_in0"), sem("xa_in1")]
        squared = sem("squared")
        ss_done = sem("ss_done")
        rs_link = sem("rs_link")
        rs_sqrt = sem("rs_sqrt")
        rb_done = sem("rb_done")
        xn_done = sem("xn_done")
        xnhi_done = sem("xnhi_done")
        xnlo_done = sem("xnlo_done")
        sim_done = sem("sim_done")
        w_in = sem("w_in")
        s_copied = sem("s_copied")
        s_turned = sem("s_turned")
        s_mirrored = sem("s_mirrored")
        s_diag = sem("s_diag")
        top = sem("top")
        adj_made = sem("adj_made")
        a_done = sem("a_done")
        dg_done = sem("dg_done")
        dg_sqrt = sem("dg_sqrt")
        dg_link = sem("dg_link")
        db_done = sem("db_done")
        anf_done = sem("anf_done")
        anhi_done = sem("anhi_done")
        an_done = sem("an_done")
        wot_turned = sem("wot_turned")
        wot_done = sem("wot_done")
        prod_done = sem("prod_done")
        prod_hi = sem("prod_hi")
        prod_lo = sem("prod_lo")
        gate_exp = sem("gate_exp")
        gate_done = sem("gate_done")
        x3_in = sem("x3_in")
        xhi_done = sem("xhi_done")
        xlo_done = sem("xlo_done")
        xb_done = sem("xb_done")
        pe_xw = sem("pe_xw")
        xwhi_done = sem("xwhi_done")
        xwlo_done = sem("xwlo_done")
        pe_mix = sem("pe_mix")
        mix_used = sem("mix_used")
        stat_done = sem("stat_done")
        dve_link = sem("dve_link")
        act_link = sem("act_link")
        var_ready = sem("var_ready")
        r0_ready = sem("r0_ready")
        norm_ready = sem("norm_ready")
        yhi_done = sem("yhi_done")
        yf_done = sem("yf_done")
        ylo_done = sem("ylo_done")
        h_done = sem("h_done")
        pe_tr = sem("pe_tr")
        trhi_done = sem("trhi_done")
        tr_used = sem("tr_used")
        pe_wide = sem("pe_wide")
        widehi_done = sem("widehi_done")
        wide_used = sem("wide_used")
        pe_gram = sem("pe_gram")
        gram_done = sem("gram_done")
        sq_ready = sem("sq_ready")
        pe_bc = sem("pe_bc")
        dist_done = sem("dist_done")
        exp_done = sem("exp_done")
        ag_done = sem("ag_done")
        cg_ready = sem("cg_ready")
        kg_done = sem("kg_done")
        k_done = sem("k_done")
        t3_done = sem("t3_done")
        st3_done = sem("st3_done")
        o_done = sem("o_done")
        out_sent = sem("out_sent")

        pool_link = sem("pool_link")
        RS_LINKS, DG_LINKS = 6, 9

        S_BANK = bank[0:4]
        SS_BANK = bank[4]
        RB_BANK = [bank[5], bank[6]]
        XW_BANK = bank[0]
        MIX_BANK = [bank[1], bank[2]]
        WIDE_BANK = [bank[3], bank[4]]
        TR_BANK = bank[5]
        GRAM_BANK = bank[6]
        BC_BANK = bank[7]

        MIX_N, WIDE_N, TR_N = 3 * G, 2 * T + 2 * G, T + 1
        mix_of = lambda layer, g, b: MIX_N * g + G * layer + b
        GRAV, LANG = 0, 1
        yt_of = lambda which, g, j: WIDE_N * g + T * which + j
        u_of = lambda g, b: WIDE_N * g + 2 * T + b
        ku_of = lambda g, b: WIDE_N * g + 2 * T + G + b
        FRONT_R, BACK_R = 3, 2

        def r_of(i, what):
            before = 0 if isinstance(i, int) and i == 0 else FRONT_R * i + BACK_R * (i - 1)
            if isinstance(i, int) and i == 0:
                return before + {"ln0": 0, "ln1": 1, "ln2": 2}[what]
            if isinstance(i, int) and i == NG:
                return before + {"lang": 0, "ln3": 1}[what]
            return before + {"ln0": 0, "ln1": 1, "lang": 2, "ln2": 3, "ln3": 4}[what]

        LINKS = {"front": 3 * 5, "back": 5 + 17}

        def bcast_mid(ap, n):
            return ap.rearrange("p (a m) -> p a m", a=1).to_broadcast([P, n, ap.shape[1]])

        def bcast_last(ap, m):
            return ap.rearrange("p (n a) -> p n a", a=1).to_broadcast([P, ap.shape[1], m])

        def tiles(ap):
            return ap.rearrange("p (t m) -> p t m", t=T)

        block = ctx.enter_context(nc.Block())

        @block.sync
        def _(eng):
            def load_xa(q, u):
                eng.dma_start(xa[u][:, :, :],
                              x[bass.ds(q * G, G), :, :].rearrange("b p n -> p b n")).then_inc(xa_in[u], 16)

            load_xa(0, 0)
            load_xa(1, 1)
            eng.dma_start(adj_sb[:, :], adj).then_inc(small_in, 16)
            eng.dma_start(bias0_col[:, :], bias0.rearrange("(p a) -> p a", a=1)).then_inc(small_in, 16)
            eng.dma_start(bias1_row[:, :], bias1.rearrange("(a n) -> a n", a=1).to_broadcast([P, N])).then_inc(small_in, 16)
            eng.dma_start(bias2_row[:, :], bias2.rearrange("(a n) -> a n", a=1).to_broadcast([P, N])).then_inc(small_in, 16)
            eng.dma_start(gate[:, 0:1], gate_logit.to_broadcast([P, 1])).then_inc(small_in, 16)
            eng.dma_start(gate[:, 1:2], log_sigma.to_broadcast([P, 1])).then_inc(small_in, 16)
            with eng.Fori(1, NG // 2) as pair:
                for u in range(2):
                    eng.wait_ge(xn_done, (2 * pair + u - 1) * G)
                    eng.wait_ge(squared, 2 * pair + u - 1)
                    load_xa(2 * pair + u, u)
            eng.wait_ge(xn_done, NB)
            eng.wait_ge(squared, NG)
            for stage, w in ((2, w_v), (3, w_o)):
                eng.dma_start(w_stage[stage][:, :, :], w.rearrange("(t p) n -> p t n", p=P)).then_inc(w_in, 16)
            eng.wait_ge(xnlo_done, NB)
            eng.wait_ge(xnhi_done, NB)
            eng.wait_ge(ss_done, NG)
            for stage, w in ((0, w_lang), (1, w_grav)):
                eng.dma_start(w_stage[stage][:, :, :], w.rearrange("(t p) n -> p t n", p=P)).then_inc(w_in, 16)

            def load_x(g):
                eng.dma_start(x_in[:, :, :], x[bass.ds(g * G, G), :, :].rearrange("b p n -> p b n")).then_inc(x3_in, 16)

            eng.wait_ge(wot_turned, T)
            load_x(0)

            def store(g):
                eng.wait_ge(o_done, G * (g + 1))
                eng.dma_start(out[bass.ds(G * g, G), :, :].rearrange("b p n -> p b n"), o_sb[:, :, :]).then_inc(out_sent, 16)

            def next_x(g):
                eng.wait_ge(xhi_done, G * g)
                eng.wait_ge(xlo_done, G * g)
                eng.wait_ge(xb_done, G * g)
                load_x(g)

            next_x(1)
            with eng.Fori(1, NG - 1) as i:
                next_x(i + 1)
                store(i - 1)
            store(NG - 2)
            store(NG - 1)
            eng.wait_ge(out_sent, 16 * NG)

        @block.tensor
        def _(eng):
            def product3(dst, a_hi, a_lo, b_hi, b_lo, start, stop):
                eng.matmul(dst, a_hi, b_hi, start=start, stop=False)
                eng.matmul(dst, a_hi, b_lo, start=False, stop=False)
                return eng.matmul(dst, a_lo, b_hi, start=False, stop=stop)

            def sum_squares(q, first=False):
                eng.wait_ge(squared, q + 1)
                if not first:
                    eng.wait_ge(rs_link, (q - 1) * RS_LINKS + 1)
                for b in range(G):
                    for t in range(T):
                        c = b * T + t
                        last = eng.matmul(SS_BANK[:, c:c + 1], sqr[:, b, t * P:(t + 1) * P], ones[:, 0:1],
                                          start=True, stop=True)
                last.then_inc(ss_done, 1)

            def spread_norms(q, b, first=False):
                if b == 0:
                    eng.wait_ge(rs_link, (q + 1) * RS_LINKS)
                if not first:
                    eng.wait_ge(xn_done, q * G + b - 1)
                for t in range(T):
                    c = b * T + t
                    last = eng.transpose(RB_BANK[b % 2][:, t * P:(t + 1) * P],
                                         rs[:, 3, c:c + 1].to_broadcast([P, P]), ident[:, :])
                last.then_inc(rb_done, 1)

            def similarity(q, b, first=False, end=False):
                eng.wait_ge(xnlo_done, q * G + b + 1)
                eng.wait_ge(xnhi_done, q * G + b + 1)
                for t in range(T):
                    c = slice(t * P, (t + 1) * P)
                    r = slice(t * P, N)
                    last = product3(S_BANK[t][:, t * P:N], xn_hi[:, b, c], xn_lo[:, b, c],
                                    xn_hi[:, b, r], xn_lo[:, b, r], start=first, stop=end)
                last.then_inc(sim_done, 1)

            def sim_group(q, first=False, end=False):
                for b in range(G):
                    spread_norms(q, b, first=first and b < 2)
                    if b == 2 and not end:
                        sum_squares(q + 1)
                    if b < 2:
                        if not first:
                            similarity(q - 1, b + 2)
                    else:
                        similarity(q, b - 2, first=first and b == 2)
                if end:
                    similarity(q, 2)
                    similarity(q, 3, end=True)

            eng.wait_ge(const_set, 5)
            sum_squares(0, first=True)
            sim_group(0, first=True)
            with eng.Fori(1, NG - 1) as q:
                sim_group(q)
            sim_group(NG - 1, end=True)

            for i in range(1, T):
                for j in range(i):
                    eng.wait_ge(s_copied, j + 1)
                    last = eng.transpose(bank[4 + i][:, j * P:(j + 1) * P], s_sb[:, j, i * P:(i + 1) * P], ident[:, :])
                last.then_inc(s_turned, 1)
            eng.wait_ge(w_in, 64)
            eng.wait_ge(s_copied, T)
            for f in range(T):
                if f >= 2:
                    eng.wait_ge(wot_done, f - 1)
                for e in range(T):
                    last = eng.transpose(bank[f % 2][:, e * P:(e + 1) * P],
                                         w_stage[3][:, f, e * P:(e + 1) * P], ident[:, :])
                last.then_inc(wot_turned, 1)
            eng.wait_ge(wot_done, T)
            k = 0
            for lhs, rhs in ((w_stage[1], w_stage[1]), (w_stage[0], w_stage[0]), (w_stage[2], wot)):
                for d in range(T):
                    if k >= 2:
                        eng.wait_ge(prod_hi, k - 1)
                    for e in range(T):
                        last = eng.matmul(bank[2 + k % 2][:, :], lhs[:, e, d * P:(d + 1) * P], rhs[:, e, :],
                                          start=(e == 0), stop=(e == T - 1))
                    last.then_inc(prod_done, 1)
                    k += 1
            eng.wait_ge(a_done, T)
            for t in range(T):
                for s in range(T):
                    last = eng.matmul(bank[4][:, t:t + 1], a_sb[:, s, t * P:(t + 1) * P], ones[:, 0:1],
                                      start=(s == 0), stop=(s == T - 1))
            last.then_inc(dg_done, 1)
            eng.wait_ge(dg_link, DG_LINKS)
            eng.wait_ge(s_mirrored, T - 1)
            for t in range(T):
                last = eng.transpose(bank[5][:, t * P:(t + 1) * P], dcol[:, 4, t:t + 1].to_broadcast([P, P]), ident[:, :])
            last.then_inc(db_done, 1)

            def xw(g, b, first=False):
                n = G * g + b
                eng.wait_ge(xhi_done, n + 1)
                eng.wait_ge(xlo_done, n + 1)
                if not first:
                    eng.wait_ge(xwlo_done, n)
                for t in range(T):
                    c = slice(t * P, (t + 1) * P)
                    last = product3(XW_BANK[:, c], x_hi[:, b, c], x_lo[:, b, c], adj_hi[:, :], adj_lo[:, :],
                                    start=True, stop=True)
                last.then_inc(pe_xw, 1)

            def mix_bank(m, first=False):
                if not first:
                    eng.wait_ge(mix_used, m - 1)

            def spread(g, b, first=False):
                n = G * g + b
                eng.wait_ge(xwlo_done, n + 1)
                mix_bank(mix_of(0, g, b), first)
                for t in range(T):
                    c = slice(t * P, (t + 1) * P)
                    last = product3(MIX_BANK[b % 2][:, :], xw_hi[:, b % 2, c], xw_lo[:, b % 2, c],
                                    an_hi[:, t, :], an_lo[:, t, :], start=(t == 0), stop=(t == T - 1))
                last.then_inc(pe_mix, 1)

            def mix(layer, g, b):
                eng.wait_ge(yhi_done, 2 * G * g + G * (layer - 1) + b + 1)
                eng.wait_ge(ylo_done, 2 * G * g + G * (layer - 1) + b + 1)
                mix_bank(mix_of(layer, g, b))
                product3(MIX_BANK[b % 2][:, :], w1_hi[:, :], w1_lo[:, :], y_hi[:, b, :], y_lo[:, b, :],
                         start=True, stop=True).then_inc(pe_mix, 1)

            def turn_h(g, j, first=False):
                eng.wait_ge(h_done, G * (g + 1))
                if not first:
                    eng.wait_ge(tr_used, TR_N * g + j)
                for b in range(G):
                    last = eng.transpose(TR_BANK[:, b * P:(b + 1) * P], h_sb[:, b, j * P:(j + 1) * P], ident[:, :])
                last.then_inc(pe_tr, 1)

            def wide_bank(w, first=False):
                if not first:
                    eng.wait_ge(wide_used, w - 1)

            def yt(which, g, j, first=False):
                if which == GRAV and j == 0:
                    eng.wait_ge(tr_used, TR_N * g + T)
                wide_bank(yt_of(which, g, j), first)
                p_hi, p_lo = ((pg_hi, pg_lo), (pl_hi, pl_lo))[which]
                c = slice(j * P, (j + 1) * P)
                for d in range(T):
                    last = product3(WIDE_BANK[j % 2][:, :], p_hi[:, d, c], p_lo[:, d, c], ht_hi[:, d, :], ht_lo[:, d, :],
                                    start=(d == 0), stop=(d == T - 1))
                last.then_inc(pe_wide, 1)

            def grams(which, g, first=False):
                eng.wait_ge(wide_used, yt_of(which, g, T - 1) + 1)
                if not first:
                    eng.wait_ge(gram_done, 2 * g + which)
                for b in range(G):
                    c = slice(b * P, (b + 1) * P)
                    for j in range(T):
                        last = product3(GRAM_BANK[:, c], yt_hi[:, which, j, c], yt_lo[:, which, j, c],
                                        ht_hi[:, j, c], ht_lo[:, j, c], start=(j == 0), stop=(j == T - 1))
                last.then_inc(pe_gram, 1)

            def u_product(g, b):
                wide_bank(u_of(g, b))
                c = slice(b * P, (b + 1) * P)
                for d in range(T):
                    last = product3(WIDE_BANK[b % 2][:, :], ht_hi[:, d, c], ht_lo[:, d, c], m_hi[:, d, :], m_lo[:, d, :],
                                    start=(d == 0), stop=(d == T - 1))
                last.then_inc(pe_wide, 1)

            def spread_column(which, g, first=False):
                if which == GRAV:
                    eng.wait_ge(sq_ready, g + 1)
                    if not first:
                        eng.wait_ge(k_done, g)
                else:
                    eng.wait_ge(norm_ready, r_of(g + 1, "lang") + 1)
                    eng.wait_ge(dist_done, g + 1)
                for b in range(G):
                    col = (sq[:, 0, b:b + 1], rstd[:, 4, b:b + 1])[which]
                    last = eng.transpose(BC_BANK[:, b * P:(b + 1) * P], col.to_broadcast([P, P]), ident[:, :])
                last.then_inc(pe_bc, 1)

            def turn_k(g):
                eng.wait_ge(k_done, g + 1)
                eng.wait_ge(tr_used, TR_N * g + T)
                for b in range(G):
                    c = slice(b * P, (b + 1) * P)
                    last = eng.transpose(TR_BANK[:, c], k_sb[:, c], ident[:, :])
                last.then_inc(pe_tr, 1)

            def ku(g, b):
                eng.wait_ge(tr_used, TR_N * (g + 1))
                wide_bank(ku_of(g, b))
                c = slice(b * P, (b + 1) * P)
                product3(WIDE_BANK[b % 2][:, :], kt_hi[:, c], kt_lo[:, c], u_hi[:, b, :], u_lo[:, b, :],
                         start=True, stop=True).then_inc(pe_wide, 1)

            def iteration(i, front=True, back=True, first_front=False, first_back=False):
                g = i - 1
                if front:
                    xw(i, 0, first=first_front)
                    xw(i, 1)
                for b in range(G):
                    if front:
                        spread(i, b, first=first_front and b < 2)
                    if back:
                        turn_h(g, b, first=first_back and b == 0)
                    if front and b + 2 < G:
                        xw(i, b + 2)
                if back:
                    for j in range(T):
                        yt(GRAV, g, j, first=first_back and j < 2)
                if front:
                    for b in range(G):
                        mix(1, i, b)
                if back:
                    grams(GRAV, g, first=first_back)
                    yt(LANG, g, 0)
                    yt(LANG, g, 1)
                    spread_column(GRAV, g, first=first_back)
                    yt(LANG, g, 2)
                    yt(LANG, g, 3)
                    u_product(g, 0)
                    grams(LANG, g)
                    u_product(g, 1)
                    u_product(g, 2)
                    spread_column(LANG, g)
                    u_product(g, 3)
                if front:
                    mix(2, i, 0)
                    mix(2, i, 1)
                if back:
                    turn_k(g)
                if front:
                    mix(2, i, 2)
                    mix(2, i, 3)
                if back:
                    for b in range(G):
                        ku(g, b)

            eng.wait_ge(an_done, T)
            eng.wait_ge(adj_made, 2)
            eng.wait_ge(prod_lo, 3 * T)
            iteration(0, back=False, first_front=True)
            iteration(1, first_back=True)
            with eng.Fori(2, NG) as i:
                iteration(i)
            iteration(NG, front=False)

        @block.scalar
        def _(eng):
            def square(q, u, loads, first=False):
                eng.wait_ge(xa_in[u], 16 * loads)
                if not first:
                    eng.wait_ge(ss_done, q)
                eng.activation(sqr[:, :, :], xa[u][:, :, :], ACT.Square).then_inc(squared, 1)

            def root(q):
                eng.wait_ge(rs_link, q * RS_LINKS + 1)
                eng.activation(rs[:, 0, :], ss[:, :], ACT.Sqrt).then_inc(rs_sqrt, 1)

            def split_hi(q, b, first=False):
                eng.wait_ge(xn_done, q * G + b + 1)
                if not first:
                    eng.wait_ge(sim_done, (q - 1) * G + b + 1)
                eng.activation(xn_hi[:, b, :], xn_f[:, b, :], ACT.Copy).then_inc(xnhi_done, 1)

            def norm_group(q, u, loads=0, first=False, end=False):
                split_hi(q, 0, first)
                if not end:
                    square(q + 1, 1 - u, loads)
                split_hi(q, 1, first)
                split_hi(q, 2, first)
                if not end:
                    root(q + 1)
                split_hi(q, 3, first)

            square(0, 0, 1, first=True)
            root(0)
            norm_group(0, 0, loads=1, first=True)
            with eng.Fori(0, NG // 2 - 1) as pair:
                norm_group(2 * pair + 1, 1, loads=pair + 2)
                norm_group(2 * pair + 2, 0, loads=pair + 2)
            norm_group(NG - 1, 1, end=True)

            eng.wait_ge(sim_done, NB)
            for t in range(T):
                eng.activation(s_sb[:, t, t * P:N], S_BANK[t][:, t * P:N], ACT.Copy,
                               scale=1.0 / (XN_SCALE * XN_SCALE * NB)).then_inc(s_copied, 1)
            for i in range(1, T):
                eng.wait_ge(s_turned, i)
                eng.activation(s_sb[:, i, 0:i * P], bank[4 + i][:, 0:i * P], ACT.Copy).then_inc(s_mirrored, 1)
            for f in range(T):
                eng.wait_ge(wot_turned, f + 1)
                eng.activation(wot[:, :, f * P:(f + 1) * P], tiles(bank[f % 2][:, :]), ACT.Copy).then_inc(wot_done, 1)
            k = 0
            for dst, scale in ((pg_hi, P_SCALE), (pl_hi, P_SCALE), (m_hi, M_SCALE)):
                for d in range(T):
                    eng.wait_ge(prod_done, k + 1)
                    if k >= T:
                        eng.wait_ge(prod_lo, k - T + 1)
                    eng.activation(prod_f[:, k % T, :], bank[2 + k % 2][:, :], ACT.Copy, scale=scale).then_inc(anhi_done, 1)
                    eng.activation(dst[:, d, :], bank[2 + k % 2][:, :], ACT.Copy, scale=scale).then_inc(prod_hi, 1)
                    k += 1
            eng.wait_ge(dg_link, 1)
            eng.activation(dcol[:, 1, :], dcol[:, 0, :], ACT.Sqrt).then_inc(dg_sqrt, 1)
            for t in range(T):
                eng.wait_ge(anf_done, t + 1)
                eng.activation(an_hi[:, t, :], an_f[:, t, :], ACT.Copy).then_inc(anhi_done, 1)

            eng.preload_act_table_set("natural_log_exp_and_others")
            eng.wait_ge(small_in, 96)
            eng.activation(gate[:, 2:3], gate[:, 0:1], ACT.Exp, scale=-1.0).then_inc(gate_exp, 1)
            eng.activation(gate[:, 3:4], gate[:, 1:2], ACT.Exp, scale=-2.0).then_inc(gate_exp, 1)

            def x_split(g, b, first=False):
                if b == 0:
                    eng.wait_ge(x3_in, 16 * (g + 1))
                if not first:
                    eng.wait_ge(pe_xw, G * (g - 1) + b + 1)
                eng.activation(x_hi[:, b, :], x_in[:, b, :], ACT.Copy).then_inc(xhi_done, 1)

            def xw_split(g, b, first=False):
                eng.wait_ge(pe_xw, G * g + b + 1)
                if not first:
                    eng.wait_ge(pe_mix, mix_of(0, g, b - 2) + 1 if b >= 2 else mix_of(0, g - 1, b + 2) + 1)
                eng.activation(xw_hi[:, b % 2, :], XW_BANK[:, :], ACT.Copy, scale=XW_SCALE / ADJ_SCALE).then_inc(xwhi_done, 1)

            def root_of(i, what):
                row = {"ln0": 0, "ln1": 1, "ln2": 2, "ln3": 3, "lang": 4}[what]
                k = r_of(i, what)
                eng.wait_ge(var_ready, k + 1)
                src = half_var[:, row, :] if row < 4 else sq_h[:, :]
                eng.activation(ln_v[:, row, :], src, ACT.Ln, scale=-2.0).then_inc(act_link, 1)
                eng.wait_ge(act_link, k + 1)
                eng.activation(r0[:, row, :], ln_v[:, row, :], ACT.Exp, scale=-0.5).then_inc(r0_ready, 1)

            def y_split(layer, i):
                eng.wait_ge(norm_ready, r_of(i, f"ln{layer}") + 1)
                for b in range(G):
                    eng.activation(y_hi[:, b, :], t_sb[:, b, :], ACT.Identity, bias=nmr[:, layer, b:b + 1],
                                   scale=rstd[:, layer, b:b + 1]).then_inc(yhi_done, 1)

            def turned_split(dst, k, scale):
                eng.wait_ge(pe_tr, k + 1)
                eng.activation(dst, TR_BANK[:, :], ACT.Copy, scale=scale).then_inc(trhi_done, 1)

            def wide_split(dst, w, j, scale):
                eng.wait_ge(pe_wide, w + 1)
                eng.activation(dst, WIDE_BANK[j % 2][:, :], ACT.Copy, scale=scale).then_inc(widehi_done, 1)

            def iteration(i, front=True, back=True, first_front=False, prep=True):
                g = i - 1
                if front:
                    xw_split(i, 0, first_front)
                    xw_split(i, 1, first_front)
                for b in range(G):
                    if back:
                        turned_split(ht_hi[:, b, :], TR_N * g + b, 1.0)
                    if front and b + 2 < G:
                        xw_split(i, b + 2)
                if front:
                    root_of(i, "ln0")
                if back:
                    wide_split(yt_hi[:, GRAV, 0, :], yt_of(GRAV, g, 0), 0, 1.0 / P_SCALE)
                if front:
                    y_split(0, i)
                if back:
                    for j in range(1, T):
                        wide_split(yt_hi[:, GRAV, j, :], yt_of(GRAV, g, j), j, 1.0 / P_SCALE)
                if front:
                    root_of(i, "ln1")
                if back:
                    eng.wait_ge(pe_gram, 2 * g + GRAV + 1)
                    eng.activation(gram[:, GRAV, :], GRAM_BANK[:, :], ACT.Copy, scale=-2.0).then_inc(gram_done, 1)
                    wide_split(yt_hi[:, LANG, 0, :], yt_of(LANG, g, 0), 0, 1.0 / P_SCALE)
                if front:
                    y_split(1, i)
                if back:
                    wide_split(yt_hi[:, LANG, 1, :], yt_of(LANG, g, 1), 1, 1.0 / P_SCALE)
                    wide_split(yt_hi[:, LANG, 2, :], yt_of(LANG, g, 2), 2, 1.0 / P_SCALE)
                    eng.wait_ge(dist_done, g + 1)
                    eng.activation(expo[:, :], dist[:, :], ACT.Exp, scale=gate[:, 5:6]).then_inc(exp_done, 1)
                    wide_split(yt_hi[:, LANG, 3, :], yt_of(LANG, g, 3), 3, 1.0 / P_SCALE)
                    wide_split(u_hi[:, 0, :], u_of(g, 0), 0, 1.0 / M_SCALE)
                    eng.wait_ge(pe_gram, 2 * g + LANG + 1)
                    eng.activation(gram[:, LANG, :], GRAM_BANK[:, :], ACT.Copy).then_inc(gram_done, 1)
                    root_of(i, "lang")
                    wide_split(u_hi[:, 1, :], u_of(g, 1), 1, 1.0 / M_SCALE)
                if front and prep:
                    x_split(i + 1, 0)
                    x_split(i + 1, 1)
                if back:
                    wide_split(u_hi[:, 2, :], u_of(g, 2), 2, 1.0 / M_SCALE)
                if front and prep:
                    x_split(i + 1, 2)
                    x_split(i + 1, 3)
                if back:
                    wide_split(u_hi[:, 3, :], u_of(g, 3), 3, 1.0 / M_SCALE)
                    turned_split(kt_hi[:, :], TR_N * g + T, K_SCALE)
                if front:
                    root_of(i, "ln2")
                if back:
                    root_of(i, "ln3")
                    eng.wait_ge(norm_ready, r_of(i, "ln3") + 1)
                    if not (isinstance(i, int) and i == 1):
                        eng.wait_ge(out_sent, 16 * g)
                    for b in range(G):
                        eng.activation(o_sb[:, b, :], t3[:, b, :], ACT.Identity, bias=nmr[:, 3, b:b + 1],
                                       scale=rstd[:, 3, b:b + 1]).then_inc(o_done, 1)

            for b in range(G):
                x_split(0, b, first=True)
            iteration(0, back=False, first_front=True)
            iteration(1)
            with eng.Fori(2, NG - 1) as i:
                iteration(i)
            iteration(NG - 1, prep=False)
            iteration(NG, front=False)

        @block.vector
        def _(eng):
            def norms(q):
                k = [0]

                def link(ins):
                    k[0] += 1
                    ins.then_inc(rs_link, 1)
                    if k[0] < RS_LINKS:
                        eng.wait_ge(rs_link, q * RS_LINKS + k[0])

                eng.wait_ge(ss_done, q + 1)
                link(eng.tensor_scalar(ss[:, :], SS_BANK[:, 0:G * T], 1e-24, None, ALU.max))
                eng.wait_ge(rs_sqrt, q + 1)
                link(eng.reciprocal(rs[:, 1, :], rs[:, 0, :]))
                link(eng.tensor_tensor(rs[:, 2, :], rs[:, 1, :], ss[:, :], ALU.mult))
                link(eng.tensor_tensor(rs[:, 2, :], rs[:, 2, :], rs[:, 1, :], ALU.mult))
                link(eng.tensor_scalar(rs[:, 2, :], rs[:, 2, :], -0.5 * XN_SCALE, 1.5 * XN_SCALE, ALU.mult, ALU.add))
                link(eng.tensor_tensor(rs[:, 3, :], rs[:, 2, :], rs[:, 1, :], ALU.mult))
                assert k[0] == RS_LINKS

            def normalise(q, u, b, first=False):
                eng.wait_ge(rb_done, q * G + b + 1)
                if not first:
                    eng.wait_ge(xnlo_done, (q - 1) * G + b + 1)
                    eng.wait_ge(xnhi_done, (q - 1) * G + b + 1)
                eng.tensor_tensor(xn_f[:, b, :], RB_BANK[b % 2][:, :], xa[u][:, b, :], ALU.mult).then_inc(xn_done, 1)

            def norm_group(q, u, first=False, end=False):
                for b in range(G):
                    normalise(q, u, b, first)
                if not end:
                    norms(q + 1)

            norms(0)
            norm_group(0, 0, first=True)
            with eng.Fori(0, NG // 2 - 1) as pair:
                norm_group(2 * pair + 1, 1)
                norm_group(2 * pair + 2, 0)
            norm_group(NG - 1, 1, end=True)

            def find(t):
                eng.max(top8[:, t, :], work[:, t, :]).then_inc(top, 1)

            def mark(t):
                eng.match_replace(out=work[:, t, :], in_to_replace=top8[:, t, :], in_values=work[:, t, :],
                                  imm_value=NEG).then_inc(top, 1)

            def all_tiles(step, before):
                eng.wait_ge(top, before)
                eng.memset(held[:, 0:1], 0.0)
                for t in range(T):
                    step(t)

            for t in range(T):
                eng.wait_ge(s_diag, 2 * t + 1)
                find(t)
            all_tiles(mark, T)
            with eng.Fori(1, TOP_ROUNDS) as r:
                all_tiles(find, 2 * T * r)
                all_tiles(mark, 2 * T * r + T)
            all_tiles(find, 2 * T * TOP_ROUNDS)
            eng.wait_ge(top, 2 * T * TOP_ROUNDS + T)
            eng.memset(top8[:, :, TOP_REST:8], NEG).then_inc(top, 1)
            all_tiles(mark, 2 * T * TOP_ROUNDS + T + 1)
            for t in range(T):
                eng.wait_ge(top, 2 * T * TOP_ROUNDS + T + t + 2)
                eng.wait_ge(s_diag, 2 * t + 2)
                eng.scalar_tensor_tensor(out=a_sb[:, t, :], in0=work[:, t, :], scalar=NEG, in1=s_sb[:, t, :],
                                         op0=ALU.is_equal, op1=ALU.mult).then_inc(a_done, 1)
            k = [0]

            def dg(ins):
                k[0] += 1
                ins.then_inc(dg_link, 1)
                eng.wait_ge(dg_link, k[0])

            eng.wait_ge(dg_done, 1)
            dg(eng.tensor_scalar(dcol[:, 0, :], bank[4][:, 0:T], 2.0 ** -110, None, ALU.max))
            dg(eng.tensor_scalar(dcol[:, 6, :], bank[4][:, 0:T], 0.0, None, ALU.is_gt))
            eng.wait_ge(dg_sqrt, 1)
            dg(eng.reciprocal(dcol[:, 2, :], dcol[:, 1, :]))
            dg(eng.tensor_tensor(dcol[:, 3, :], dcol[:, 2, :], dcol[:, 0, :], ALU.mult))
            dg(eng.tensor_tensor(dcol[:, 3, :], dcol[:, 3, :], dcol[:, 2, :], ALU.mult))
            dg(eng.tensor_scalar(dcol[:, 3, :], dcol[:, 3, :], -0.5, 1.5, ALU.mult, ALU.add))
            dg(eng.tensor_tensor(dcol[:, 3, :], dcol[:, 3, :], dcol[:, 2, :], ALU.mult))
            dg(eng.tensor_tensor(dcol[:, 4, :], dcol[:, 3, :], dcol[:, 6, :], ALU.mult))
            dg(eng.tensor_scalar(dcol[:, 5, :], dcol[:, 4, :], AN_SCALE, None, ALU.mult))
            assert k[0] == DG_LINKS
            eng.wait_ge(db_done, 1)
            eng.wait_ge(prod_lo, 3 * T)
            for t in range(T):
                eng.scalar_tensor_tensor(out=an_f[:, t, :], in0=a_sb[:, t, :], scalar=dcol[:, 5, t:t + 1],
                                         in1=bank[5][:, :], op0=ALU.mult, op1=ALU.mult).then_inc(anf_done, 1)
            for t in range(T):
                eng.wait_ge(anhi_done, 3 * T + t + 1)
                eng.tensor_tensor(an_lo[:, t, :], an_f[:, t, :], an_hi[:, t, :], ALU.subtract).then_inc(an_done, 1)

            eng.wait_ge(gate_exp, 2)
            eng.tensor_scalar(gate[:, 4:5], gate[:, 2:3], 1.0, None, ALU.add).then_inc(gate_done, 1)
            eng.tensor_scalar(gate[:, 5:6], gate[:, 3:4], -0.5, None, ALU.mult).then_inc(gate_done, 1)
            eng.wait_ge(gate_done, 2)
            eng.reciprocal(gate[:, 6:7], gate[:, 4:5]).then_inc(gate_done, 1)
            eng.wait_ge(gate_done, 3)
            eng.tensor_scalar(gate[:, 7:8], gate[:, 6:7], -1.0, 1.0, ALU.mult, ALU.add).then_inc(gate_done, 1)
            eng.wait_ge(gate_done, 4)

            def iteration(i, front=True, back=True):
                g = i - 1
                base = 0 if isinstance(i, int) and i == 0 else LINKS["front"] * i + LINKS["back"] * (i - 1)
                k = [0]

                def link(ins):
                    k[0] += 1
                    ins.then_inc(dve_link, 1)
                    eng.wait_ge(dve_link, base + k[0])

                def xw_rest(b):
                    eng.wait_ge(xwhi_done, G * i + b + 1)
                    eng.scalar_tensor_tensor(out=xw_lo[:, b % 2, :], in0=XW_BANK[:, :], scalar=XW_SCALE / ADJ_SCALE,
                                             in1=xw_hi[:, b % 2, :], op0=ALU.mult, op1=ALU.subtract).then_inc(xwlo_done, 1)

                def add_up(layer, b):
                    m = mix_of(layer, i, b)
                    eng.wait_ge(pe_mix, m + 1)
                    if layer == 0:
                        eng.wait_ge(xb_done, G * i + b + 1)
                        scale, other = 1.0 / (XW_SCALE * AN_SCALE), xb[:, b, :]
                    else:
                        eng.wait_ge(yhi_done, 2 * G * i + G * (layer - 1) + b + 1)
                        scale, other = 1.0 / W1_SCALE, (bias1_row, bias2_row)[layer - 1][:, :]
                    eng.scalar_tensor_tensor(out=t_sb[:, b, :], in0=MIX_BANK[b % 2][:, :], scalar=scale,
                                             in1=other, op0=ALU.mult, op1=ALU.add).then_inc(mix_used, 1)
                    eng.wait_ge(mix_used, m + 1)
                    eng.bn_stats(stats[:, layer, b, :], t_sb[:, b, :]).then_inc(stat_done, 1)

                def refine(row, what, source):
                    eng.wait_ge(r0_ready, r_of(i, what) + 1)
                    link(eng.tensor_tensor(r_t[:, row, :], r0[:, row, :], r0[:, row, :], ALU.mult))
                    link(eng.tensor_tensor(r_t[:, row, :], r_t[:, row, :], source, ALU.mult))
                    return eng.scalar_tensor_tensor(out=rstd[:, row, :], in0=r_t[:, row, :], scalar=1.5,
                                                    in1=r0[:, row, :], op0=ALU.add, op1=ALU.mult)

                def layer_norm(layer):
                    what = f"ln{layer}"
                    if layer < 3:
                        eng.wait_ge(stat_done, mix_of(layer, i, G - 1) + 1)
                    else:
                        eng.wait_ge(st3_done, G * g + G)
                    eng.memset(held[:, 1:2], 0.0)
                    for b in range(G):
                        ins = eng.bn_aggr(mv[:, layer, b, :], stats[:, layer, b, :])
                    link(ins)
                    eng.tensor_scalar(half_var[:, layer, :], mv[:, layer, :, 1], LN_EPS, -0.5, ALU.add, ALU.mult).then_inc(var_ready, 1)
                    link(refine(layer, what, half_var[:, layer, :]))
                    link(eng.scalar_tensor_tensor(out=nmr[:, layer, :], in0=mv[:, layer, :, 0], scalar=-1.0,
                                                  in1=rstd[:, layer, :], op0=ALU.mult, op1=ALU.mult))
                    eng.tensor_copy(r_t[:, layer, 0:1], rstd[:, layer, 0:1]).then_inc(norm_ready, 1)

                def y_full(layer, b):
                    if not (isinstance(i, int) and i == 0 and layer == 0):
                        eng.wait_ge(ylo_done, 2 * G * i + G * (layer - 1) + b + 1)
                    eng.tensor_scalar(y_f[:, b, :], t_sb[:, b, :], rstd[:, layer, b:b + 1], nmr[:, layer, b:b + 1],
                                      ALU.mult, ALU.add).then_inc(yf_done, 1)

                def turned_rest(dst, hi, c, scale):
                    eng.wait_ge(trhi_done, c + 1)
                    eng.scalar_tensor_tensor(out=dst, in0=TR_BANK[:, :], scalar=scale, in1=hi,
                                             op0=ALU.mult, op1=ALU.subtract).then_inc(tr_used, 1)

                def wide_rest(dst, hi, k, j, scale):
                    eng.wait_ge(widehi_done, (WIDE_N - G) * g + k + 1)
                    eng.scalar_tensor_tensor(out=dst, in0=WIDE_BANK[j % 2][:, :], scalar=scale, in1=hi,
                                             op0=ALU.mult, op1=ALU.subtract).then_inc(wide_used, 1)

                def yt_rest(which, j):
                    wide_rest(yt_lo[:, which, j, :], yt_hi[:, which, j, :], T * which + j, j, 1.0 / P_SCALE)

                def u_rest(b):
                    wide_rest(u_lo[:, b, :], u_hi[:, b, :], 2 * T + b, b, 1.0 / M_SCALE)

                def squares(which):
                    eng.wait_ge(gram_done, 2 * g + which + 1)
                    link(eng.tensor_tensor(tiles(diag[:, :]), tiles(gram[:, which, :]), bcast_mid(ident[:, :], G), ALU.mult))
                    ins = eng.tensor_reduce(sq[:, which, :], tiles(diag[:, :]), AX.X, ALU.add)
                    if which == GRAV:
                        ins.then_inc(sq_ready, 1)
                        eng.wait_ge(sq_ready, g + 1)
                    else:
                        link(ins)

                if front:
                    xw_rest(0)
                    xw_rest(1)
                for b in range(G):
                    if front:
                        add_up(0, b)
                    if back:
                        turned_rest(ht_lo[:, b, :], ht_hi[:, b, :], TR_N * g + b, 1.0)
                    if front and b + 2 < G:
                        xw_rest(b + 2)
                if front:
                    layer_norm(0)
                if back:
                    yt_rest(GRAV, 0)
                if front:
                    for b in range(G):
                        y_full(0, b)
                if back:
                    for j in range(1, T):
                        yt_rest(GRAV, j)
                if front:
                    for b in range(G):
                        add_up(1, b)
                    layer_norm(1)
                if back:
                    squares(GRAV)
                    yt_rest(LANG, 0)
                if front:
                    for b in range(G):
                        y_full(1, b)
                if back:
                    yt_rest(LANG, 1)
                    eng.wait_ge(pe_bc, 2 * g + 1)
                    link(eng.scalar_tensor_tensor(out=diag[:, :], in0=BC_BANK[:, :], scalar=-0.5, in1=gram[:, GRAV, :],
                                                  op0=ALU.mult, op1=ALU.add))
                    link(eng.scalar_tensor_tensor(out=tiles(dist[:, :]), in0=bcast_last(sq[:, 0, :], P), scalar=-0.5,
                                                  in1=tiles(diag[:, :]), op0=ALU.mult, op1=ALU.add))
                    eng.tensor_scalar(dist[:, :], dist[:, :], 0.0, None, ALU.max).then_inc(dist_done, 1)
                    yt_rest(LANG, 2)
                    yt_rest(LANG, 3)
                    eng.wait_ge(ag_done, g + 1)
                    link(eng.tensor_reduce(deg[:, 0, :], tiles(a_g[:, :]), AX.X, ALU.add))
                    u_rest(0)
                    squares(LANG)
                    eng.tensor_scalar(sq_h[:, :], sq[:, 1, :], NORM_EPS * NORM_EPS, -0.5, ALU.max, ALU.mult).then_inc(var_ready, 1)
                    link(eng.scalar_tensor_tensor(out=tiles(a_l[:, :]), in0=tiles(gram[:, LANG, :]), scalar=0.0,
                                                  in1=bcast_mid(adj_off[:, :], G), op0=ALU.max, op1=ALU.mult))
                    link(refine(4, "lang", sq_h[:, :]))
                    eng.tensor_copy(r_t[:, 4, 0:1], rstd[:, 4, 0:1]).then_inc(norm_ready, 1)
                    u_rest(1)
                    u_rest(2)
                    eng.wait_ge(pe_bc, 2 * g + 2)
                    link(eng.tensor_tensor(a_l[:, :], BC_BANK[:, :], a_l[:, :], ALU.mult))
                    link(eng.tensor_reduce(deg_c[:, 1, :], tiles(a_l[:, :]), AX.X, ALU.add))
                    link(eng.tensor_tensor(deg[:, 1, :], deg_c[:, 1, :], rstd[:, 4, :], ALU.mult))
                    link(eng.tensor_scalar(deg_c[:, :, :], deg[:, :, :], NORM_EPS, None, ALU.max))
                    link(eng.reciprocal(inv_deg[:, :, :], deg_c[:, :, :]))
                    eng.tensor_scalar(coef[:, 0, :], inv_deg[:, 0, :], gate[:, 7:8], None, ALU.mult).then_inc(cg_ready, 1)
                    link(eng.scalar_tensor_tensor(out=coef[:, 1, :], in0=inv_deg[:, 1, :], scalar=gate[:, 6:7],
                                                  in1=rstd[:, 4, :], op0=ALU.mult, op1=ALU.mult))
                    link(eng.tensor_tensor(tiles(diag[:, :]), tiles(a_l[:, :]), bcast_last(coef[:, 1, :], P), ALU.mult))
                    eng.wait_ge(kg_done, g + 1)
                    eng.tensor_tensor(k_sb[:, :], diag[:, :], k_g[:, :], ALU.add).then_inc(k_done, 1)
                    u_rest(3)
                if front:
                    add_up(2, 0)
                    add_up(2, 1)
                if back:
                    turned_rest(kt_lo[:, :], kt_hi[:, :], TR_N * g + T, K_SCALE)
                if front:
                    add_up(2, 2)
                    add_up(2, 3)
                    layer_norm(2)
                for b in range(G):
                    if back:
                        w = ku_of(g, b)
                        eng.wait_ge(pe_wide, w + 1)
                        eng.scalar_tensor_tensor(out=t3[:, b, :], in0=WIDE_BANK[b % 2][:, :], scalar=1.0 / K_SCALE,
                                                 in1=h_sb[:, b, :], op0=ALU.mult, op1=ALU.add).then_inc(wide_used, 1)
                        eng.wait_ge(wide_used, w + 1)
                        eng.bn_stats(stats[:, 3, b, :], t3[:, b, :]).then_inc(st3_done, 1)
                    if front:
                        eng.tensor_scalar(h_sb[:, b, :], t_sb[:, b, :], rstd[:, 2, b:b + 1], nmr[:, 2, b:b + 1],
                                          ALU.mult, ALU.add).then_inc(h_done, 1)
                if back:
                    layer_norm(3)
                want = LINKS["front"] * front + LINKS["back"] * back
                assert k[0] == want, (k[0], want, front, back)

            iteration(0, back=False)
            with eng.Fori(1, NG) as i:
                iteration(i)
            iteration(NG, front=False)

        @block.gpsimd
        def _(eng):
            eng.memset(zeros[:, :], 0.0).then_inc(const_set, 1)
            eng.memset(ones[:, :], 1.0).then_inc(const_set, 1)
            eng.wait_ge(const_set, 2)
            eng.affine_select(out=ident[:, :], in_=zeros[:, :], compare_op=ALU.not_equal, fill=1.0, base=0,
                              pattern=[[-1, P]], channel_multiplier=1).then_inc(const_set, 1)
            eng.affine_select(out=not_eye[:, :], in_=ones[:, :], compare_op=ALU.not_equal, fill=0.0, base=0,
                              pattern=[[-1, P]], channel_multiplier=1).then_inc(const_set, 1)
            eng.memset(w1_f[:, :], 0.0).then_inc(const_set, 1)

            def split_lo(q, b, first=False):
                eng.wait_ge(xnhi_done, q * G + b + 1)
                eng.tensor_tensor(xn_lo[:, b, :], xn_f[:, b, :], xn_hi[:, b, :], ALU.subtract).then_inc(xnlo_done, 1)

            with eng.Fori(0, NG) as q:
                for b in range(G):
                    split_lo(q, b)

            for t in range(T):
                eng.wait_ge(s_copied, t + 1)
                if t >= 1:
                    eng.wait_ge(s_mirrored, t)
                eng.affine_select(out=work[:, t, :], in_=s_sb[:, t, :], compare_op=ALU.not_equal, fill=NEG, base=t * P,
                                  pattern=[[-1, N]], channel_multiplier=1).then_inc(s_diag, 1)
                eng.wait_ge(s_turned, T - 1)
                eng.wait_ge(s_diag, 2 * t + 1)
                eng.affine_select(out=s_sb[:, t, :], in_=s_sb[:, t, :], compare_op=ALU.not_equal, fill=0.0, base=t * P,
                                  pattern=[[-1, N]], channel_multiplier=1).then_inc(s_diag, 1)
            eng.wait_ge(small_in, 96)
            eng.wait_ge(const_set, 5)
            k = [0]

            def made(ins):
                k[0] += 1
                ins.then_inc(pool_link, 1)
                eng.wait_ge(pool_link, k[0])

            made(eng.tensor_tensor(adj_off[:, :], adj_sb[:, :], not_eye[:, :], ALU.mult))
            made(eng.tensor_scalar(adj_s[:, :], adj_sb[:, :], ADJ_SCALE, 0.0, ALU.mult, ALU.add))
            made(eng.tensor_copy(adj_hi[:, :], adj_s[:, :]))
            eng.tensor_tensor(adj_lo[:, :], adj_s[:, :], adj_hi[:, :], ALU.subtract).then_inc(adj_made, 1)
            made(eng.tensor_tensor(w1_f[:, :], adj_sb[:, :], adj_sb[:, :], ALU.mult))
            made(eng.tensor_tensor(w1_f[:, :], w1_f[:, :], ident[:, :], ALU.add))
            made(eng.tensor_scalar(w1_f[:, :], w1_f[:, :], W1_SCALE, 0.0, ALU.mult, ALU.add))
            made(eng.tensor_copy(w1_hi[:, :], w1_f[:, :]))
            eng.tensor_tensor(w1_lo[:, :], w1_f[:, :], w1_hi[:, :], ALU.subtract).then_inc(adj_made, 1)
            k2 = 0
            for hi, lo in ((pg_hi, pg_lo), (pl_hi, pl_lo), (m_hi, m_lo)):
                for d in range(T):
                    eng.wait_ge(prod_hi, k2 + 1)
                    eng.tensor_tensor(lo[:, d, :], prod_f[:, k2 % T, :], hi[:, d, :], ALU.subtract).then_inc(prod_lo, 1)
                    k2 += 1

            def x_rest(g, b, first=False):
                if not first:
                    eng.wait_ge(mix_used, mix_of(0, g - 1, b) + 1)
                eng.wait_ge(xhi_done, G * g + b + 1)
                eng.tensor_tensor(x_lo[:, b, :], x_in[:, b, :], x_hi[:, b, :], ALU.subtract).then_inc(xlo_done, 1)
                eng.tensor_scalar(xb[:, b, :], x_in[:, b, :], 1.0, bias0_col[:, :], ALU.mult, ALU.add).then_inc(xb_done, 1)

            def y_rest(layer, i):
                for b in range(G):
                    n = 2 * G * i + G * layer + b
                    eng.wait_ge(yf_done, n + 1)
                    eng.wait_ge(yhi_done, n + 1)
                    eng.tensor_tensor(y_lo[:, b, :], y_f[:, b, :], y_hi[:, b, :], ALU.subtract).then_inc(ylo_done, 1)

            def iteration(i, front=True, back=True, prep=True):
                g = i - 1
                if front:
                    y_rest(0, i)
                    y_rest(1, i)
                if back:
                    eng.wait_ge(exp_done, g + 1)
                    eng.tensor_tensor(tiles(a_g[:, :]), tiles(expo[:, :]), bcast_mid(adj_off[:, :], G), ALU.mult).then_inc(ag_done, 1)
                if front and prep:
                    for b in range(G):
                        x_rest(i + 1, b)
                if back:
                    eng.wait_ge(cg_ready, g + 1)
                    eng.tensor_tensor(tiles(k_g[:, :]), tiles(a_g[:, :]), bcast_last(coef[:, 0, :], P), ALU.mult).then_inc(kg_done, 1)

            for b in range(G):
                x_rest(0, b, first=True)
            iteration(0, back=False)
            with eng.Fori(1, NG - 1) as i:
                iteration(i)
            iteration(NG - 1, prep=False)
            iteration(NG, front=False)


_INS = ['x', 'adj', 'L0_gnn_bias', 'L1_gnn_bias', 'L2_gnn_bias', 'L3_gnn_W_lang', 'L3_gnn_W_grav', 'L3_gnn_W_V',
        'L3_gnn_W_O', 'L3_gnn_gate_logit', 'L3_gnn_log_sigma']
_OUT = (64, 128, 512)


def kernel(**inputs):
    import numpy as np
    import concourse.bacc as bacc
    from concourse.bass_utils import run_bass_kernel_spmd as run

    nc = bacc.Bacc("TRN2", target_bir_lowering=False, num_devices=1)
    arrays, args = {}, []
    for name in _INS:
        a = np.asarray(inputs[name])
        if a.ndim == 0:
            a = a.reshape(1, 1)
        a = np.ascontiguousarray(a)
        arrays[f"in_{name}"] = a
        args.append(nc.dram_tensor(f"in_{name}", a.shape, mybir.dt.from_np(a.dtype), kind="ExternalInput").ap())
    args.append(nc.dram_tensor("out_0", _OUT, F32, kind="ExternalOutput").ap())
    gnn_kernel(nc, *args)
    r = run(nc, [arrays], core_ids=[0])
    return r.results[0]["out_0"]
```

```python
import concourse.bass as bass
from concourse import mybir
from contextlib import ExitStack

F32 = mybir.dt.float32
F16 = mybir.dt.float16
ALU = mybir.AluOpType
ACT = mybir.ActivationFunctionType
AX = mybir.AxisListType


def gnn_kernel(nc, x, adj, bias0, bias1, bias2, w_lang, w_grav, w_v, w_o, gate_logit, log_sigma, out):
    NB, L, N = x.shape
    P = 128
    assert L == P
    T = N // P
    G = 4
    NG = NB // G
    K_KEEP = max(int(N * 0.3), 1)
    TOP_ROUNDS = (K_KEEP - 1) // 8
    TOP_REST = K_KEEP - 8 * TOP_ROUNDS
    LN_EPS = 1e-05
    NORM_EPS = 1e-08
    NEG = -(2.0 ** 100)
    XN_SCALE = 2.0 ** 8
    ADJ_SCALE = 2.0 ** 10
    W1_SCALE = 2.0 ** 8
    XW_SCALE = 2.0 ** 6
    AN_SCALE = 2.0 ** 10
    P_SCALE = 2.0 ** 6
    M_SCALE = 2.0 ** 8
    K_SCALE = 2.0 ** 8

    ctx = ExitStack()
    with ctx:
        ctx.enter_context(nc.allow_non_contiguous_dma(reason="biases of one element per partition"))

        def sb(name, shape, dt):
            return ctx.enter_context(nc.sbuf_tensor(name, shape, dt))

        def sem(name):
            return ctx.enter_context(nc.semaphore(name))

        bank = [ctx.enter_context(nc.psum_tensor(f"bank{i}", [P, N], F32)) for i in range(8)]

        ident = sb("ident", [P, P], F32)
        ones = sb("ones", [P, P], F32)
        zeros = sb("zeros", [P, P], F32)
        not_eye = sb("not_eye", [P, P], F32)
        adj_sb = sb("adj_sb", [P, P], F32)
        adj_off = sb("adj_off", [P, P], F32)
        adj_s = sb("adj_s", [P, P], F32)
        adj_hi = sb("adj_hi", [P, P], F16)
        adj_lo = sb("adj_lo", [P, P], F16)
        w1_f = sb("w1_f", [P, P], F32)
        w1_hi = sb("w1_hi", [P, P], F16)
        w1_lo = sb("w1_lo", [P, P], F16)
        bias0_col = sb("bias0_col", [P, 1], F32)
        bias1_row = sb("bias1_row", [P, N], F32)
        bias2_row = sb("bias2_row", [P, N], F32)
        gate = sb("gate", [P, 8], F32)
        an_hi = sb("an_hi", [P, T, N], F16)
        an_lo = sb("an_lo", [P, T, N], F16)
        pg_hi = sb("pg_hi", [P, T, N], F16)
        pg_lo = sb("pg_lo", [P, T, N], F16)
        pl_hi = sb("pl_hi", [P, T, N], F16)
        pl_lo = sb("pl_lo", [P, T, N], F16)
        m_hi = sb("m_hi", [P, T, N], F16)
        m_lo = sb("m_lo", [P, T, N], F16)

        x_in = sb("x_in", [P, G, N], F32)
        xb = sb("xb", [P, G, N], F32)
        x_hi = sb("x_hi", [P, G, N], F16)
        x_lo = sb("x_lo", [P, G, N], F16)
        xw_hi = sb("xw_hi", [P, 2, N], F16)
        xw_lo = sb("xw_lo", [P, 2, N], F16)
        t_sb = sb("t_sb", [P, G, N], F32)
        y_f = sb("y_f", [P, G, N], F32)
        y_hi = sb("y_hi", [P, G, N], F16)
        y_lo = sb("y_lo", [P, G, N], F16)
        h_two = [sb("h_sb0", [P, G, N], F32), sb("h_sb1", [P, G, N], F32)]
        ht_hi = sb("ht_hi", [P, T, N], F16)
        ht_lo = sb("ht_lo", [P, T, N], F16)
        yt_hi = sb("yt_hi", [P, 2, T, N], F16)
        yt_lo = sb("yt_lo", [P, 2, T, N], F16)
        u_hi = sb("u_hi", [P, G, N], F16)
        u_lo = sb("u_lo", [P, G, N], F16)
        t3 = sb("t3", [P, G, N], F32)
        o_sb = sb("o_sb", [P, G, N], F32)
        gram = sb("gram", [P, 2, N], F32)
        diag = sb("diag", [P, N], F32)
        half_dist = sb("half_dist", [P, N], F32)
        dist = sb("dist", [P, N], F32)
        expo = sb("expo", [P, N], F32)
        a_g = sb("a_g", [P, N], F32)
        a_l = sb("a_l", [P, N], F32)
        k_l = sb("k_l", [P, N], F32)
        deg_r = sb("deg_r", [P, G], F32)
        k_g = sb("k_g", [P, N], F32)
        k_sb = sb("k_sb", [P, N], F32)
        kt_hi = sb("kt_hi", [P, N], F16)
        kt_lo = sb("kt_lo", [P, N], F16)
        stats = sb("stats", [P, 4, G, 6], F32)
        mv = sb("mv", [P, 4, G, 2], F32)
        half_var = sb("half_var", [P, 4, G], F32)
        ln_v = sb("ln_v", [P, 5, G], F32)
        r0 = sb("r0", [P, 5, G], F32)
        r_t = sb("r_t", [P, 5, G], F32)
        rstd = sb("rstd", [P, 5, G], F32)
        nmr = sb("nmr", [P, 4, G], F32)
        sq = sb("sq", [P, 2, G], F32)
        sq_h = sb("sq_h", [P, G], F32)
        deg = sb("deg", [P, 2, G], F32)
        deg_c = sb("deg_c", [P, 2, G], F32)
        inv_deg = sb("inv_deg", [P, 2, G], F32)
        coef = sb("coef", [P, 2, G], F32)

        xa = [x_in, xb, h_two[1]]
        sqr = t_sb
        xn_f = y_f
        xn_hi, xn_lo = y_hi, y_lo
        ss = sb("ss", [P, G * T], F32)
        ssm = sb("ssm", [P, G * T], F32)
        rs = sb("rs", [P, 6, G * T], F32)
        s_sb = h_two[0]
        work = t3
        a_sb = o_sb
        w_stage = [y_f, t_sb, xb, x_in]
        wot = yt_hi[:, :, :, :].rearrange("p a t n -> p (a t n)").bitcast(F32).rearrange(
            "p (t n) -> p t n", t=T)
        prod_f = yt_lo[:, :, :, :].rearrange("p a t n -> p (a t n)").bitcast(F32).rearrange(
            "p (t n) -> p t n", t=T)
        an_f = prod_f
        top8 = sb("top8", [P, T, 8], F32)
        held = sb("held", [P, 2], F32)
        pool_held = sb("pool_held", [P, 1], F32)
        dcol = sb("dcol", [P, 8, T], F32)

        const_set = sem("const_set")
        small_in = sem("small_in")
        xa_in = [sem("xa_in0"), sem("xa_in1"), sem("xa_in2")]
        squared = sem("squared")
        x_turned = sem("x_turned")
        ss_done = sem("ss_done")
        rs_link = sem("rs_link")
        rs_sqrt = sem("rs_sqrt")
        rb_done = sem("rb_done")
        xn_done = sem("xn_done")
        xnhi_done = sem("xnhi_done")
        xnlo_done = sem("xnlo_done")
        sim_done = sem("sim_done")
        w_in = sem("w_in")
        s_copied = sem("s_copied")
        s_turned = sem("s_turned")
        s_mirrored = sem("s_mirrored")
        s_diag = sem("s_diag")
        top = sem("top")
        adj_made = sem("adj_made")
        a_done = sem("a_done")
        dg_done = sem("dg_done")
        dg_sqrt = sem("dg_sqrt")
        dg_link = sem("dg_link")
        db_done = sem("db_done")
        anf_done = sem("anf_done")
        anhi_done = sem("anhi_done")
        an_done = sem("an_done")
        wot_turned = sem("wot_turned")
        wot_done = sem("wot_done")
        prod_done = sem("prod_done")
        prod_f_done = sem("prod_f_done")
        prod_hi = sem("prod_hi")
        prod_lo = sem("prod_lo")
        gate_exp = sem("gate_exp")
        gate_done = sem("gate_done")
        x3_in = sem("x3_in")
        xhi_done = sem("xhi_done")
        xlo_done = sem("xlo_done")
        xb_done = sem("xb_done")
        pe_xw = sem("pe_xw")
        xwhi_done = sem("xwhi_done")
        xwlo_done = sem("xwlo_done")
        pe_mix = sem("pe_mix")
        mix_used = sem("mix_used")
        stat_done = sem("stat_done")
        dve_link = sem("dve_link")
        act_link = sem("act_link")
        var_ready = sem("var_ready")
        r0_ready = sem("r0_ready")
        norm_ready = sem("norm_ready")
        yhi_done = sem("yhi_done")
        yf_done = sem("yf_done")
        ylo_done = sem("ylo_done")
        h_done = sem("h_done")
        h_rest = sem("h_rest")
        pe_tr = sem("pe_tr")
        trhi_done = sem("trhi_done")
        tr_used = sem("tr_used")
        pe_wide = sem("pe_wide")
        widehi_done = sem("widehi_done")
        wide_used = sem("wide_used")
        pe_gram = sem("pe_gram")
        gram_done = sem("gram_done")
        gram_turned = sem("gram_turned")
        sum_ready = sem("sum_ready")
        al_scaled = sem("al_scaled")
        half_ready = sem("half_ready")
        pe_bc = sem("pe_bc")
        dist_done = sem("dist_done")
        exp_done = sem("exp_done")
        ag_done = sem("ag_done")
        cg_ready = sem("cg_ready")
        kg_done = sem("kg_done")
        k_done = sem("k_done")
        t3_done = sem("t3_done")
        st3_done = sem("st3_done")
        o_done = sem("o_done")
        out_sent = sem("out_sent")

        pool_link = sem("pool_link")
        XA = len(xa)
        assert NG % XA == 1
        RS_LINKS, DG_LINKS = 6, 9

        S_BANK = bank[0:4]
        XT_BANK = [bank[4], bank[7]]
        RB_BANK = [bank[5], bank[6]]
        XW_BANK = [bank[0], bank[6]]
        MIX_BANK = [bank[1], bank[2]]
        WIDE_BANK = [bank[3], bank[4]]
        GRAM_BANK = bank[6]
        BC_BANK = bank[7]

        GRAV, LANG = 0, 1
        def stages_before(i):
            if isinstance(i, int):
                return min(i, NG), max(i - 1, 0), max(i - 2, 0)
            return i, i - 1, i - 2

        def roles(i):
            return i < NG, 1 <= i <= NG, i >= 2

        def count_of(order, i, what):
            per = [sum(role == n for _, role in order) for n in range(3)]
            before = sum(n * m for n, m in zip(per, stages_before(i))) if isinstance(i, int) else (
                sum(per) * i - (per[1] + 2 * per[2]))
            here = roles(i) if isinstance(i, int) else (True, True, True)
            return before + [name for name, role in order if here[role]].index(what)

        FRONT, BACK, TAIL = 0, 1, 2
        R_ORDER = [("ln0", FRONT), ("ln1", FRONT), ("ln3", TAIL), ("lang", BACK), ("ln2", FRONT)]
        r_of = lambda i, what: count_of(R_ORDER, i, what)
        WIDE_ORDER = [("U3", TAIL), ("G0", BACK), ("G1", BACK), ("G2", BACK), ("G3", BACK), ("U0", BACK),
                      ("L0", BACK), ("L1", BACK), ("L2", BACK), ("L3", BACK), ("U1", BACK), ("U2", BACK)]
        YT = ("G", "L")
        wide_of = lambda i, what: count_of(WIDE_ORDER, i, what)
        wide_at = [w for w, _ in WIDE_ORDER].index
        WIDE = lambda what: WIDE_BANK[wide_at(what) % 2]
        MIX_ORDER = ([(f"A{b}", FRONT) for b in range(G)] + [(f"K{b}", TAIL) for b in range(G)]
                     + [(f"B{b}", FRONT) for b in range(G)] + [(f"C{b}", FRONT) for b in range(G)])
        mix_at = [w for w, _ in MIX_ORDER].index
        MIX = lambda what: MIX_BANK[mix_at(what) % 2]
        mix_of = lambda layer, i, b: count_of(MIX_ORDER, i, f"{'ABC'[layer]}{b}")
        ku_of = lambda i, b: count_of(MIX_ORDER, i, f"K{b}")

        def bank_free(order, bank_of, i, what):
            if not isinstance(i, int):
                return count_of(order, i, what) - 1
            everything = [(i1, w) for i1 in range(i + 1) for w, role in order if roles(i1)[role]]
            n = everything.index((i, what))
            return max([k + 1 for k in range(n) if bank_of(everything[k][1]) is bank_of(what)], default=0)

        LINKS = (10, 13, 15)

        def links_before(i):
            if isinstance(i, int):
                return sum(n * m for n, m in zip(LINKS, stages_before(i)))
            return sum(LINKS) * i - (LINKS[1] + 2 * LINKS[2])

        TR_ORDER = [("H0", BACK), ("H1", BACK), ("H2", BACK), ("H3", BACK), ("K", TAIL)]
        TR_BANK = {"H0": bank[5], "H1": bank[7], "H2": bank[5], "H3": bank[7], "K": bank[5]}
        TURNS = ((), (0, 1), (2, 3), ())
        tr_of = lambda i, what: count_of(TR_ORDER, i, what)

        def bcast_mid(ap, n):
            return ap.rearrange("p (a m) -> p a m", a=1).to_broadcast([P, n, ap.shape[1]])

        def bcast_last(ap, m):
            return ap.rearrange("p (n a) -> p n a", a=1).to_broadcast([P, ap.shape[1], m])

        def tiles(ap):
            return ap.rearrange("p (t m) -> p t m", t=T)

        block = ctx.enter_context(nc.Block())

        @block.sync
        def _(eng):
            def load_xa(q, u):
                eng.dma_start(xa[u][:, :, :],
                              x[bass.ds(q * G, G), :, :].rearrange("b p n -> p b n")).then_inc(xa_in[u], 16)

            for u in range(XA):
                load_xa(u, u)
            eng.dma_start(adj_sb[:, :], adj).then_inc(small_in, 16)
            eng.dma_start(bias0_col[:, :], bias0.rearrange("(p a) -> p a", a=1)).then_inc(small_in, 16)
            eng.dma_start(bias1_row[:, :], bias1.rearrange("(a n) -> a n", a=1).to_broadcast([P, N])).then_inc(small_in, 16)
            eng.dma_start(bias2_row[:, :], bias2.rearrange("(a n) -> a n", a=1).to_broadcast([P, N])).then_inc(small_in, 16)
            eng.dma_start(gate[:, 0:1], gate_logit.to_broadcast([P, 1])).then_inc(small_in, 16)
            eng.dma_start(gate[:, 1:2], log_sigma.to_broadcast([P, 1])).then_inc(small_in, 16)
            def next_xa(q, u):
                eng.wait_ge(xn_done, (q - XA + 1) * G)
                eng.wait_ge(x_turned, (q - XA + 1) * G)
                load_xa(q, u)

            with eng.Fori(1, NG // XA) as turn:
                for u in range(XA):
                    next_xa(XA * turn + u, u)
            next_xa(NG - 1, (NG - 1) % XA)
            eng.wait_ge(xn_done, NB)
            for stage, w in ((2, w_v), (3, w_o)):
                eng.dma_start(w_stage[stage][:, :, :], w.rearrange("(t p) n -> p t n", p=P)).then_inc(w_in, 16)
            eng.wait_ge(xnlo_done, NB)
            eng.wait_ge(xnhi_done, NB)
            eng.wait_ge(ss_done, NB)
            for stage, w in ((0, w_lang), (1, w_grav)):
                eng.dma_start(w_stage[stage][:, :, :], w.rearrange("(t p) n -> p t n", p=P)).then_inc(w_in, 16)

            def load_x(g):
                eng.dma_start(x_in[:, :, :], x[bass.ds(g * G, G), :, :].rearrange("b p n -> p b n")).then_inc(x3_in, 16)

            eng.wait_ge(wot_turned, T)
            load_x(0)

            def store(g):
                eng.wait_ge(o_done, G * (g + 1))
                eng.dma_start(out[bass.ds(G * g, G), :, :].rearrange("b p n -> p b n"), o_sb[:, :, :]).then_inc(out_sent, 16)

            def next_x(g):
                eng.wait_ge(xhi_done, G * g)
                eng.wait_ge(xlo_done, G * g)
                eng.wait_ge(xb_done, G * g)
                load_x(g)

            next_x(1)
            next_x(2)
            with eng.Fori(2, NG - 1) as i:
                next_x(i + 1)
                store(i - 2)
            for g in range(NG - 3, NG):
                store(g)
            eng.wait_ge(out_sent, 16 * NG)

        @block.tensor
        def _(eng):
            def product3(dst, a_hi, a_lo, b_hi, b_lo, start, stop):
                eng.matmul(dst, a_hi, b_hi, start=start, stop=False)
                eng.matmul(dst, a_hi, b_lo, start=False, stop=False)
                return eng.matmul(dst, a_lo, b_hi, start=False, stop=stop)

            def turn_x(q, u, b, loads=0, first=False):
                if b == 0:
                    eng.wait_ge(xa_in[u], 16 * loads)
                if not (first and b < 2):
                    eng.wait_ge(squared, q * G + b - 1)
                for t in range(T):
                    c = slice(t * P, (t + 1) * P)
                    last = eng.transpose(XT_BANK[b % 2][:, c], xa[u][:, b, c], ident[:, :])
                last.then_inc(x_turned, 1)

            def spread_norms(q, u, b, first=False):
                if b == 0:
                    eng.wait_ge(rs_link, (q + 1) * RS_LINKS)
                if not first:
                    eng.wait_ge(xn_done, q * G + b - 1)
                for t in range(T):
                    c = b * T + t
                    last = eng.transpose(RB_BANK[b % 2][:, t * P:(t + 1) * P],
                                         rs[:, 3 + u, c:c + 1].to_broadcast([P, P]), ident[:, :])
                last.then_inc(rb_done, 1)

            def similarity(q, b, first=False, end=False):
                eng.wait_ge(xnlo_done, q * G + b + 1)
                eng.wait_ge(xnhi_done, q * G + b + 1)
                for t in range(T):
                    c = slice(t * P, (t + 1) * P)
                    r = slice(t * P, N)
                    last = product3(S_BANK[t][:, t * P:N], xn_hi[:, b, c], xn_lo[:, b, c],
                                    xn_hi[:, b, r], xn_lo[:, b, r], start=first, stop=end)
                last.then_inc(sim_done, 1)

            def sim_group(q, u, loads=0, first=False, end=False):
                for b in range(G):
                    if b in (1, 2) and not end:
                        for b1 in (2 * b - 2, 2 * b - 1):
                            turn_x(q + 1, (u + 1) % XA, b1, loads)
                    spread_norms(q, u, b, first=first and b < 2)
                    if b < 2:
                        if not first:
                            similarity(q - 1, b + 2)
                    else:
                        similarity(q, b - 2, first=first and b == 2)
                if end:
                    similarity(q, 2)
                    similarity(q, 3, end=True)

            eng.wait_ge(const_set, 5)
            for b in range(G):
                turn_x(0, 0, b, loads=1, first=True)
            sim_group(0, 0, loads=1, first=True)
            with eng.Fori(0, NG // XA - 1) as turn:
                for u in range(1, XA + 1):
                    sim_group(XA * turn + u, u % XA, loads=turn + (u + 1) // XA + 1)
            for q in range(NG - XA, NG):
                sim_group(q, q % XA, loads=(q + 1) // XA + 1, end=q == NG - 1)

            for i in range(1, T):
                for j in range(i):
                    eng.wait_ge(s_copied, j + 1)
                    last = eng.transpose(bank[4 + i][:, j * P:(j + 1) * P], s_sb[:, j, i * P:(i + 1) * P], ident[:, :])
                last.then_inc(s_turned, 1)
            eng.wait_ge(w_in, 64)
            eng.wait_ge(s_copied, T)
            for f in range(T):
                if f >= 2:
                    eng.wait_ge(wot_done, f - 1)
                for e in range(T):
                    last = eng.transpose(bank[f % 2][:, e * P:(e + 1) * P],
                                         w_stage[3][:, f, e * P:(e + 1) * P], ident[:, :])
                last.then_inc(wot_turned, 1)
            eng.wait_ge(wot_done, T)
            k = 0
            for lhs, rhs in ((w_stage[1], w_stage[1]), (w_stage[0], w_stage[0]), (w_stage[2], wot)):
                for d in range(T):
                    if k >= 2:
                        eng.wait_ge(prod_hi, k - 1)
                    r = slice(d * P if lhs is rhs else 0, N)
                    for e in range(T):
                        last = eng.matmul(bank[2 + k % 2][:, r], lhs[:, e, d * P:(d + 1) * P], rhs[:, e, r],
                                          start=(e == 0), stop=(e == T - 1))
                    last.then_inc(prod_done, 1)
                    k += 1
            eng.wait_ge(a_done, T)
            for t in range(T):
                for s in range(T):
                    last = eng.matmul(bank[4][:, t:t + 1], a_sb[:, s, t * P:(t + 1) * P], ones[:, 0:1],
                                      start=(s == 0), stop=(s == T - 1))
            last.then_inc(dg_done, 1)
            eng.wait_ge(dg_link, DG_LINKS)
            eng.wait_ge(s_mirrored, T - 1)
            for t in range(T):
                last = eng.transpose(bank[5][:, t * P:(t + 1) * P], dcol[:, 4, t:t + 1].to_broadcast([P, P]), ident[:, :])
            last.then_inc(db_done, 1)

            def xw(g, b, first=False):
                n = G * g + b
                eng.wait_ge(xhi_done, n + 1)
                eng.wait_ge(xlo_done, n + 1)
                if b >= 2:
                    eng.wait_ge(xwlo_done, n - 1)
                if b == 1 and not first:
                    eng.wait_ge(sum_ready, g - 1)
                for t in range(T):
                    c = slice(t * P, (t + 1) * P)
                    last = product3(XW_BANK[b % 2][:, c], x_hi[:, b, c], x_lo[:, b, c], adj_hi[:, :], adj_lo[:, :],
                                    start=True, stop=True)
                last.then_inc(pe_xw, 1)

            def mix_bank(i, what):
                free = bank_free(MIX_ORDER, MIX, i, what)
                if not (isinstance(free, int) and free == 0):
                    eng.wait_ge(mix_used, free)

            def spread(i, b):
                eng.wait_ge(xwlo_done, G * i + b + 1)
                mix_bank(i, f"A{b}")
                for t in range(T):
                    c = slice(t * P, (t + 1) * P)
                    last = product3(MIX(f"A{b}")[:, :], xw_hi[:, b % 2, c], xw_lo[:, b % 2, c],
                                    an_hi[:, t, :], an_lo[:, t, :], start=(t == 0), stop=(t == T - 1))
                last.then_inc(pe_mix, 1)

            def mix(layer, i, b):
                eng.wait_ge(yhi_done, 2 * G * i + G * (layer - 1) + b + 1)
                eng.wait_ge(ylo_done, 2 * G * i + G * (layer - 1) + b + 1)
                what = f"{'ABC'[layer]}{b}"
                mix_bank(i, what)
                product3(MIX(what)[:, :], w1_hi[:, :], w1_lo[:, :], y_hi[:, b, :], y_lo[:, b, :],
                         start=True, stop=True).then_inc(pe_mix, 1)

            def turn_h(i, g, par, j):
                if j == 0:
                    eng.wait_ge(h_done, 2 * (g + 1))
                    eng.wait_ge(h_rest, 2 * (g + 1))
                    if not (isinstance(i, int) and i == 1):
                        eng.wait_ge(tr_used, tr_of(i, "H0"))
                if j == 1 and not (isinstance(i, int) and i == 1):
                    eng.wait_ge(al_scaled, g)
                if j >= 2:
                    eng.wait_ge(tr_used, tr_of(i, f"H{j - 2}") + 1)
                for b in range(G):
                    last = eng.transpose(TR_BANK[f"H{j}"][:, b * P:(b + 1) * P], h_two[par][:, b, j * P:(j + 1) * P],
                                         ident[:, :])
                last.then_inc(pe_tr, 1)

            def wide_bank(i, what):
                free = bank_free(WIDE_ORDER, WIDE, i, what)
                if not (isinstance(free, int) and free == 0):
                    eng.wait_ge(wide_used, free)

            def yt(i, which, j):
                if which == GRAV and j == 0:
                    eng.wait_ge(tr_used, tr_of(i, "H3") + 1)
                what = f"{YT[which]}{j}"
                wide_bank(i, what)
                p_hi, p_lo = ((pg_hi, pg_lo), (pl_hi, pl_lo))[which]
                c = slice(j * P, (j + 1) * P)
                for d in range(j + 1):
                    last = product3(WIDE(what)[:, :], p_hi[:, d, c], p_lo[:, d, c], ht_hi[:, d, :], ht_lo[:, d, :],
                                    start=(d == 0), stop=(d == j))
                last.then_inc(pe_wide, 1)

            def grams(i, which, g, first=False):
                eng.wait_ge(wide_used, wide_of(i, f"{YT[which]}{T - 1}") + 1)
                if not first:
                    eng.wait_ge(gram_done, 2 * g + which)
                for b in range(G):
                    c = slice(b * P, (b + 1) * P)
                    for j in range(T):
                        last = product3(GRAM_BANK[:, c], yt_hi[:, which, j, c], yt_lo[:, which, j, c],
                                        ht_hi[:, j, c], ht_lo[:, j, c], start=(j == 0), stop=(j == T - 1))
                last.then_inc(pe_gram, 1)

            def u_product(i, b):
                wide_bank(i, f"U{b}")
                c = slice(b * P, (b + 1) * P)
                for d in range(T):
                    last = product3(WIDE(f"U{b}")[:, :], ht_hi[:, d, c], ht_lo[:, d, c], m_hi[:, d, :], m_lo[:, d, :],
                                    start=(d == 0), stop=(d == T - 1))
                last.then_inc(pe_wide, 1)

            def turn_half_distances(i, g):
                eng.wait_ge(half_ready, g + 1)
                eng.wait_ge(tr_used, tr_of(i, "H3") + 1)
                for b in range(G):
                    c = slice(b * P, (b + 1) * P)
                    last = eng.transpose(BC_BANK[:, c], half_dist[:, c], ident[:, :])
                last.then_inc(pe_bc, 1)

            def turn_gram(g):
                eng.wait_ge(gram_done, 2 * g + LANG + 1)
                for b in range(G):
                    c = slice(b * P, (b + 1) * P)
                    last = eng.transpose(GRAM_BANK[:, c], gram[:, LANG, c], ident[:, :])
                last.then_inc(gram_turned, 1)

            def spread_norm_column(g):
                eng.wait_ge(norm_ready, r_of(g + 1, "lang") + 1)
                eng.wait_ge(dist_done, g + 1)
                for b in range(G):
                    last = eng.transpose(BC_BANK[:, b * P:(b + 1) * P], rstd[:, 4, b:b + 1].to_broadcast([P, P]),
                                         ident[:, :])
                last.then_inc(pe_bc, 1)

            def turn_k(i, g):
                eng.wait_ge(k_done, g + 1)
                if not (isinstance(i, int) and i == NG + 1):
                    eng.wait_ge(tr_used, tr_of(i, "H2") + 1)
                for b in range(G):
                    c = slice(b * P, (b + 1) * P)
                    last = eng.transpose(TR_BANK["K"][:, c], k_sb[:, c], ident[:, :])
                last.then_inc(pe_tr, 1)

            def ku(i, b):
                if b == 0:
                    eng.wait_ge(tr_used, tr_of(i, "K") + 1)
                eng.wait_ge(wide_used, wide_of(i, "U3") + 1)
                mix_bank(i, f"K{b}")
                c = slice(b * P, (b + 1) * P)
                product3(MIX(f"K{b}")[:, :], kt_hi[:, c], kt_lo[:, c], u_hi[:, b, :], u_lo[:, b, :],
                         start=True, stop=True).then_inc(pe_mix, 1)

            def iteration(i, par, front=True, back=True, tail=True):
                g, c = i - 1, i - 2
                first_back = back and not tail
                if front:
                    xw(i, 0)
                if tail:
                    u_product(i, 3)
                if front:
                    xw(i, 1, first=not tail)
                if tail:
                    spread_norm_column(c)
                for b in range(G):
                    if front:
                        spread(i, b)
                        if b + 2 < G:
                            xw(i, b + 2)
                    if back:
                        for j in TURNS[b]:
                            turn_h(i, g, 1 - par, j)
                if tail:
                    turn_k(i, c)
                if back:
                    yt(i, GRAV, 0)
                    yt(i, GRAV, 1)
                if tail:
                    ku(i, 0)
                if back:
                    yt(i, GRAV, 2)
                if tail:
                    ku(i, 1)
                if back:
                    yt(i, GRAV, 3)
                if tail:
                    ku(i, 2)
                if back:
                    u_product(i, 0)
                if tail:
                    ku(i, 3)
                if front:
                    mix(1, i, 0)
                    mix(1, i, 1)
                if back:
                    grams(i, GRAV, g, first=first_back)
                if front:
                    mix(1, i, 2)
                    mix(1, i, 3)
                if back:
                    for j in range(T):
                        yt(i, LANG, j)
                    u_product(i, 1)
                    turn_half_distances(i, g)
                    grams(i, LANG, g)
                if front:
                    mix(2, i, 0)
                    mix(2, i, 1)
                if back:
                    u_product(i, 2)
                    turn_gram(g)
                if front:
                    mix(2, i, 2)
                    mix(2, i, 3)

            eng.wait_ge(an_done, T)
            eng.wait_ge(adj_made, 2)
            eng.wait_ge(prod_lo, 3 * T)
            iteration(0, 0, back=False, tail=False)
            iteration(1, 1, tail=False)
            with eng.Fori(1, NG // 2) as pair:
                iteration(2 * pair, 0)
                iteration(2 * pair + 1, 1)
            iteration(NG, 0, front=False)
            iteration(NG + 1, 1, front=False, back=False)

        @block.scalar
        def _(eng):
            def square(q, b, first=False):
                eng.wait_ge(x_turned, q * G + b + 1)
                if not first:
                    eng.wait_ge(ss_done, (q - 1) * G + b + 1)
                eng.activation(sqr[:, b, :], XT_BANK[b % 2][:, :], ACT.Square).then_inc(squared, 1)

            def root(q):
                eng.wait_ge(rs_link, q * RS_LINKS + 1)
                eng.activation(rs[:, 0, :], ssm[:, :], ACT.Sqrt).then_inc(rs_sqrt, 1)

            def split_hi(q, b, first=False):
                eng.wait_ge(xn_done, q * G + b + 1)
                if not first:
                    eng.wait_ge(sim_done, (q - 1) * G + b + 1)
                eng.activation(xn_hi[:, b, :], xn_f[:, b, :], ACT.Copy).then_inc(xnhi_done, 1)

            def norm_group(q, first=False, end=False):
                for b in range(G):
                    split_hi(q, b, first)
                    if b < 2 and not end:
                        square(q + 1, 2 * b)
                        square(q + 1, 2 * b + 1)
                    if b == 1 and not end:
                        root(q + 1)

            for b in range(G):
                square(0, b, first=True)
            root(0)
            norm_group(0, first=True)
            with eng.Fori(1, NG - 1) as q:
                norm_group(q)
            norm_group(NG - 1, end=True)

            eng.wait_ge(sim_done, NB)
            for t in range(T):
                eng.activation(s_sb[:, t, t * P:N], S_BANK[t][:, t * P:N], ACT.Copy,
                               scale=1.0 / (XN_SCALE * XN_SCALE * NB)).then_inc(s_copied, 1)
            for i in range(1, T):
                eng.wait_ge(s_turned, i)
                eng.activation(s_sb[:, i, 0:i * P], bank[4 + i][:, 0:i * P], ACT.Copy).then_inc(s_mirrored, 1)
            for f in range(T):
                eng.wait_ge(wot_turned, f + 1)
                eng.activation(wot[:, :, f * P:(f + 1) * P], tiles(bank[f % 2][:, :]), ACT.Copy).then_inc(wot_done, 1)
            k = 0
            for dst, scale in ((pg_hi, P_SCALE), (pl_hi, P_SCALE), (m_hi, M_SCALE)):
                for d in range(T):
                    eng.wait_ge(prod_done, k + 1)
                    if k >= T:
                        eng.wait_ge(prod_lo, k - T + 1)
                    diagonal = slice(d * P, (d + 1) * P)
                    src = bank[2 + k % 2]
                    if dst is m_hi:
                        eng.activation(prod_f[:, k % T, :], src[:, :], ACT.Copy, scale=scale).then_inc(prod_f_done, 1)
                        eng.activation(dst[:, d, :], src[:, :], ACT.Copy, scale=scale).then_inc(prod_hi, 1)
                    else:
                        r = slice((d + 1) * P, N)
                        if d < T - 1:
                            eng.activation(prod_f[:, k % T, r], src[:, r], ACT.Copy, scale=scale)
                            eng.activation(dst[:, d, r], src[:, r], ACT.Copy, scale=scale)
                        eng.activation(prod_f[:, k % T, diagonal], src[:, diagonal], ACT.Copy, scale=scale / 2).then_inc(prod_f_done, 1)
                        eng.activation(dst[:, d, diagonal], src[:, diagonal], ACT.Copy, scale=scale / 2).then_inc(prod_hi, 1)
                    k += 1
            eng.wait_ge(dg_link, 1)
            eng.activation(dcol[:, 1, :], dcol[:, 0, :], ACT.Sqrt).then_inc(dg_sqrt, 1)
            for t in range(T):
                eng.wait_ge(anf_done, t + 1)
                eng.activation(an_hi[:, t, :], an_f[:, t, :], ACT.Copy).then_inc(anhi_done, 1)

            eng.preload_act_table_set("natural_log_exp_and_others")
            eng.wait_ge(small_in, 96)
            eng.activation(gate[:, 2:3], gate[:, 0:1], ACT.Exp, scale=-1.0).then_inc(gate_exp, 1)
            eng.activation(gate[:, 3:4], gate[:, 1:2], ACT.Exp, scale=-2.0).then_inc(gate_exp, 1)

            def x_split(g, b, first=False):
                if b == 0:
                    eng.wait_ge(x3_in, 16 * (g + 1))
                if not first:
                    eng.wait_ge(pe_xw, G * (g - 1) + b + 1)
                eng.activation(x_hi[:, b, :], x_in[:, b, :], ACT.Copy).then_inc(xhi_done, 1)

            def xw_split(g, b, first=False):
                eng.wait_ge(pe_xw, G * g + b + 1)
                if not first:
                    eng.wait_ge(pe_mix, mix_of(0, g, b - 2) + 1 if b >= 2 else mix_of(0, g - 1, b + 2) + 1)
                eng.activation(xw_hi[:, b % 2, :], XW_BANK[b % 2][:, :], ACT.Copy, scale=XW_SCALE / ADJ_SCALE).then_inc(xwhi_done, 1)

            def root_of(i, what):
                row = {"ln0": 0, "ln1": 1, "ln2": 2, "ln3": 3, "lang": 4}[what]
                k = r_of(i, what)
                eng.wait_ge(var_ready, k + 1)
                src = half_var[:, row, :] if row < 4 else sq_h[:, :]
                eng.activation(ln_v[:, row, :], src, ACT.Ln, scale=-2.0).then_inc(act_link, 1)
                eng.wait_ge(act_link, k + 1)
                eng.activation(r0[:, row, :], ln_v[:, row, :], ACT.Exp, scale=-0.5).then_inc(r0_ready, 1)

            def y_row(layer, i, b):
                if b == 0:
                    eng.wait_ge(norm_ready, r_of(i, f"ln{layer}") + 1)
                eng.activation(y_hi[:, b, :], t_sb[:, b, :], ACT.Identity, bias=nmr[:, layer, b:b + 1],
                               scale=rstd[:, layer, b:b + 1]).then_inc(yhi_done, 1)

            def turned_split(dst, i, what, scale):
                eng.wait_ge(pe_tr, tr_of(i, what) + 1)
                eng.activation(dst, TR_BANK[what][:, :], ACT.Copy, scale=scale).then_inc(trhi_done, 1)

            def wide_split(dst, i, what, scale):
                eng.wait_ge(pe_wide, wide_of(i, what) + 1)
                eng.activation(dst, WIDE(what)[:, :], ACT.Copy, scale=scale).then_inc(widehi_done, 1)

            def yt_split(i, which, j):
                wide_split(yt_hi[:, which, j, :], i, f"{YT[which]}{j}", 1.0 / P_SCALE)

            def u_split(i, b):
                wide_split(u_hi[:, b, :], i, f"U{b}", 1.0 / M_SCALE)

            def h_row(i, par, g, b):
                if b == 0:
                    eng.wait_ge(norm_ready, r_of(g, "ln2") + 1)
                eng.activation(h_two[par][:, b, :], t_sb[:, b, :], ACT.Identity, bias=nmr[:, 2, b:b + 1],
                               scale=rstd[:, 2, b:b + 1]).then_inc(h_done, 1)

            def output(i, g):
                eng.wait_ge(norm_ready, r_of(i, "ln3") + 1)
                if not (isinstance(g, int) and g == 0):
                    eng.wait_ge(out_sent, 16 * g)
                for b in range(G):
                    eng.activation(o_sb[:, b, :], t3[:, b, :], ACT.Identity, bias=nmr[:, 3, b:b + 1],
                                   scale=rstd[:, 3, b:b + 1]).then_inc(o_done, 1)

            def iteration(i, par, front=True, back=True, tail=True, prep=True):
                g, c = i - 1, i - 2
                first_front = front and not back and not tail
                if front:
                    xw_split(i, 0, first_front)
                if tail:
                    u_split(i, 3)
                if front:
                    xw_split(i, 1, first_front)
                if back:
                    root_of(g, "ln2")
                if back:
                    h_row(i, 1 - par, g, 0)
                    h_row(i, 1 - par, g, 1)
                if front:
                    xw_split(i, 2)
                    xw_split(i, 3)
                if back:
                    for j in range(T):
                        turned_split(ht_hi[:, j, :], i, f"H{j}", 1.0)
                if not (isinstance(i, int) and i < 3):
                    output(i - 1, i - 3)
                if tail:
                    turned_split(kt_hi[:, :], i, "K", K_SCALE)
                if back:
                    yt_split(i, GRAV, 0)
                    yt_split(i, GRAV, 1)
                if back:
                    yt_split(i, GRAV, 2)
                if front:
                    root_of(i, "ln0")
                    y_row(0, i, 0)
                    y_row(0, i, 1)
                if back:
                    yt_split(i, GRAV, 3)
                if front:
                    y_row(0, i, 2)
                    y_row(0, i, 3)
                if back:
                    u_split(i, 0)
                if front and prep:
                    for b in range(G):
                        x_split(i + 1, b)
                if back:
                    eng.wait_ge(pe_gram, 2 * g + GRAV + 1)
                    eng.activation(gram[:, GRAV, :], GRAM_BANK[:, :], ACT.Copy, scale=-2.0).then_inc(gram_done, 1)
                    yt_split(i, LANG, 0)
                    yt_split(i, LANG, 1)
                if front:
                    root_of(i, "ln1")
                if back:
                    yt_split(i, LANG, 2)
                if back:
                    yt_split(i, LANG, 3)
                if front:
                    y_row(1, i, 0)
                    y_row(1, i, 1)
                    y_row(1, i, 2)
                    y_row(1, i, 3)
                if tail:
                    root_of(i, "ln3")
                if back:
                    u_split(i, 1)
                    eng.wait_ge(pe_gram, 2 * g + LANG + 1)
                    eng.activation(gram[:, LANG, :], GRAM_BANK[:, :], ACT.Copy).then_inc(gram_done, 1)
                    eng.wait_ge(dist_done, g + 1)
                    eng.activation(expo[:, :], dist[:, :], ACT.Exp, scale=gate[:, 5:6]).then_inc(exp_done, 1)
                    root_of(i, "lang")
                    u_split(i, 2)

            for b in range(G):
                x_split(0, b, first=True)
            iteration(0, 0, back=False, tail=False)
            iteration(1, 1, tail=False)
            iteration(2, 0)
            iteration(3, 1)
            with eng.Fori(2, NG // 2 - 1) as pair:
                iteration(2 * pair, 0)
                iteration(2 * pair + 1, 1)
            iteration(NG - 2, 0)
            iteration(NG - 1, 1, prep=False)
            iteration(NG, 0, front=False)
            iteration(NG + 1, 1, front=False, back=False)
            output(NG + 1, NG - 1)

        @block.vector
        def _(eng):
            def sum_squares(q, b):
                eng.wait_ge(squared, q * G + b + 1)
                if b == 0 and not (isinstance(q, int) and q == 0):
                    eng.wait_ge(rs_link, q * RS_LINKS)
                eng.tensor_reduce(ss[:, b * T:(b + 1) * T], tiles(sqr[:, b, :]), AX.X, ALU.add).then_inc(ss_done, 1)

            def norms(q, u, meanwhile=None):
                k = [0]

                def link(ins):
                    k[0] += 1
                    ins.then_inc(rs_link, 1)
                    if k[0] < RS_LINKS:
                        eng.wait_ge(rs_link, q * RS_LINKS + k[0])

                eng.wait_ge(ss_done, G * (q + 1))
                link(eng.tensor_scalar(ssm[:, :], ss[:, :], 1e-24, None, ALU.max))
                if meanwhile:
                    meanwhile()
                eng.wait_ge(rs_sqrt, q + 1)
                link(eng.reciprocal(rs[:, 1, :], rs[:, 0, :]))
                link(eng.tensor_tensor(rs[:, 2, :], rs[:, 1, :], ssm[:, :], ALU.mult))
                link(eng.tensor_tensor(rs[:, 2, :], rs[:, 2, :], rs[:, 1, :], ALU.mult))
                link(eng.tensor_scalar(rs[:, 2, :], rs[:, 2, :], -0.5 * XN_SCALE, 1.5 * XN_SCALE, ALU.mult, ALU.add))
                link(eng.tensor_tensor(rs[:, 3 + u, :], rs[:, 2, :], rs[:, 1, :], ALU.mult))
                assert k[0] == RS_LINKS

            def normalise(q, u, b, first=False):
                eng.wait_ge(rb_done, q * G + b + 1)
                if not first:
                    eng.wait_ge(xnlo_done, (q - 1) * G + b + 1)
                    eng.wait_ge(xnhi_done, (q - 1) * G + b + 1)
                eng.tensor_tensor(xn_f[:, b, :], RB_BANK[b % 2][:, :], xa[u][:, b, :], ALU.mult).then_inc(xn_done, 1)

            def norm_group(q, u, first=False, end=False):
                normalise(q, u, 0, first)
                if not end:
                    sum_squares(q + 1, 0)
                normalise(q, u, 1, first)
                if not end:
                    for b in range(1, G):
                        sum_squares(q + 1, b)
                    norms(q + 1, (u + 1) % XA, meanwhile=lambda: normalise(q, u, 2, first))
                else:
                    normalise(q, u, 2, first)
                normalise(q, u, 3, first)

            for b in range(G):
                sum_squares(0, b)
            norms(0, 0)
            norm_group(0, 0, first=True)
            with eng.Fori(0, NG // XA - 1) as turn:
                for u in range(1, XA + 1):
                    norm_group(XA * turn + u, u % XA)
            for q in range(NG - XA, NG):
                norm_group(q, q % XA, end=q == NG - 1)

            def find(t):
                eng.max(top8[:, t, :], work[:, t, :]).then_inc(top, 1)

            def mark(t):
                eng.match_replace(out=work[:, t, :], in_to_replace=top8[:, t, :], in_values=work[:, t, :],
                                  imm_value=NEG).then_inc(top, 1)

            def all_tiles(step, before):
                eng.wait_ge(top, before)
                eng.memset(held[:, 0:1], 0.0)
                for t in range(T):
                    step(t)

            for t in range(T):
                eng.wait_ge(s_diag, 2 * t + 1)
                find(t)
            all_tiles(mark, T)
            with eng.Fori(1, TOP_ROUNDS) as r:
                all_tiles(find, 2 * T * r)
                all_tiles(mark, 2 * T * r + T)
            all_tiles(find, 2 * T * TOP_ROUNDS)
            eng.wait_ge(top, 2 * T * TOP_ROUNDS + T)
            eng.memset(top8[:, :, TOP_REST:8], NEG).then_inc(top, 1)
            all_tiles(mark, 2 * T * TOP_ROUNDS + T + 1)
            for t in range(T):
                eng.wait_ge(top, 2 * T * TOP_ROUNDS + T + t + 2)
                eng.wait_ge(s_diag, 2 * t + 2)
                eng.scalar_tensor_tensor(out=a_sb[:, t, :], in0=work[:, t, :], scalar=NEG, in1=s_sb[:, t, :],
                                         op0=ALU.is_equal, op1=ALU.mult).then_inc(a_done, 1)
            k = [0]

            def dg(ins):
                k[0] += 1
                ins.then_inc(dg_link, 1)
                eng.wait_ge(dg_link, k[0])

            eng.wait_ge(dg_done, 1)
            dg(eng.tensor_scalar(dcol[:, 0, :], bank[4][:, 0:T], 2.0 ** -110, None, ALU.max))
            dg(eng.tensor_scalar(dcol[:, 6, :], bank[4][:, 0:T], 0.0, None, ALU.is_gt))
            eng.wait_ge(dg_sqrt, 1)
            dg(eng.reciprocal(dcol[:, 2, :], dcol[:, 1, :]))
            dg(eng.tensor_tensor(dcol[:, 3, :], dcol[:, 2, :], dcol[:, 0, :], ALU.mult))
            dg(eng.tensor_tensor(dcol[:, 3, :], dcol[:, 3, :], dcol[:, 2, :], ALU.mult))
            dg(eng.tensor_scalar(dcol[:, 3, :], dcol[:, 3, :], -0.5, 1.5, ALU.mult, ALU.add))
            dg(eng.tensor_tensor(dcol[:, 3, :], dcol[:, 3, :], dcol[:, 2, :], ALU.mult))
            dg(eng.tensor_tensor(dcol[:, 4, :], dcol[:, 3, :], dcol[:, 6, :], ALU.mult))
            dg(eng.tensor_scalar(dcol[:, 5, :], dcol[:, 4, :], AN_SCALE, None, ALU.mult))
            assert k[0] == DG_LINKS
            eng.wait_ge(db_done, 1)
            eng.wait_ge(prod_lo, 3 * T)
            for t in range(T):
                eng.scalar_tensor_tensor(out=an_f[:, t, :], in0=a_sb[:, t, :], scalar=dcol[:, 5, t:t + 1],
                                         in1=bank[5][:, :], op0=ALU.mult, op1=ALU.mult).then_inc(anf_done, 1)
            for t in range(T):
                eng.wait_ge(anhi_done, t + 1)
                eng.tensor_tensor(an_lo[:, t, :], an_f[:, t, :], an_hi[:, t, :], ALU.subtract).then_inc(an_done, 1)

            eng.wait_ge(gate_exp, 2)
            eng.tensor_scalar(gate[:, 4:5], gate[:, 2:3], 1.0, None, ALU.add).then_inc(gate_done, 1)
            eng.tensor_scalar(gate[:, 5:6], gate[:, 3:4], -0.5, None, ALU.mult).then_inc(gate_done, 1)
            eng.wait_ge(gate_done, 2)
            eng.reciprocal(gate[:, 6:7], gate[:, 4:5]).then_inc(gate_done, 1)
            eng.wait_ge(gate_done, 3)
            eng.tensor_scalar(gate[:, 7:8], gate[:, 6:7], -1.0, 1.0, ALU.mult, ALU.add).then_inc(gate_done, 1)
            eng.wait_ge(gate_done, 4)

            def iteration(i, par, front=True, back=True, tail=True):
                g, c = i - 1, i - 2
                base = links_before(i)
                k = [0]

                def link(ins):
                    k[0] += 1
                    ins.then_inc(dve_link, 1)
                    eng.wait_ge(dve_link, base + k[0])

                def xw_rest(b):
                    eng.wait_ge(xwhi_done, G * i + b + 1)
                    eng.scalar_tensor_tensor(out=xw_lo[:, b % 2, :], in0=XW_BANK[b % 2][:, :], scalar=XW_SCALE / ADJ_SCALE,
                                             in1=xw_hi[:, b % 2, :], op0=ALU.mult, op1=ALU.subtract).then_inc(xwlo_done, 1)

                def add_up(layer, b):
                    m = mix_of(layer, i, b)
                    eng.wait_ge(pe_mix, m + 1)
                    if layer == 0:
                        eng.wait_ge(xb_done, G * i + b + 1)
                        if not (isinstance(i, int) and i == 0):
                            eng.wait_ge((h_done, h_rest)[b // 2], 2 * (i - 1) + b % 2 + 1)
                        scale, other = 1.0 / (XW_SCALE * AN_SCALE), xb[:, b, :]
                    else:
                        eng.wait_ge(ylo_done, 2 * G * i + G * (layer - 1) + b + 1)
                        scale, other = 1.0 / W1_SCALE, (bias1_row, bias2_row)[layer - 1][:, :]
                    eng.scalar_tensor_tensor(out=t_sb[:, b, :], in0=MIX(f"{'ABC'[layer]}{b}")[:, :], scalar=scale,
                                             in1=other, op0=ALU.mult, op1=ALU.add).then_inc(mix_used, 1)

                def measure(layer, b, at=i):
                    eng.wait_ge(mix_used, mix_of(layer, at, b) + 1)
                    eng.bn_stats(stats[:, layer, b, :], t_sb[:, b, :]).then_inc(stat_done, 1)

                def two_sums(layer, b):
                    add_up(layer, b)
                    add_up(layer, b + 1)
                    measure(layer, b)
                    measure(layer, b + 1)

                def refine(row, at, what, source):
                    eng.wait_ge(r0_ready, r_of(at, what) + 1)
                    link(eng.tensor_tensor(r_t[:, row, :], r0[:, row, :], r0[:, row, :], ALU.mult))
                    link(eng.tensor_tensor(r_t[:, row, :], r_t[:, row, :], source, ALU.mult))
                    return eng.scalar_tensor_tensor(out=rstd[:, row, :], in0=r_t[:, row, :], scalar=1.5,
                                                    in1=r0[:, row, :], op0=ALU.add, op1=ALU.mult)

                def variance(layer, of):
                    if layer < 3:
                        eng.wait_ge(stat_done, 3 * G * of + G * (layer + 1))
                    else:
                        eng.wait_ge(st3_done, G * of + G)
                    eng.memset(held[:, 1:2], 0.0)
                    for b in range(G):
                        ins = eng.bn_aggr(mv[:, layer, b, :], stats[:, layer, b, :])
                    link(ins)
                    eng.tensor_scalar(half_var[:, layer, :], mv[:, layer, :, 1], LN_EPS, -0.5, ALU.add, ALU.mult).then_inc(var_ready, 1)

                def norm(layer, at):
                    link(refine(layer, at, f"ln{layer}", half_var[:, layer, :]))
                    link(eng.scalar_tensor_tensor(out=nmr[:, layer, :], in0=mv[:, layer, :, 0], scalar=-1.0,
                                                  in1=rstd[:, layer, :], op0=ALU.mult, op1=ALU.mult))
                    eng.tensor_copy(r_t[:, layer, 0:1], rstd[:, layer, 0:1]).then_inc(norm_ready, 1)

                def turned_rest(dst, hi, what, scale):
                    eng.wait_ge(trhi_done, tr_of(i, what) + 1)
                    eng.scalar_tensor_tensor(out=dst, in0=TR_BANK[what][:, :], scalar=scale, in1=hi,
                                             op0=ALU.mult, op1=ALU.subtract).then_inc(tr_used, 1)

                def wide_rest(dst, hi, at, what, scale):
                    eng.wait_ge(widehi_done, wide_of(at, what) + 1)
                    eng.scalar_tensor_tensor(out=dst, in0=WIDE(what)[:, :], scalar=scale, in1=hi,
                                             op0=ALU.mult, op1=ALU.subtract).then_inc(wide_used, 1)

                def yt_rest(which, j):
                    wide_rest(yt_lo[:, which, j, :], yt_hi[:, which, j, :], i, f"{YT[which]}{j}", 1.0 / P_SCALE)

                def u_rest(at, b):
                    wide_rest(u_lo[:, b, :], u_hi[:, b, :], at, f"U{b}", 1.0 / M_SCALE)

                def diagonal_sums(which):
                    eng.wait_ge(gram_done, 2 * g + which + 1)
                    link(eng.tensor_tensor(tiles(diag[:, :]), tiles(gram[:, which, :]), bcast_mid(ident[:, :], G), ALU.mult))
                    link(eng.tensor_reduce(sq[:, which, :], tiles(diag[:, :]), AX.X, ALU.add))

                def last_sum(b):
                    eng.wait_ge(pe_mix, ku_of(i, b) + 1)
                    if not (isinstance(i, int) and i == 2):
                        eng.wait_ge(o_done, G * (c - 1) + b + 1)
                    eng.scalar_tensor_tensor(out=t3[:, b, :], in0=MIX(f"K{b}")[:, :], scalar=1.0 / K_SCALE,
                                             in1=h_two[par][:, b, :], op0=ALU.mult, op1=ALU.add).then_inc(mix_used, 1)

                def last_measure(b):
                    eng.wait_ge(mix_used, ku_of(i, b) + 1)
                    eng.bn_stats(stats[:, 3, b, :], t3[:, b, :]).then_inc(st3_done, 1)

                if front:
                    xw_rest(0)
                if back:
                    measure(2, 2, g)
                    measure(2, 3, g)
                    variance(2, g)
                if front:
                    xw_rest(1)
                if tail:
                    eng.wait_ge(sum_ready, c + 1)
                    link(eng.scalar_tensor_tensor(out=tiles(a_l[:, :]), in0=tiles(diag[:, :]), scalar=0.0,
                                                  in1=bcast_mid(adj_off[:, :], G), op0=ALU.max, op1=ALU.mult))
                if back:
                    norm(2, g)
                if tail:
                    eng.wait_ge(ag_done, c + 1)
                    link(eng.tensor_reduce(deg[:, 0, :], tiles(a_g[:, :]), AX.X, ALU.add))
                    link(eng.tensor_scalar(deg_c[:, 0, :], deg[:, 0, :], NORM_EPS, None, ALU.max))
                    link(eng.reciprocal(inv_deg[:, 0, :], deg_c[:, 0, :]))
                    eng.tensor_scalar(coef[:, 0, :], inv_deg[:, 0, :], gate[:, 7:8], None, ALU.mult).then_inc(cg_ready, 1)
                    u_rest(i - 1, 2)
                    u_rest(i, 3)
                if front:
                    add_up(0, 0)
                if tail:
                    eng.wait_ge(pe_bc, 2 * c + 2)
                    eng.tensor_tensor(a_l[:, :], BC_BANK[:, :], a_l[:, :], ALU.mult).then_inc(al_scaled, 1)
                if front:
                    xw_rest(2)
                if tail:
                    eng.wait_ge(al_scaled, c + 1)
                    link(eng.tensor_reduce(deg[:, 1, :], tiles(a_l[:, :]), AX.X, ALU.add))
                    link(eng.tensor_tensor(deg_r[:, :], deg[:, 1, :], rstd[:, 4, :], ALU.mult))
                    link(eng.tensor_scalar(deg_c[:, 1, :], deg_r[:, :], NORM_EPS, None, ALU.max))
                    link(eng.reciprocal(inv_deg[:, 1, :], deg_c[:, 1, :]))
                    link(eng.scalar_tensor_tensor(out=coef[:, 1, :], in0=inv_deg[:, 1, :], scalar=gate[:, 6:7],
                                                  in1=rstd[:, 4, :], op0=ALU.mult, op1=ALU.mult))
                if back:
                    turned_rest(ht_lo[:, 0, :], ht_hi[:, 0, :], "H0", 1.0)
                if front:
                    xw_rest(3)
                if back:
                    turned_rest(ht_lo[:, 1, :], ht_hi[:, 1, :], "H1", 1.0)
                if front:
                    add_up(0, 1)
                if tail:
                    link(eng.tensor_tensor(tiles(k_l[:, :]), tiles(a_l[:, :]), bcast_last(coef[:, 1, :], P), ALU.mult))
                    eng.wait_ge(kg_done, c + 1)
                    eng.tensor_tensor(k_sb[:, :], k_l[:, :], k_g[:, :], ALU.add).then_inc(k_done, 1)
                if front:
                    add_up(0, 2)
                if back:
                    for j in TURNS[2]:
                        turned_rest(ht_lo[:, j, :], ht_hi[:, j, :], f"H{j}", 1.0)
                if front:
                    add_up(0, 3)
                    measure(0, 0)
                if tail:
                    turned_rest(kt_lo[:, :], kt_hi[:, :], "K", K_SCALE)
                if back:
                    yt_rest(GRAV, 0)
                if front:
                    measure(0, 1)
                if back:
                    yt_rest(GRAV, 1)
                if tail:
                    last_sum(0)
                if front:
                    measure(0, 2)
                    measure(0, 3)
                if back:
                    yt_rest(GRAV, 2)
                if front:
                    variance(0, i)
                if tail:
                    last_sum(1)
                if front:
                    norm(0, i)
                if back:
                    yt_rest(GRAV, 3)
                if tail:
                    last_measure(0)
                    last_measure(1)
                if tail:
                    last_sum(2)
                    last_sum(3)
                if back:
                    u_rest(i, 0)
                if front:
                    add_up(1, 0)
                    add_up(1, 1)
                if front:
                    measure(1, 0)
                    measure(1, 1)
                if tail:
                    last_measure(2)
                    last_measure(3)
                if front:
                    add_up(1, 2)
                    add_up(1, 3)
                if back:
                    yt_rest(LANG, 0)
                if front:
                    measure(1, 2)
                    measure(1, 3)
                if back:
                    yt_rest(LANG, 1)
                if front:
                    variance(1, i)
                if back:
                    yt_rest(LANG, 2)
                if front:
                    norm(1, i)
                if back:
                    diagonal_sums(GRAV)
                    eng.scalar_tensor_tensor(out=tiles(half_dist[:, :]), in0=bcast_last(sq[:, 0, :], P), scalar=-1.0,
                                             in1=tiles(gram[:, GRAV, :]), op0=ALU.mult, op1=ALU.add).then_inc(half_ready, 1)
                    yt_rest(LANG, 3)
                if tail:
                    variance(3, c)
                if back:
                    u_rest(i, 1)
                if tail:
                    norm(3, i)
                if back:
                    eng.wait_ge(pe_bc, 2 * g + 1)
                    eng.wait_ge(half_ready, g + 1)
                    link(eng.tensor_tensor(dist[:, :], BC_BANK[:, :], half_dist[:, :], ALU.add))
                    eng.tensor_scalar(dist[:, :], dist[:, :], 0.0, None, ALU.max).then_inc(dist_done, 1)
                if front:
                    add_up(2, 0)
                    add_up(2, 1)
                if back:
                    diagonal_sums(LANG)
                    eng.tensor_scalar(sq_h[:, :], sq[:, 1, :], NORM_EPS * NORM_EPS / 2, -1.0, ALU.max, ALU.mult).then_inc(var_ready, 1)
                if front:
                    measure(2, 0)
                    measure(2, 1)
                if back:
                    eng.wait_ge(gram_turned, g + 1)
                    eng.tensor_tensor(diag[:, :], GRAM_BANK[:, :], gram[:, LANG, :], ALU.add).then_inc(sum_ready, 1)
                if front:
                    add_up(2, 2)
                    add_up(2, 3)
                if back:
                    link(refine(4, i, "lang", sq_h[:, :]))
                    eng.tensor_copy(r_t[:, 4, 0:1], rstd[:, 4, 0:1]).then_inc(norm_ready, 1)
                want = LINKS[0] * front + LINKS[1] * back + LINKS[2] * tail
                assert k[0] == want, (k[0], want, front, back, tail)

            iteration(0, 0, back=False, tail=False)
            iteration(1, 1, tail=False)
            iteration(2, 0)
            iteration(3, 1)
            with eng.Fori(2, NG // 2) as pair:
                iteration(2 * pair, 0)
                iteration(2 * pair + 1, 1)
            iteration(NG, 0, front=False)
            iteration(NG + 1, 1, front=False, back=False)

        @block.gpsimd
        def _(eng):
            eng.memset(zeros[:, :], 0.0).then_inc(const_set, 1)
            eng.memset(ones[:, :], 1.0).then_inc(const_set, 1)
            eng.wait_ge(const_set, 2)
            eng.affine_select(out=ident[:, :], in_=zeros[:, :], compare_op=ALU.not_equal, fill=1.0, base=0,
                              pattern=[[-1, P]], channel_multiplier=1).then_inc(const_set, 1)
            eng.affine_select(out=not_eye[:, :], in_=ones[:, :], compare_op=ALU.not_equal, fill=0.0, base=0,
                              pattern=[[-1, P]], channel_multiplier=1).then_inc(const_set, 1)
            eng.memset(w1_f[:, :], 0.0).then_inc(const_set, 1)

            def split_lo(q, b, first=False):
                eng.wait_ge(xnhi_done, q * G + b + 1)
                eng.tensor_tensor(xn_lo[:, b, :], xn_f[:, b, :], xn_hi[:, b, :], ALU.subtract).then_inc(xnlo_done, 1)

            with eng.Fori(0, NG) as q:
                for b in range(G):
                    split_lo(q, b)

            for t in range(T):
                eng.wait_ge(s_copied, t + 1)
                if t >= 1:
                    eng.wait_ge(s_mirrored, t)
                eng.affine_select(out=work[:, t, :], in_=s_sb[:, t, :], compare_op=ALU.not_equal, fill=NEG, base=t * P,
                                  pattern=[[-1, N]], channel_multiplier=1).then_inc(s_diag, 1)
                eng.wait_ge(s_turned, T - 1)
                eng.wait_ge(s_diag, 2 * t + 1)
                eng.affine_select(out=s_sb[:, t, :], in_=s_sb[:, t, :], compare_op=ALU.not_equal, fill=0.0, base=t * P,
                                  pattern=[[-1, N]], channel_multiplier=1).then_inc(s_diag, 1)
            eng.wait_ge(small_in, 96)
            eng.wait_ge(const_set, 5)
            k = [0]

            def made(ins):
                k[0] += 1
                ins.then_inc(pool_link, 1)
                eng.wait_ge(pool_link, k[0])

            made(eng.tensor_tensor(adj_off[:, :], adj_sb[:, :], not_eye[:, :], ALU.mult))
            made(eng.tensor_scalar(adj_s[:, :], adj_sb[:, :], ADJ_SCALE, 0.0, ALU.mult, ALU.add))
            made(eng.tensor_copy(adj_hi[:, :], adj_s[:, :]))
            eng.tensor_tensor(adj_lo[:, :], adj_s[:, :], adj_hi[:, :], ALU.subtract).then_inc(adj_made, 1)
            made(eng.tensor_tensor(w1_f[:, :], adj_sb[:, :], adj_sb[:, :], ALU.mult))
            made(eng.tensor_tensor(w1_f[:, :], w1_f[:, :], ident[:, :], ALU.add))
            made(eng.tensor_scalar(w1_f[:, :], w1_f[:, :], W1_SCALE, 0.0, ALU.mult, ALU.add))
            made(eng.tensor_copy(w1_hi[:, :], w1_f[:, :]))
            eng.tensor_tensor(w1_lo[:, :], w1_f[:, :], w1_hi[:, :], ALU.subtract).then_inc(adj_made, 1)
            k2 = 0
            for hi, lo in ((pg_hi, pg_lo), (pl_hi, pl_lo), (m_hi, m_lo)):
                for d in range(T):
                    eng.wait_ge(prod_hi, k2 + 1)
                    r = slice(0 if hi is m_hi else d * P, N)
                    eng.tensor_tensor(lo[:, d, r], prod_f[:, k2 % T, r], hi[:, d, r], ALU.subtract).then_inc(prod_lo, 1)
                    k2 += 1

            def x_rest(g, b, first=False):
                if not first:
                    eng.wait_ge(mix_used, mix_of(0, g - 1, b) + 1)
                eng.wait_ge(xhi_done, G * g + b + 1)
                eng.tensor_tensor(x_lo[:, b, :], x_in[:, b, :], x_hi[:, b, :], ALU.subtract).then_inc(xlo_done, 1)
                eng.tensor_scalar(xb[:, b, :], x_in[:, b, :], 1.0, bias0_col[:, :], ALU.mult, ALU.add).then_inc(xb_done, 1)

            def hold(root):
                eng.wait_ge(norm_ready, root + 1)
                eng.tensor_tensor(pool_held[:, :], ones[:, 0:1], ones[:, 0:1], ALU.mult)

            def y_rest(layer, i):
                hold(r_of(i, f"ln{layer}"))
                for b in range(G):
                    n = 2 * G * i + G * layer + b
                    eng.tensor_scalar(y_f[:, b, :], t_sb[:, b, :], rstd[:, layer, b:b + 1], nmr[:, layer, b:b + 1],
                                      ALU.mult, ALU.add).then_inc(yf_done, 1)
                    eng.wait_ge(yf_done, n + 1)
                    eng.wait_ge(yhi_done, n + 1)
                    eng.tensor_tensor(y_lo[:, b, :], y_f[:, b, :], y_hi[:, b, :], ALU.subtract).then_inc(ylo_done, 1)

            def h_rows(i, par):
                hold(r_of(i, "ln2"))
                for b in range(2, G):
                    eng.tensor_scalar(h_two[par][:, b, :], t_sb[:, b, :], rstd[:, 2, b:b + 1], nmr[:, 2, b:b + 1],
                                      ALU.mult, ALU.add).then_inc(h_rest, 1)

            def iteration(i, par, front=True, back=True, tail=True, prep=True):
                g, c = i - 1, i - 2
                if back:
                    h_rows(g, 1 - par)
                if tail:
                    eng.wait_ge(cg_ready, c + 1)
                    eng.tensor_tensor(tiles(k_g[:, :]), tiles(a_g[:, :]), bcast_last(coef[:, 0, :], P), ALU.mult).then_inc(kg_done, 1)
                if front:
                    y_rest(0, i)
                if front and prep:
                    for b in range(G):
                        x_rest(i + 1, b)
                if front:
                    y_rest(1, i)
                if back:
                    eng.wait_ge(exp_done, g + 1)
                    eng.tensor_tensor(tiles(a_g[:, :]), tiles(expo[:, :]), bcast_mid(adj_off[:, :], G), ALU.mult).then_inc(ag_done, 1)

            for b in range(G):
                x_rest(0, b, first=True)
            iteration(0, 0, back=False, tail=False)
            iteration(1, 1, tail=False)
            iteration(2, 0)
            iteration(3, 1)
            with eng.Fori(2, NG // 2 - 1) as pair:
                iteration(2 * pair, 0)
                iteration(2 * pair + 1, 1)
            iteration(NG - 2, 0)
            iteration(NG - 1, 1, prep=False)
            iteration(NG, 0, front=False)
            iteration(NG + 1, 1, front=False, back=False)


_INS = ['x', 'adj', 'L0_gnn_bias', 'L1_gnn_bias', 'L2_gnn_bias', 'L3_gnn_W_lang', 'L3_gnn_W_grav', 'L3_gnn_W_V',
        'L3_gnn_W_O', 'L3_gnn_gate_logit', 'L3_gnn_log_sigma']
_OUT = (64, 128, 512)


def kernel(**inputs):
    import numpy as np
    import concourse.bacc as bacc
    from concourse.bass_utils import run_bass_kernel_spmd as run

    nc = bacc.Bacc("TRN2", target_bir_lowering=False, num_devices=1)
    arrays, args = {}, []
    for name in _INS:
        a = np.asarray(inputs[name])
        if a.ndim == 0:
            a = a.reshape(1, 1)
        a = np.ascontiguousarray(a)
        arrays[f"in_{name}"] = a
        args.append(nc.dram_tensor(f"in_{name}", a.shape, mybir.dt.from_np(a.dtype), kind="ExternalInput").ap())
    args.append(nc.dram_tensor("out_0", _OUT, F32, kind="ExternalOutput").ap())
    gnn_kernel(nc, *args)
    r = run(nc, [arrays], core_ids=[0])
    return r.results[0]["out_0"]
```

```python
import concourse.bass as bass
from concourse import mybir
from contextlib import ExitStack
import math

F32 = mybir.dt.float32
F16 = mybir.dt.float16
ALU = mybir.AluOpType
ACT = mybir.ActivationFunctionType
AX = mybir.AxisListType


def gnn_kernel(nc, x, adj, bias0, bias1, bias2, w_lang, w_grav, w_v, w_o, gate_logit, log_sigma, out):
    NB, L, N = x.shape
    P = 128
    assert L == P
    T = N // P
    G = 4
    NG = NB // G
    K_KEEP = max(int(N * 0.3), 1)
    TOP_ROUNDS = (K_KEEP - 1) // 8
    TOP_REST = K_KEEP - 8 * TOP_ROUNDS
    LN_EPS = 1e-05
    NORM_EPS = 1e-08
    NEG = -(2.0 ** 100)
    XN_SCALE = 2.0 ** 8
    ADJ_SCALE = 2.0 ** 10
    W1_SCALE = 2.0 ** 8
    XW_SCALE = 2.0 ** 6
    AN_SCALE = 2.0 ** 10
    P_SCALE = 2.0 ** 6
    M_SCALE = 2.0 ** 8
    K_SCALE = 2.0 ** 8

    ctx = ExitStack()
    with ctx:
        ctx.enter_context(nc.allow_non_contiguous_dma(reason="biases of one element per partition"))

        def sb(name, shape, dt):
            return ctx.enter_context(nc.sbuf_tensor(name, shape, dt))

        def sem(name):
            return ctx.enter_context(nc.semaphore(name))

        bank = [ctx.enter_context(nc.psum_tensor(f"bank{i}", [P, N], F32)) for i in range(8)]

        arena = sb("arena", [P, NG * 2 * G * N], F16)
        xn = arena[:, :].rearrange("p (q s b n) -> p q s b n", q=NG, s=2, b=G)
        taken = [0]

        def part_of_arena(shape, dt):
            size = math.prod(shape[1:]) * (2 if dt == F32 else 1)
            ap = arena[:, taken[0]:taken[0] + size]
            taken[0] += size
            assert taken[0] <= NG * 2 * G * N
            if dt == F32:
                ap = ap.bitcast(F32)
            if len(shape) == 2:
                return ap
            names = "abc"[:len(shape) - 1]
            sizes = dict(zip(names, shape[1:]))
            return ap.rearrange(f"p ({' '.join(names)}) -> p {' '.join(names)}", **sizes)

        def xn_part(q, which, b):
            if isinstance(q, int):
                return xn[:, q, which, b, :]
            return xn[:, bass.ds(q, 1), which, b, :].rearrange("p a n -> p (a n)")

        HI, LO = 0, 1
        ident = sb("ident", [P, P], F32)
        ones = sb("ones", [P, P], F32)
        zeros = sb("zeros", [P, P], F32)
        not_eye = sb("not_eye", [P, P], F32)
        adj_sb = sb("adj_sb", [P, P], F32)
        adj_off = sb("adj_off", [P, P], F32)
        adj_s = sb("adj_s", [P, P], F32)
        adj_hi = sb("adj_hi", [P, P], F16)
        adj_lo = sb("adj_lo", [P, P], F16)
        w1_f = sb("w1_f", [P, P], F32)
        w1_hi = sb("w1_hi", [P, P], F16)
        w1_lo = sb("w1_lo", [P, P], F16)
        bias0_col = sb("bias0_col", [P, 1], F32)
        bias1_row = sb("bias1_row", [P, N], F32)
        bias2_row = sb("bias2_row", [P, N], F32)
        gate = sb("gate", [P, 8], F32)
        an_hi = part_of_arena([P, T, N], F16)
        an_lo = part_of_arena([P, T, N], F16)
        pg_hi = part_of_arena([P, T, N], F16)
        pg_lo = part_of_arena([P, T, N], F16)
        pl_hi = part_of_arena([P, T, N], F16)
        pl_lo = part_of_arena([P, T, N], F16)
        m_hi = part_of_arena([P, T, N], F16)
        m_lo = part_of_arena([P, T, N], F16)

        x_in = part_of_arena([P, G, N], F32)
        xb = part_of_arena([P, G, N], F32)
        x_hi = part_of_arena([P, G, N], F16)
        x_lo = part_of_arena([P, G, N], F16)
        xw_hi = sb("xw_hi", [P, 2, N], F16)
        xw_lo = sb("xw_lo", [P, 2, N], F16)
        t_sb = sb("t_sb", [P, G, N], F32)
        y_f = sb("y_f", [P, G, N], F32)
        y_hi = part_of_arena([P, G, N], F16)
        y_lo = part_of_arena([P, G, N], F16)
        h_two = [part_of_arena([P, G, N], F32), sb("h_sb1", [P, G, N], F32)]
        ht_hi = part_of_arena([P, T, N], F16)
        ht_lo = part_of_arena([P, T, N], F16)
        yt_hi = part_of_arena([P, 2, T, N], F16)
        yt_lo = part_of_arena([P, 2, T, N], F16)
        u_hi = part_of_arena([P, G, N], F16)
        u_lo = part_of_arena([P, G, N], F16)
        t3 = sb("t3", [P, G, N], F32)
        o_sb = sb("o_sb", [P, G, N], F32)
        gram = part_of_arena([P, 2, N], F32)
        diag = part_of_arena([P, N], F32)
        half_dist = part_of_arena([P, N], F32)
        dist = part_of_arena([P, N], F32)
        expo = part_of_arena([P, N], F32)
        a_g = part_of_arena([P, N], F32)
        a_l = part_of_arena([P, N], F32)
        k_l = part_of_arena([P, N], F32)
        deg_r = sb("deg_r", [P, G], F32)
        k_g = part_of_arena([P, N], F32)
        k_sb = part_of_arena([P, N], F32)
        kt_hi = part_of_arena([P, N], F16)
        kt_lo = part_of_arena([P, N], F16)
        stats = sb("stats", [P, 4, G, 6], F32)
        mv = sb("mv", [P, 4, G, 2], F32)
        half_var = sb("half_var", [P, 4, G], F32)
        ln_v = sb("ln_v", [P, 5, G], F32)
        r0 = sb("r0", [P, 5, G], F32)
        r_t = sb("r_t", [P, 5, G], F32)
        rstd = sb("rstd", [P, 5, G], F32)
        nmr = sb("nmr", [P, 4, G], F32)
        sq = sb("sq", [P, 2, G], F32)
        sq_h = sb("sq_h", [P, G], F32)
        deg = sb("deg", [P, 2, G], F32)
        deg_c = sb("deg_c", [P, 2, G], F32)
        inv_deg = sb("inv_deg", [P, 2, G], F32)
        coef = sb("coef", [P, 2, G], F32)

        xa = [h_two[1], o_sb, t3]
        sqr = t_sb
        xn_f = y_f
        ss = sb("ss", [P, G * T], F32)
        ssm = sb("ssm", [P, G * T], F32)
        rs = sb("rs", [P, 6, G * T], F32)
        s_sb = h_two[1]
        work = t3
        a_sb = o_sb
        w_stage = [y_f, t_sb, xb, x_in]
        wot = yt_hi[:, :, :, :].rearrange("p a t n -> p (a t n)").bitcast(F32).rearrange(
            "p (t n) -> p t n", t=T)
        prod_f = yt_lo[:, :, :, :].rearrange("p a t n -> p (a t n)").bitcast(F32).rearrange(
            "p (t n) -> p t n", t=T)
        an_f = prod_f
        top8 = sb("top8", [P, T, 8], F32)
        held = sb("held", [P, 3], F32)
        pool_held = sb("pool_held", [P, 1], F32)
        dcol = sb("dcol", [P, 8, T], F32)

        const_set = sem("const_set")
        small_in = sem("small_in")
        x_first = sem("x_first")
        xa_in = [sem("xa_in0"), sem("xa_in1"), sem("xa_in2")]
        squared = sem("squared")
        x_turned = sem("x_turned")
        ss_done = sem("ss_done")
        rs_link = sem("rs_link")
        rs_sqrt = sem("rs_sqrt")
        rb_done = sem("rb_done")
        xn_done = sem("xn_done")
        xnhi_done = sem("xnhi_done")
        xnlo_done = sem("xnlo_done")
        sim_done = sem("sim_done")
        row_done = sem("row_done")
        w_in = sem("w_in")
        wvo_in = sem("wvo_in")
        s_copied = sem("s_copied")
        s_turned = sem("s_turned")
        s_mirrored = sem("s_mirrored")
        s_diag = sem("s_diag")
        top = sem("top")
        adj_made = sem("adj_made")
        a_done = sem("a_done")
        dg_done = sem("dg_done")
        dg_sqrt = sem("dg_sqrt")
        dg_link = sem("dg_link")
        db_done = sem("db_done")
        anf_done = sem("anf_done")
        anhi_done = sem("anhi_done")
        an_done = sem("an_done")
        an_done_pool = sem("an_done_pool")
        wot_turned = sem("wot_turned")
        wot_done = sem("wot_done")
        prod_done = sem("prod_done")
        prod_f_done = sem("prod_f_done")
        prod_hi = sem("prod_hi")
        prod_lo = sem("prod_lo")
        gate_exp = sem("gate_exp")
        gate_done = sem("gate_done")
        x3_in = sem("x3_in")
        xhi_done = sem("xhi_done")
        xlo_done = sem("xlo_done")
        xb_done = sem("xb_done")
        pe_xw = sem("pe_xw")
        xwhi_done = sem("xwhi_done")
        xwlo_done = sem("xwlo_done")
        pe_mix = sem("pe_mix")
        mix_used = sem("mix_used")
        stat_done = sem("stat_done")
        dve_link = sem("dve_link")
        act_link = sem("act_link")
        var_ready = sem("var_ready")
        r0_ready = sem("r0_ready")
        norm_ready = sem("norm_ready")
        yhi_done = sem("yhi_done")
        yf_done = sem("yf_done")
        ylo_done = sem("ylo_done")
        h_done = sem("h_done")
        h_rest = sem("h_rest")
        pe_tr = sem("pe_tr")
        trhi_done = sem("trhi_done")
        tr_used = sem("tr_used")
        pe_wide = sem("pe_wide")
        widehi_done = sem("widehi_done")
        wide_used = sem("wide_used")
        pe_gram = sem("pe_gram")
        gram_done = sem("gram_done")
        gram_turned = sem("gram_turned")
        sum_ready = sem("sum_ready")
        al_scaled = sem("al_scaled")
        half_ready = sem("half_ready")
        pe_bc = sem("pe_bc")
        dist_done = sem("dist_done")
        exp_done = sem("exp_done")
        ag_done = sem("ag_done")
        cg_ready = sem("cg_ready")
        kg_done = sem("kg_done")
        kl_done = sem("kl_done")
        relu_done = sem("relu_done")
        al_ready = sem("al_ready")
        k_done = sem("k_done")
        st3_done = sem("st3_done")
        o_done = sem("o_done")
        out_sent = sem("out_sent")
        pool_link = sem("pool_link")

        XA = len(xa)
        assert NG % XA == 1
        DEG_BANK = bank[1:5]
        RS_LINKS, DG_LINKS = 6, 10

        S_BANK = bank[0:4]
        XT_BANK = [bank[4], bank[7]]
        RB_BANK = [bank[5], bank[6]]
        XW_BANK = [bank[0], bank[6]]
        MIX_BANK = [bank[1], bank[2]]
        WIDE_BANK = [bank[3], bank[4]]
        GRAM_BANK = bank[6]
        BC_BANK = bank[7]

        GRAV, LANG = 0, 1
        def stages_before(i):
            if isinstance(i, int):
                return min(i, NG), max(i - 1, 0), max(i - 2, 0)
            return i, i - 1, i - 2

        def roles(i):
            return i < NG, 1 <= i <= NG, i >= 2

        def count_of(order, i, what):
            per = [sum(role == n for _, role in order) for n in range(3)]
            before = sum(n * m for n, m in zip(per, stages_before(i))) if isinstance(i, int) else (
                sum(per) * i - (per[1] + 2 * per[2]))
            here = roles(i) if isinstance(i, int) else (True, True, True)
            return before + [name for name, role in order if here[role]].index(what)

        FRONT, BACK, TAIL = 0, 1, 2
        R_ORDER = [("ln0", FRONT), ("ln1", FRONT), ("ln3", TAIL), ("lang", BACK), ("ln2", FRONT)]
        r_of = lambda i, what: count_of(R_ORDER, i, what)
        WIDE_ORDER = [("U3", TAIL), ("G0", BACK), ("G1", BACK), ("G2", BACK), ("G3", BACK), ("U0", BACK),
                      ("L0", BACK), ("L1", BACK), ("L2", BACK), ("L3", BACK), ("U1", BACK), ("U2", BACK)]
        YT = ("G", "L")
        wide_of = lambda i, what: count_of(WIDE_ORDER, i, what)
        wide_at = [w for w, _ in WIDE_ORDER].index
        WIDE = lambda what: WIDE_BANK[wide_at(what) % 2]
        MIX_ORDER = ([(f"A{b}", FRONT) for b in range(G)] + [(f"K{b}", TAIL) for b in range(G)]
                     + [(f"B{b}", FRONT) for b in range(G)] + [(f"C{b}", FRONT) for b in range(G)])
        mix_at = [w for w, _ in MIX_ORDER].index
        MIX = lambda what: MIX_BANK[mix_at(what) % 2]
        mix_of = lambda layer, i, b: count_of(MIX_ORDER, i, f"{'ABC'[layer]}{b}")
        ku_of = lambda i, b: count_of(MIX_ORDER, i, f"K{b}")

        def bank_free(order, i, what):
            return count_of(order, i, what) - 1

        LINKS = (10, 13, 13)

        def links_before(i):
            if isinstance(i, int):
                return sum(n * m for n, m in zip(LINKS, stages_before(i)))
            return sum(LINKS) * i - (LINKS[1] + 2 * LINKS[2])

        TR_ORDER = [("H0", BACK), ("H1", BACK), ("H2", BACK), ("H3", BACK), ("K", TAIL)]
        TR_BANK = {"H0": bank[5], "H1": bank[7], "H2": bank[5], "H3": bank[7], "K": bank[5]}
        TURNS = ((), (0, 1), (2, 3), ())
        tr_of = lambda i, what: count_of(TR_ORDER, i, what)

        def bcast_mid(ap, n):
            return ap.rearrange("p (a m) -> p a m", a=1).to_broadcast([P, n, ap.shape[1]])

        def bcast_last(ap, m):
            return ap.rearrange("p (n a) -> p n a", a=1).to_broadcast([P, ap.shape[1], m])

        def tiles(ap):
            return ap.rearrange("p (t m) -> p t m", t=T)

        block = ctx.enter_context(nc.Block())

        @block.sync
        def _(eng):
            def load_xa(q, u):
                eng.dma_start(xa[u][:, :, :],
                              x[bass.ds(q * G, G), :, :].rearrange("b p n -> p b n")).then_inc(xa_in[u], 16)

            eng.dma_start(xa[0][:, 0, :], x[0, :, :]).then_inc(x_first, 16)
            eng.dma_start(xa[0][:, 1:G, :], x[1:G, :, :].rearrange("b p n -> p b n")).then_inc(xa_in[0], 16)
            for u in range(1, XA):
                load_xa(u, u)
            eng.dma_start(adj_sb[:, :], adj).then_inc(small_in, 16)
            eng.dma_start(bias0_col[:, :], bias0.rearrange("(p a) -> p a", a=1)).then_inc(small_in, 16)
            eng.dma_start(bias1_row[:, :],
                          bias1.rearrange("(a n) -> a n", a=1).to_broadcast([P, N])).then_inc(small_in, 16)
            eng.dma_start(bias2_row[:, :],
                          bias2.rearrange("(a n) -> a n", a=1).to_broadcast([P, N])).then_inc(small_in, 16)
            eng.dma_start(gate[:, 0:1], gate_logit.to_broadcast([P, 1])).then_inc(small_in, 16)
            eng.dma_start(gate[:, 1:2], log_sigma.to_broadcast([P, 1])).then_inc(small_in, 16)

            def next_xa(q, u):
                eng.wait_ge(xn_done, (q - XA + 1) * G)
                eng.wait_ge(x_turned, (q - XA + 1) * G)
                load_xa(q, u)

            with eng.Fori(1, NG // XA) as turn:
                for u in range(XA):
                    next_xa(XA * turn + u, u)
            next_xa(NG - 1, (NG - 1) % XA)

            def load_w(stage, w, loaded):
                eng.dma_start(w_stage[stage][:, :, :],
                              w.rearrange("(t p) n -> p t n", p=P)).then_inc(loaded, 16)

            eng.wait_ge(xnlo_done, NB)
            eng.wait_ge(xnhi_done, NB)
            eng.wait_ge(ss_done, NB)
            load_w(0, w_lang, w_in)
            load_w(1, w_grav, w_in)
            eng.wait_ge(row_done, T - 2)
            load_w(2, w_v, wvo_in)
            load_w(3, w_o, wvo_in)

            def load_x(g):
                eng.dma_start(x_in[:, :, :],
                              x[bass.ds(g * G, G), :, :].rearrange("b p n -> p b n")).then_inc(x3_in, 16)

            eng.wait_ge(wot_turned, T)
            load_x(0)

            def store(g):
                eng.wait_ge(o_done, G * (g + 1))
                eng.dma_start(out[bass.ds(G * g, G), :, :].rearrange("b p n -> p b n"),
                              o_sb[:, :, :]).then_inc(out_sent, 16)

            def next_x(g):
                eng.wait_ge(xhi_done, G * g)
                eng.wait_ge(xlo_done, G * g)
                eng.wait_ge(xb_done, G * g)
                load_x(g)

            next_x(1)
            next_x(2)
            with eng.Fori(2, NG - 1) as i:
                next_x(i + 1)
                store(i - 2)
            for g in range(NG - 3, NG - 1):
                store(g)
            for b in range(0, G, 2):
                eng.wait_ge(o_done, G * (NG - 1) + b + 2)
                eng.dma_start(out[G * (NG - 1) + b:G * (NG - 1) + b + 2, :, :].rearrange("b p n -> p b n"),
                              o_sb[:, b:b + 2, :]).then_inc(out_sent, 16)
            eng.wait_ge(out_sent, 16 * (NG + 1))

        @block.tensor
        def _(eng):
            def product3(dst, a_hi, a_lo, b_hi, b_lo, start, stop):
                eng.matmul(dst, a_hi, b_hi, start=start, stop=False)
                eng.matmul(dst, a_hi, b_lo, start=False, stop=False)
                return eng.matmul(dst, a_lo, b_hi, start=False, stop=stop)

            def turn_x(q, u, b, loads=0, first=False):
                if first and b == 0:
                    eng.wait_ge(x_first, 16)
                if b == (1 if first else 0):
                    eng.wait_ge(xa_in[u], 16 * loads)
                if not (first and b < 2):
                    eng.wait_ge(squared, q * G + b - 1)
                for t in range(T):
                    c = slice(t * P, (t + 1) * P)
                    last = eng.transpose(XT_BANK[b % 2][:, c], xa[u][:, b, c], ident[:, :])
                last.then_inc(x_turned, 1)

            def spread_norms(q, u, b, first=False):
                if b == 0:
                    eng.wait_ge(rs_link, (q + 1) * RS_LINKS)
                if not first:
                    eng.wait_ge(xn_done, q * G + b - 1)
                for t in range(T):
                    c = b * T + t
                    last = eng.transpose(RB_BANK[b % 2][:, t * P:(t + 1) * P],
                                         rs[:, 3 + u, c:c + 1].to_broadcast([P, P]), ident[:, :])
                last.then_inc(rb_done, 1)

            def add_similarity(t, q, b, first=False, end=False):
                c, r = slice(t * P, (t + 1) * P), slice(t * P, N)
                hi, lo = xn_part(q, HI, b), xn_part(q, LO, b)
                return product3(S_BANK[t][:, r], hi[:, c], lo[:, c], hi[:, r], lo[:, r], start=first, stop=end)

            def similarity(q, b, first=False, end=False):
                eng.wait_ge(xnlo_done, q * G + b + 1)
                eng.wait_ge(xnhi_done, q * G + b + 1)
                add_similarity(0, q, b, first, end)
                add_similarity(T - 1, q, b, first, end).then_inc(sim_done, 1)

            def sim_group(q, u, loads=0, first=False, end=False):
                for b in range(G):
                    if b < 2 and not end:
                        turn_x(q + 1, (u + 1) % XA, 2 * b, loads)
                        turn_x(q + 1, (u + 1) % XA, 2 * b + 1, loads)
                    spread_norms(q, u, b, first=first and b < 2)
                    if b < G - 1 and not first:
                        similarity(q - 1, b + 1)
                similarity(q, 0, first=first)
                if end:
                    for b in range(1, G):
                        similarity(q, b, end=b == G - 1)

            eng.wait_ge(const_set, 5)
            for b in range(G):
                turn_x(0, 0, b, loads=1, first=True)
            sim_group(0, 0, loads=1, first=True)
            with eng.Fori(0, NG // XA - 1) as turn:
                for u in range(1, XA + 1):
                    sim_group(XA * turn + u, u % XA, loads=turn + (u + 1) // XA + 1)
            for q in range(NG - XA, NG):
                sim_group(q, q % XA, loads=(q + 1) // XA + 1, end=q == NG - 1)

            for i in range(1, T):
                if i < T - 1:
                    for b in range(G):
                        add_similarity(i, 0, b, first=b == 0)
                    with eng.Fori(0, NG // 2 - 1) as pair:
                        for q in (2 * pair + 1, 2 * pair + 2):
                            for b in range(G):
                                add_similarity(i, q, b)
                    for b in range(G):
                        last = add_similarity(i, NG - 1, b, end=b == G - 1)
                    last.then_inc(row_done, 1)
                for j in range(i):
                    eng.wait_ge(s_copied, j + 1)
                    last = eng.transpose(bank[4 + i][:, j * P:(j + 1) * P], s_sb[:, j, i * P:(i + 1) * P], ident[:, :])
                last.then_inc(s_turned, 1)
            eng.wait_ge(s_copied, T)

            def turn_wo():
                eng.wait_ge(wvo_in, 32)
                for f in range(T):
                    if f >= 2:
                        eng.wait_ge(wot_done, f - 1)
                    for e in range(T):
                        last = eng.transpose(bank[f % 2][:, e * P:(e + 1) * P],
                                             w_stage[3][:, f, e * P:(e + 1) * P], ident[:, :])
                    last.then_inc(wot_turned, 1)
                eng.wait_ge(wot_done, T)

            eng.wait_ge(w_in, 32)
            k = 0
            for lhs, rhs in ((w_stage[1], w_stage[1]), (w_stage[0], w_stage[0]), (w_stage[2], wot)):
                if rhs is wot:
                    turn_wo()
                for d in range(T):
                    if k >= 2:
                        eng.wait_ge(prod_hi, k - 1)
                    r = slice(d * P if lhs is rhs else 0, N)
                    for e in range(T):
                        last = eng.matmul(bank[2 + k % 2][:, r], lhs[:, e, d * P:(d + 1) * P], rhs[:, e, r],
                                          start=(e == 0), stop=(e == T - 1))
                    last.then_inc(prod_done, 1)
                    k += 1

            def xw(g, b, first=False):
                n = G * g + b
                eng.wait_ge(xhi_done, n + 1)
                eng.wait_ge(xlo_done, n + 1)
                if b >= 2:
                    eng.wait_ge(xwlo_done, n - 1)
                if b == 1 and not first:
                    eng.wait_ge(sum_ready, g - 1)
                for t in range(T):
                    c = slice(t * P, (t + 1) * P)
                    last = product3(XW_BANK[b % 2][:, c], x_hi[:, b, c], x_lo[:, b, c], adj_hi[:, :], adj_lo[:, :],
                                    start=True, stop=True)
                last.then_inc(pe_xw, 1)

            eng.wait_ge(adj_made, 2)
            eng.wait_ge(s_mirrored, T - 1)
            xw(0, 0)
            xw(0, 1, first=True)
            eng.wait_ge(prod_hi, 3 * T)
            for s in range(T):
                eng.wait_ge(a_done, s + 1)
                for t in range(T):
                    last = eng.matmul(DEG_BANK[t][:, 0:1], a_sb[:, s, t * P:(t + 1) * P], ones[:, 0:1],
                                      start=(s == 0), stop=(s == T - 1))
            last.then_inc(dg_done, 1)
            eng.wait_ge(dg_link, DG_LINKS)
            eng.wait_ge(s_mirrored, T - 1)
            for t in range(T):
                last = eng.transpose(bank[5][:, t * P:(t + 1) * P], dcol[:, 4, t:t + 1].to_broadcast([P, P]),
                                     ident[:, :])
            last.then_inc(db_done, 1)

            def mix_bank(i, what):
                free = bank_free(MIX_ORDER, i, what)
                if not (isinstance(free, int) and free <= 0):
                    eng.wait_ge(mix_used, free)

            def spread(i, b):
                eng.wait_ge(xwlo_done, G * i + b + 1)
                mix_bank(i, f"A{b}")
                for t in range(T):
                    c = slice(t * P, (t + 1) * P)
                    last = product3(MIX(f"A{b}")[:, :], xw_hi[:, b % 2, c], xw_lo[:, b % 2, c],
                                    an_hi[:, t, :], an_lo[:, t, :], start=(t == 0), stop=(t == T - 1))
                last.then_inc(pe_mix, 1)

            def mix(layer, i, b):
                eng.wait_ge(yhi_done, 2 * G * i + G * (layer - 1) + b + 1)
                eng.wait_ge(ylo_done, 2 * G * i + G * (layer - 1) + b + 1)
                what = f"{'ABC'[layer]}{b}"
                mix_bank(i, what)
                product3(MIX(what)[:, :], w1_hi[:, :], w1_lo[:, :], y_hi[:, b, :], y_lo[:, b, :],
                         start=True, stop=True).then_inc(pe_mix, 1)

            def turn_h(i, g, par, j):
                if j == 0:
                    eng.wait_ge(h_done, 2 * (g + 1))
                    eng.wait_ge(h_rest, 2 * (g + 1))
                    if not (isinstance(i, int) and i == 1):
                        eng.wait_ge(tr_used, tr_of(i, "H0"))
                if j == 1 and not (isinstance(i, int) and i == 1):
                    eng.wait_ge(al_scaled, g)
                if j >= 2:
                    eng.wait_ge(tr_used, tr_of(i, f"H{j - 2}") + 1)
                for b in range(G):
                    last = eng.transpose(TR_BANK[f"H{j}"][:, b * P:(b + 1) * P], h_two[par][:, b, j * P:(j + 1) * P],
                                         ident[:, :])
                last.then_inc(pe_tr, 1)

            def wide_bank(i, what):
                free = bank_free(WIDE_ORDER, i, what)
                if not (isinstance(free, int) and free <= 0):
                    eng.wait_ge(wide_used, free)

            def yt(i, which, j):
                if which == GRAV and j == 0:
                    eng.wait_ge(tr_used, tr_of(i, "H3") + 1)
                what = f"{YT[which]}{j}"
                wide_bank(i, what)
                p_hi, p_lo = ((pg_hi, pg_lo), (pl_hi, pl_lo))[which]
                c = slice(j * P, (j + 1) * P)
                for d in range(j + 1):
                    last = product3(WIDE(what)[:, :], p_hi[:, d, c], p_lo[:, d, c], ht_hi[:, d, :], ht_lo[:, d, :],
                                    start=(d == 0), stop=(d == j))
                last.then_inc(pe_wide, 1)

            def grams(i, which, g, first=False):
                eng.wait_ge(wide_used, wide_of(i, f"{YT[which]}{T - 1}") + 1)
                if not first:
                    eng.wait_ge(gram_done, 2 * g + which)
                for b in range(G):
                    c = slice(b * P, (b + 1) * P)
                    for j in range(T):
                        last = product3(GRAM_BANK[:, c], yt_hi[:, which, j, c], yt_lo[:, which, j, c],
                                        ht_hi[:, j, c], ht_lo[:, j, c], start=(j == 0), stop=(j == T - 1))
                last.then_inc(pe_gram, 1)

            def u_product(i, b):
                wide_bank(i, f"U{b}")
                c = slice(b * P, (b + 1) * P)
                for d in range(T):
                    last = product3(WIDE(f"U{b}")[:, :], ht_hi[:, d, c], ht_lo[:, d, c], m_hi[:, d, :], m_lo[:, d, :],
                                    start=(d == 0), stop=(d == T - 1))
                last.then_inc(pe_wide, 1)

            def turn_half_distances(i, g):
                eng.wait_ge(half_ready, g + 1)
                eng.wait_ge(tr_used, tr_of(i, "H3") + 1)
                for b in range(G):
                    c = slice(b * P, (b + 1) * P)
                    last = eng.transpose(BC_BANK[:, c], half_dist[:, c], ident[:, :])
                last.then_inc(pe_bc, 1)

            def turn_gram(g):
                eng.wait_ge(gram_done, 2 * g + LANG + 1)
                for b in range(G):
                    c = slice(b * P, (b + 1) * P)
                    last = eng.transpose(GRAM_BANK[:, c], gram[:, LANG, c], ident[:, :])
                last.then_inc(gram_turned, 1)

            def spread_norm_column(g):
                eng.wait_ge(norm_ready, r_of(g + 1, "lang") + 1)
                eng.wait_ge(dist_done, g + 1)
                for b in range(G):
                    last = eng.transpose(BC_BANK[:, b * P:(b + 1) * P], rstd[:, 4, b:b + 1].to_broadcast([P, P]),
                                         ident[:, :])
                last.then_inc(pe_bc, 1)

            def turn_k(i, g):
                eng.wait_ge(k_done, g + 1)
                if not (isinstance(i, int) and i == NG + 1):
                    eng.wait_ge(tr_used, tr_of(i, "H2") + 1)
                for b in range(G):
                    c = slice(b * P, (b + 1) * P)
                    last = eng.transpose(TR_BANK["K"][:, c], k_sb[:, c], ident[:, :])
                last.then_inc(pe_tr, 1)

            def ku(i, b):
                if b == 0:
                    eng.wait_ge(tr_used, tr_of(i, "K") + 1)
                eng.wait_ge(wide_used, wide_of(i, "U3") + 1)
                mix_bank(i, f"K{b}")
                c = slice(b * P, (b + 1) * P)
                product3(MIX(f"K{b}")[:, :], kt_hi[:, c], kt_lo[:, c], u_hi[:, b, :], u_lo[:, b, :],
                         start=True, stop=True).then_inc(pe_mix, 1)

            def iteration(i, par, front=True, back=True, tail=True):
                g, c = i - 1, i - 2
                first_back = back and not tail
                if front and back:
                    xw(i, 0)
                if tail:
                    u_product(i, 3)
                if front and back:
                    xw(i, 1, first=not tail)
                if tail:
                    spread_norm_column(c)
                for b in range(G):
                    if front:
                        spread(i, b)
                        if b + 2 < G:
                            xw(i, b + 2)
                    if back:
                        for j in TURNS[b]:
                            turn_h(i, g, 1 - par, j)
                if tail:
                    turn_k(i, c)
                if back:
                    yt(i, GRAV, 0)
                    yt(i, GRAV, 1)
                if tail:
                    ku(i, 0)
                if back:
                    yt(i, GRAV, 2)
                if tail:
                    ku(i, 1)
                if back:
                    yt(i, GRAV, 3)
                if tail:
                    ku(i, 2)
                    ku(i, 3)
                if back:
                    u_product(i, 0)
                if front:
                    mix(1, i, 0)
                    mix(1, i, 1)
                if back:
                    grams(i, GRAV, g, first=first_back)
                if front:
                    mix(1, i, 2)
                if back:
                    yt(i, LANG, 0)
                if front:
                    mix(1, i, 3)
                if back:
                    for j in range(1, T):
                        yt(i, LANG, j)
                    u_product(i, 1)
                    turn_half_distances(i, g)
                    grams(i, LANG, g)
                if front:
                    mix(2, i, 0)
                    mix(2, i, 1)
                if back:
                    u_product(i, 2)
                    turn_gram(g)
                if front:
                    mix(2, i, 2)
                    mix(2, i, 3)

            eng.wait_ge(an_done, T // 2)
            eng.wait_ge(an_done_pool, T // 2)
            eng.wait_ge(prod_lo, 3 * T)
            iteration(0, 0, back=False, tail=False)
            iteration(1, 1, tail=False)
            with eng.Fori(1, NG // 2) as pair:
                iteration(2 * pair, 0)
                iteration(2 * pair + 1, 1)
            iteration(NG, 0, front=False)
            iteration(NG + 1, 1, front=False, back=False)

        @block.scalar
        def _(eng):
            def square(q, b, first=False):
                eng.wait_ge(x_turned, q * G + b + 1)
                if not first:
                    eng.wait_ge(ss_done, (q - 1) * G + b + 1)
                eng.activation(sqr[:, b, :], XT_BANK[b % 2][:, :], ACT.Square).then_inc(squared, 1)

            def root(q):
                eng.wait_ge(rs_link, q * RS_LINKS + 1)
                eng.activation(rs[:, 0, :], ssm[:, :], ACT.Sqrt).then_inc(rs_sqrt, 1)

            def split_hi(q, b):
                eng.wait_ge(xn_done, q * G + b + 1)
                eng.activation(xn_part(q, HI, b), xn_f[:, b, :], ACT.Copy).then_inc(xnhi_done, 1)

            def norm_group(q, first=False, end=False):
                if not end:
                    square(q + 1, 0)
                    square(q + 1, 1)
                if not first:
                    split_hi(q - 1, 2)
                    split_hi(q - 1, 3)
                if not end:
                    square(q + 1, 2)
                    square(q + 1, 3)
                split_hi(q, 0)
                if not end:
                    root(q + 1)
                split_hi(q, 1)
                if end:
                    split_hi(q, 2)
                    split_hi(q, 3)

            for b in range(G):
                square(0, b, first=True)
            root(0)
            norm_group(0, first=True)
            with eng.Fori(1, NG - 1) as q:
                norm_group(q)
            norm_group(NG - 1, end=True)

            eng.wait_ge(sim_done, NB)
            for t in range(T):
                if 0 < t < T - 1:
                    eng.wait_ge(row_done, t)
                eng.activation(s_sb[:, t, t * P:N], S_BANK[t][:, t * P:N], ACT.Copy,
                               scale=1.0 / (XN_SCALE * XN_SCALE * NB)).then_inc(s_copied, 1)
                if t > 0:
                    eng.wait_ge(s_turned, t)
                    eng.activation(s_sb[:, t, 0:t * P], bank[4 + t][:, 0:t * P],
                                   ACT.Copy).then_inc(s_mirrored, 1)
            k = 0
            for dst, scale in ((pg_hi, P_SCALE), (pl_hi, P_SCALE), (m_hi, M_SCALE)):
                if dst is m_hi:
                    for f in range(T):
                        eng.wait_ge(wot_turned, f + 1)
                        eng.activation(wot[:, :, f * P:(f + 1) * P], tiles(bank[f % 2][:, :]),
                                       ACT.Copy).then_inc(wot_done, 1)
                for d in range(T):
                    eng.wait_ge(prod_done, k + 1)
                    if k >= T:
                        eng.wait_ge(prod_lo, k - T + 1)
                    diagonal = slice(d * P, (d + 1) * P)
                    src = bank[2 + k % 2]
                    if dst is m_hi:
                        eng.activation(prod_f[:, k % T, :], src[:, :], ACT.Copy,
                                       scale=scale).then_inc(prod_f_done, 1)
                        eng.activation(dst[:, d, :], src[:, :], ACT.Copy, scale=scale).then_inc(prod_hi, 1)
                    else:
                        r = slice((d + 1) * P, N)
                        if d < T - 1:
                            eng.activation(prod_f[:, k % T, r], src[:, r], ACT.Copy, scale=scale)
                            eng.activation(dst[:, d, r], src[:, r], ACT.Copy, scale=scale)
                        eng.activation(prod_f[:, k % T, diagonal], src[:, diagonal], ACT.Copy,
                                       scale=scale / 2).then_inc(prod_f_done, 1)
                        eng.activation(dst[:, d, diagonal], src[:, diagonal], ACT.Copy,
                                       scale=scale / 2).then_inc(prod_hi, 1)
                    k += 1

            def x_split(g, b, first=False):
                if b == 0:
                    eng.wait_ge(x3_in, 16 * (g + 1))
                if not first:
                    eng.wait_ge(pe_xw, G * (g - 1) + b + 1)
                eng.activation(x_hi[:, b, :], x_in[:, b, :], ACT.Copy).then_inc(xhi_done, 1)

            def xw_split(g, b, first=False):
                eng.wait_ge(pe_xw, G * g + b + 1)
                if not first:
                    eng.wait_ge(pe_mix, mix_of(0, g, b - 2) + 1 if b >= 2 else mix_of(0, g - 1, b + 2) + 1)
                eng.activation(xw_hi[:, b % 2, :], XW_BANK[b % 2][:, :], ACT.Copy,
                               scale=XW_SCALE / ADJ_SCALE).then_inc(xwhi_done, 1)

            for b in range(G):
                x_split(0, b, first=True)
            xw_split(0, 0, first=True)
            xw_split(0, 1, first=True)
            eng.wait_ge(dg_link, 2)
            eng.activation(dcol[:, 1, :], dcol[:, 0, :], ACT.Sqrt).then_inc(dg_sqrt, 1)
            eng.preload_act_table_set("natural_log_exp_and_others")
            for t in range(T):
                eng.wait_ge(anf_done, t + 1)
                eng.activation(an_hi[:, t, :], an_f[:, t, :], ACT.Copy).then_inc(anhi_done, 1)
            eng.wait_ge(small_in, 96)
            eng.activation(gate[:, 2:3], gate[:, 0:1], ACT.Exp, scale=-1.0).then_inc(gate_exp, 1)
            eng.activation(gate[:, 3:4], gate[:, 1:2], ACT.Exp, scale=-2.0).then_inc(gate_exp, 1)

            def root_of(i, what):
                row = {"ln0": 0, "ln1": 1, "ln2": 2, "ln3": 3, "lang": 4}[what]
                k = r_of(i, what)
                eng.wait_ge(var_ready, k + 1)
                src = half_var[:, row, :] if row < 4 else sq_h[:, :]
                eng.activation(ln_v[:, row, :], src, ACT.Ln, scale=-2.0).then_inc(act_link, 1)
                eng.wait_ge(act_link, k + 1)
                eng.activation(r0[:, row, :], ln_v[:, row, :], ACT.Exp, scale=-0.5).then_inc(r0_ready, 1)

            def y_row(layer, i, b):
                if b == 0:
                    eng.wait_ge(norm_ready, r_of(i, f"ln{layer}") + 1)
                eng.activation(y_hi[:, b, :], t_sb[:, b, :], ACT.Identity, bias=nmr[:, layer, b:b + 1],
                               scale=rstd[:, layer, b:b + 1]).then_inc(yhi_done, 1)

            def turned_split(dst, i, what, scale):
                eng.wait_ge(pe_tr, tr_of(i, what) + 1)
                eng.activation(dst, TR_BANK[what][:, :], ACT.Copy, scale=scale).then_inc(trhi_done, 1)

            def wide_split(dst, i, what, scale):
                eng.wait_ge(pe_wide, wide_of(i, what) + 1)
                eng.activation(dst, WIDE(what)[:, :], ACT.Copy, scale=scale).then_inc(widehi_done, 1)

            def yt_split(i, which, j):
                wide_split(yt_hi[:, which, j, :], i, f"{YT[which]}{j}", 1.0 / P_SCALE)

            def u_split(i, b):
                wide_split(u_hi[:, b, :], i, f"U{b}", 1.0 / M_SCALE)

            def h_row(i, par, g, b):
                if b == 0:
                    eng.wait_ge(norm_ready, r_of(g, "ln2") + 1)
                eng.activation(h_two[par][:, b, :], t_sb[:, b, :], ACT.Identity, bias=nmr[:, 2, b:b + 1],
                               scale=rstd[:, 2, b:b + 1]).then_inc(h_done, 1)

            def output(i, g):
                eng.wait_ge(norm_ready, r_of(i, "ln3") + 1)
                if not (isinstance(g, int) and g == 0):
                    eng.wait_ge(out_sent, 16 * g)
                for b in range(G):
                    eng.activation(o_sb[:, b, :], t3[:, b, :], ACT.Identity, bias=nmr[:, 3, b:b + 1],
                                   scale=rstd[:, 3, b:b + 1]).then_inc(o_done, 1)

            def iteration(i, par, front=True, back=True, tail=True, prep=True):
                g, c = i - 1, i - 2
                if front and back:
                    xw_split(i, 0)
                if tail:
                    u_split(i, 3)
                if front and back:
                    xw_split(i, 1)
                if back:
                    root_of(g, "ln2")
                    h_row(i, 1 - par, g, 0)
                    h_row(i, 1 - par, g, 1)
                if front:
                    xw_split(i, 2)
                    xw_split(i, 3)
                if back:
                    for j in range(T):
                        turned_split(ht_hi[:, j, :], i, f"H{j}", 1.0)
                if not (isinstance(i, int) and i < 3):
                    output(i - 1, i - 3)
                if tail:
                    turned_split(kt_hi[:, :], i, "K", K_SCALE)
                if back:
                    yt_split(i, GRAV, 0)
                    yt_split(i, GRAV, 1)
                    yt_split(i, GRAV, 2)
                if front:
                    root_of(i, "ln0")
                if back:
                    yt_split(i, GRAV, 3)
                if front:
                    for b in range(G):
                        y_row(0, i, b)
                if back:
                    u_split(i, 0)
                if front and prep:
                    for b in range(G):
                        x_split(i + 1, b)
                if back:
                    eng.wait_ge(pe_gram, 2 * g + GRAV + 1)
                    eng.activation(gram[:, GRAV, :], GRAM_BANK[:, :], ACT.Copy,
                                   scale=-2.0).then_inc(gram_done, 1)
                    yt_split(i, LANG, 0)
                    yt_split(i, LANG, 1)
                if front:
                    root_of(i, "ln1")
                if back:
                    yt_split(i, LANG, 2)
                    yt_split(i, LANG, 3)
                if front:
                    y_row(1, i, 0)
                    y_row(1, i, 1)
                    y_row(1, i, 2)
                    y_row(1, i, 3)
                if tail:
                    root_of(i, "ln3")
                if back:
                    u_split(i, 1)
                    eng.wait_ge(pe_gram, 2 * g + LANG + 1)
                    eng.activation(gram[:, LANG, :], GRAM_BANK[:, :], ACT.Copy).then_inc(gram_done, 1)
                    eng.wait_ge(dist_done, g + 1)
                    eng.activation(expo[:, :], dist[:, :], ACT.Exp, scale=gate[:, 5:6]).then_inc(exp_done, 1)
                    root_of(i, "lang")
                    u_split(i, 2)
                    eng.wait_ge(sum_ready, g + 1)
                    eng.activation(diag[:, :], diag[:, :], ACT.Relu).then_inc(relu_done, 1)

            iteration(0, 0, back=False, tail=False)
            iteration(1, 1, tail=False)
            iteration(2, 0)
            iteration(3, 1)
            with eng.Fori(2, NG // 2 - 1) as pair:
                iteration(2 * pair, 0)
                iteration(2 * pair + 1, 1)
            iteration(NG - 2, 0)
            iteration(NG - 1, 1, prep=False)
            iteration(NG, 0, front=False)
            iteration(NG + 1, 1, front=False, back=False)
            output(NG + 1, NG - 1)

        @block.vector
        def _(eng):
            def sum_squares(q, b):
                eng.wait_ge(squared, q * G + b + 1)
                if b == 0 and not (isinstance(q, int) and q == 0):
                    eng.wait_ge(rs_link, q * RS_LINKS)
                eng.tensor_reduce(ss[:, b * T:(b + 1) * T], tiles(sqr[:, b, :]), AX.X,
                                  ALU.add).then_inc(ss_done, 1)

            def norms(q, u, meanwhile=None):
                k = [0]

                def link(ins):
                    k[0] += 1
                    ins.then_inc(rs_link, 1)
                    if k[0] < RS_LINKS:
                        eng.wait_ge(rs_link, q * RS_LINKS + k[0])

                eng.wait_ge(ss_done, G * (q + 1))
                link(eng.tensor_scalar(ssm[:, :], ss[:, :], 1e-24, None, ALU.max))
                if meanwhile:
                    meanwhile()
                eng.wait_ge(rs_sqrt, q + 1)
                link(eng.reciprocal(rs[:, 1, :], rs[:, 0, :]))
                link(eng.tensor_tensor(rs[:, 2, :], rs[:, 1, :], ssm[:, :], ALU.mult))
                link(eng.tensor_tensor(rs[:, 2, :], rs[:, 2, :], rs[:, 1, :], ALU.mult))
                link(eng.tensor_scalar(rs[:, 2, :], rs[:, 2, :], -0.5 * XN_SCALE, 1.5 * XN_SCALE, ALU.mult, ALU.add))
                link(eng.tensor_tensor(rs[:, 3 + u, :], rs[:, 2, :], rs[:, 1, :], ALU.mult))
                assert k[0] == RS_LINKS

            def normalise(q, u, b, first=False):
                eng.wait_ge(rb_done, q * G + b + 1)
                if not first:
                    eng.wait_ge(xnlo_done, (q - 1) * G + b + 1)
                    eng.wait_ge(xnhi_done, (q - 1) * G + b + 1)
                eng.tensor_tensor(xn_f[:, b, :], RB_BANK[b % 2][:, :], xa[u][:, b, :],
                                  ALU.mult).then_inc(xn_done, 1)

            def norm_group(q, u, first=False, end=False):
                if not end:
                    sum_squares(q + 1, 0)
                    sum_squares(q + 1, 1)
                normalise(q, u, 0, first)
                if not end:
                    sum_squares(q + 1, 2)
                    sum_squares(q + 1, 3)
                    norms(q + 1, (u + 1) % XA, meanwhile=lambda: normalise(q, u, 1, first))
                else:
                    normalise(q, u, 1, first)
                normalise(q, u, 2, first)
                normalise(q, u, 3, first)

            for b in range(G):
                sum_squares(0, b)
            norms(0, 0)
            norm_group(0, 0, first=True)
            with eng.Fori(0, NG // XA - 1) as turn:
                for u in range(1, XA + 1):
                    norm_group(XA * turn + u, u % XA)
            for q in range(NG - XA, NG):
                norm_group(q, q % XA, end=q == NG - 1)

            def find(t):
                eng.max(top8[:, t, :], work[:, t, :]).then_inc(top, 1)

            def mark(t):
                eng.match_replace(out=work[:, t, :], in_to_replace=top8[:, t, :], in_values=work[:, t, :],
                                  imm_value=NEG).then_inc(top, 1)

            def step(do, some, before):
                for k, t in enumerate(some):
                    eng.wait_ge(top, before - len(some) + k + 1)
                    eng.memset(held[:, 1 + k:2 + k], 0.0)
                    do(t)

            def search(some, base):
                n = len(some)
                for t in some:
                    eng.wait_ge(s_diag, 2 * t + 1)
                    find(t)
                step(mark, some, base + n)
                with eng.Fori(1, TOP_ROUNDS) as r:
                    step(find, some, base + 2 * n * r)
                    step(mark, some, base + 2 * n * r + n)
                step(find, some, base + 2 * n * TOP_ROUNDS)
                eng.wait_ge(top, base + 2 * n * TOP_ROUNDS + n)
                for t in some:
                    eng.memset(top8[:, t, TOP_REST:8], NEG).then_inc(top, 1)
                done = base + 2 * n * TOP_ROUNDS + 2 * n
                eng.wait_ge(top, done)
                for k, t in enumerate(some):
                    mark(t)
                for k, t in enumerate(some):
                    eng.wait_ge(top, done + k + 1)
                    eng.wait_ge(s_diag, 2 * t + 2)
                    keep(t)
                return done + n

            def keep(t):
                eng.scalar_tensor_tensor(out=a_sb[:, t, :], in0=work[:, t, :], scalar=NEG, in1=s_sb[:, t, :],
                                         op0=ALU.is_equal, op1=ALU.mult).then_inc(a_done, 1)

            searched = search([0], 0)
            searched = search([1], searched)
            search([2, 3], searched)
            for b in range(2):
                eng.wait_ge(xwhi_done, b + 1)
                eng.scalar_tensor_tensor(out=xw_lo[:, b, :], in0=XW_BANK[b][:, :], scalar=XW_SCALE / ADJ_SCALE,
                                         in1=xw_hi[:, b, :], op0=ALU.mult, op1=ALU.subtract).then_inc(xwlo_done, 1)
            k = [0]

            def dg(ins):
                k[0] += 1
                ins.then_inc(dg_link, 1)
                eng.wait_ge(dg_link, k[0])

            eng.wait_ge(dg_done, 1)
            for t in range(T):
                ins = eng.tensor_copy(dcol[:, 7, t:t + 1], DEG_BANK[t][:, 0:1])
            dg(ins)
            dg(eng.tensor_scalar(dcol[:, 0, :], dcol[:, 7, :], 2.0 ** -110, None, ALU.max))
            dg(eng.tensor_scalar(dcol[:, 6, :], dcol[:, 7, :], 0.0, None, ALU.is_gt))
            eng.wait_ge(dg_sqrt, 1)
            dg(eng.reciprocal(dcol[:, 2, :], dcol[:, 1, :]))
            dg(eng.tensor_tensor(dcol[:, 3, :], dcol[:, 2, :], dcol[:, 0, :], ALU.mult))
            dg(eng.tensor_tensor(dcol[:, 3, :], dcol[:, 3, :], dcol[:, 2, :], ALU.mult))
            dg(eng.tensor_scalar(dcol[:, 3, :], dcol[:, 3, :], -0.5, 1.5, ALU.mult, ALU.add))
            dg(eng.tensor_tensor(dcol[:, 3, :], dcol[:, 3, :], dcol[:, 2, :], ALU.mult))
            dg(eng.tensor_tensor(dcol[:, 4, :], dcol[:, 3, :], dcol[:, 6, :], ALU.mult))
            dg(eng.tensor_scalar(dcol[:, 5, :], dcol[:, 4, :], AN_SCALE, None, ALU.mult))
            assert k[0] == DG_LINKS
            eng.wait_ge(db_done, 1)
            eng.wait_ge(prod_lo, 3 * T)
            for t in range(T):
                eng.scalar_tensor_tensor(out=an_f[:, t, :], in0=a_sb[:, t, :], scalar=dcol[:, 5, t:t + 1],
                                         in1=bank[5][:, :], op0=ALU.mult, op1=ALU.mult).then_inc(anf_done, 1)
            for t in range(T // 2, T):
                eng.wait_ge(anhi_done, t + 1)
                eng.tensor_tensor(an_lo[:, t, :], an_f[:, t, :], an_hi[:, t, :],
                                  ALU.subtract).then_inc(an_done, 1)

            eng.wait_ge(gate_exp, 2)
            eng.tensor_scalar(gate[:, 4:5], gate[:, 2:3], 1.0, None, ALU.add).then_inc(gate_done, 1)
            eng.tensor_scalar(gate[:, 5:6], gate[:, 3:4], -0.5, None, ALU.mult).then_inc(gate_done, 1)
            eng.wait_ge(gate_done, 2)
            eng.reciprocal(gate[:, 6:7], gate[:, 4:5]).then_inc(gate_done, 1)
            eng.wait_ge(gate_done, 3)
            eng.tensor_scalar(gate[:, 7:8], gate[:, 6:7], -1.0, 1.0, ALU.mult, ALU.add).then_inc(gate_done, 1)
            eng.wait_ge(gate_done, 4)

            def iteration(i, par, front=True, back=True, tail=True):
                g, c = i - 1, i - 2
                base = links_before(i)
                k = [0]

                def link(ins):
                    k[0] += 1
                    ins.then_inc(dve_link, 1)
                    eng.wait_ge(dve_link, base + k[0])

                def xw_rest(b):
                    eng.wait_ge(xwhi_done, G * i + b + 1)
                    eng.scalar_tensor_tensor(out=xw_lo[:, b % 2, :], in0=XW_BANK[b % 2][:, :],
                                             scalar=XW_SCALE / ADJ_SCALE, in1=xw_hi[:, b % 2, :], op0=ALU.mult, op1=ALU.subtract).then_inc(xwlo_done, 1)

                def add_up(layer, b):
                    m = mix_of(layer, i, b)
                    eng.wait_ge(pe_mix, m + 1)
                    if layer == 0:
                        eng.wait_ge(xb_done, G * i + b + 1)
                        if not (isinstance(i, int) and i == 0):
                            eng.wait_ge((h_done, h_rest)[b // 2], 2 * (i - 1) + b % 2 + 1)
                        scale, other = 1.0 / (XW_SCALE * AN_SCALE), xb[:, b, :]
                    else:
                        eng.wait_ge(ylo_done, 2 * G * i + G * (layer - 1) + b + 1)
                        scale, other = 1.0 / W1_SCALE, (bias1_row, bias2_row)[layer - 1][:, :]
                    eng.scalar_tensor_tensor(out=t_sb[:, b, :], in0=MIX(f"{'ABC'[layer]}{b}")[:, :], scalar=scale,
                                             in1=other, op0=ALU.mult, op1=ALU.add).then_inc(mix_used, 1)

                def measure(layer, b, at=i):
                    eng.wait_ge(mix_used, mix_of(layer, at, b) + 1)
                    eng.bn_stats(stats[:, layer, b, :], t_sb[:, b, :]).then_inc(stat_done, 1)

                def two_sums(layer, b):
                    add_up(layer, b)
                    add_up(layer, b + 1)
                    measure(layer, b)
                    measure(layer, b + 1)

                def refine(row, at, what, source):
                    eng.wait_ge(r0_ready, r_of(at, what) + 1)
                    link(eng.tensor_tensor(r_t[:, row, :], r0[:, row, :], r0[:, row, :], ALU.mult))
                    link(eng.tensor_tensor(r_t[:, row, :], r_t[:, row, :], source, ALU.mult))
                    return eng.scalar_tensor_tensor(out=rstd[:, row, :], in0=r_t[:, row, :], scalar=1.5,
                                                    in1=r0[:, row, :], op0=ALU.add, op1=ALU.mult)

                def variance(layer, of):
                    if layer < 3:
                        eng.wait_ge(stat_done, 3 * G * of + G * (layer + 1))
                    else:
                        eng.wait_ge(st3_done, G * of + G)
                    eng.memset(held[:, 0:1], 0.0)
                    for b in range(G):
                        ins = eng.bn_aggr(mv[:, layer, b, :], stats[:, layer, b, :])
                    link(ins)
                    eng.tensor_scalar(half_var[:, layer, :], mv[:, layer, :, 1], LN_EPS, -0.5, ALU.add,
                                      ALU.mult).then_inc(var_ready, 1)

                def norm(layer, at):
                    link(refine(layer, at, f"ln{layer}", half_var[:, layer, :]))
                    link(eng.scalar_tensor_tensor(out=nmr[:, layer, :], in0=mv[:, layer, :, 0], scalar=-1.0,
                                                  in1=rstd[:, layer, :], op0=ALU.mult, op1=ALU.mult))
                    eng.tensor_copy(r_t[:, layer, 0:1], rstd[:, layer, 0:1]).then_inc(norm_ready, 1)

                def y_low(layer):
                    for b in range(G):
                        eng.wait_ge(yf_done, G * layer + b + 1)
                        eng.wait_ge(yhi_done, G * layer + b + 1)
                        eng.tensor_tensor(y_lo[:, b, :], y_f[:, b, :], y_hi[:, b, :],
                                          ALU.subtract).then_inc(ylo_done, 1)

                def first_iteration():
                    for b in range(G):
                        add_up(0, b)
                        if b + 2 < G:
                            xw_rest(b + 2)
                        measure(0, b)
                    for layer in (1, 2):
                        variance(layer - 1, 0)
                        norm(layer - 1, 0)
                        y_low(layer - 1)
                        two_sums(layer, 0)
                        add_up(layer, 2)
                        add_up(layer, 3)
                        if layer == 1:
                            measure(1, 2)
                            measure(1, 3)
                    assert k[0] == LINKS[0]

                def turned_rest(dst, hi, what, scale):
                    eng.wait_ge(trhi_done, tr_of(i, what) + 1)
                    eng.scalar_tensor_tensor(out=dst, in0=TR_BANK[what][:, :], scalar=scale, in1=hi,
                                             op0=ALU.mult, op1=ALU.subtract).then_inc(tr_used, 1)

                def wide_rest(dst, hi, at, what, scale):
                    eng.wait_ge(widehi_done, wide_of(at, what) + 1)
                    eng.scalar_tensor_tensor(out=dst, in0=WIDE(what)[:, :], scalar=scale, in1=hi,
                                             op0=ALU.mult, op1=ALU.subtract).then_inc(wide_used, 1)

                def yt_rest(which, j):
                    wide_rest(yt_lo[:, which, j, :], yt_hi[:, which, j, :], i, f"{YT[which]}{j}", 1.0 / P_SCALE)

                def u_rest(at, b):
                    wide_rest(u_lo[:, b, :], u_hi[:, b, :], at, f"U{b}", 1.0 / M_SCALE)

                def diagonal_sums(which):
                    eng.wait_ge(gram_done, 2 * g + which + 1)
                    link(eng.tensor_tensor(tiles(diag[:, :]), tiles(gram[:, which, :]), bcast_mid(ident[:, :], G),
                                           ALU.mult))
                    link(eng.tensor_reduce(sq[:, which, :], tiles(diag[:, :]), AX.X, ALU.add))

                def last_sum(b):
                    eng.wait_ge(pe_mix, ku_of(i, b) + 1)
                    if not (isinstance(i, int) and i == 2):
                        eng.wait_ge(o_done, G * (c - 1) + b + 1)
                    eng.scalar_tensor_tensor(out=t3[:, b, :], in0=MIX(f"K{b}")[:, :], scalar=1.0 / K_SCALE,
                                             in1=h_two[par][:, b, :], op0=ALU.mult, op1=ALU.add).then_inc(mix_used, 1)

                def last_measure(b):
                    eng.wait_ge(mix_used, ku_of(i, b) + 1)
                    eng.bn_stats(stats[:, 3, b, :], t3[:, b, :]).then_inc(st3_done, 1)

                if not back and not tail:
                    first_iteration()
                    return
                if front:
                    xw_rest(0)
                if back:
                    measure(2, 2, g)
                    measure(2, 3, g)
                    variance(2, g)
                if front:
                    xw_rest(1)
                if back:
                    norm(2, g)
                if tail:
                    eng.wait_ge(ag_done, c + 1)
                    link(eng.tensor_reduce(deg[:, 0, :], tiles(a_g[:, :]), AX.X, ALU.add))
                    link(eng.tensor_scalar(deg_c[:, 0, :], deg[:, 0, :], NORM_EPS, None, ALU.max))
                    link(eng.reciprocal(inv_deg[:, 0, :], deg_c[:, 0, :]))
                    eng.tensor_scalar(coef[:, 0, :], inv_deg[:, 0, :], gate[:, 7:8], None,
                                      ALU.mult).then_inc(cg_ready, 1)
                    u_rest(i - 1, 2)
                    u_rest(i, 3)
                if front:
                    add_up(0, 0)
                if tail:
                    eng.wait_ge(pe_bc, 2 * c + 2)
                    eng.wait_ge(al_ready, c + 1)
                    eng.tensor_tensor(a_l[:, :], BC_BANK[:, :], a_l[:, :], ALU.mult).then_inc(al_scaled, 1)
                if front:
                    xw_rest(2)
                if tail:
                    eng.wait_ge(al_scaled, c + 1)
                    link(eng.tensor_reduce(deg[:, 1, :], tiles(a_l[:, :]), AX.X, ALU.add))
                    link(eng.tensor_tensor(deg_r[:, :], deg[:, 1, :], rstd[:, 4, :], ALU.mult))
                    link(eng.tensor_scalar(deg_c[:, 1, :], deg_r[:, :], NORM_EPS, None, ALU.max))
                    link(eng.reciprocal(inv_deg[:, 1, :], deg_c[:, 1, :]))
                    link(eng.scalar_tensor_tensor(out=coef[:, 1, :], in0=inv_deg[:, 1, :], scalar=gate[:, 6:7],
                                                  in1=rstd[:, 4, :], op0=ALU.mult, op1=ALU.mult))
                if back:
                    turned_rest(ht_lo[:, 0, :], ht_hi[:, 0, :], "H0", 1.0)
                if front:
                    xw_rest(3)
                if back:
                    turned_rest(ht_lo[:, 1, :], ht_hi[:, 1, :], "H1", 1.0)
                if front:
                    add_up(0, 1)
                if tail:
                    eng.tensor_tensor(tiles(k_l[:, :]), tiles(a_l[:, :]), bcast_last(coef[:, 1, :], P),
                                      ALU.mult).then_inc(kl_done, 1)
                if front:
                    add_up(0, 2)
                if back:
                    for j in TURNS[2]:
                        turned_rest(ht_lo[:, j, :], ht_hi[:, j, :], f"H{j}", 1.0)
                if front:
                    add_up(0, 3)
                    measure(0, 0)
                if tail:
                    turned_rest(kt_lo[:, :], kt_hi[:, :], "K", K_SCALE)
                if back:
                    yt_rest(GRAV, 0)
                if front:
                    measure(0, 1)
                if back:
                    yt_rest(GRAV, 1)
                if tail:
                    last_sum(0)
                if front:
                    measure(0, 2)
                    measure(0, 3)
                if back:
                    yt_rest(GRAV, 2)
                if front:
                    variance(0, i)
                if tail:
                    last_sum(1)
                if front:
                    norm(0, i)
                if back:
                    yt_rest(GRAV, 3)
                if tail:
                    last_sum(2)
                    last_sum(3)
                    last_measure(0)
                    last_measure(1)
                if back:
                    u_rest(i, 0)
                if front:
                    add_up(1, 0)
                    add_up(1, 1)
                    measure(1, 0)
                    measure(1, 1)
                if tail:
                    last_measure(2)
                    last_measure(3)
                if front:
                    add_up(1, 2)
                if back:
                    yt_rest(LANG, 0)
                if front:
                    add_up(1, 3)
                    measure(1, 2)
                    measure(1, 3)
                if back:
                    yt_rest(LANG, 1)
                if front:
                    variance(1, i)
                if back:
                    yt_rest(LANG, 2)
                if front:
                    norm(1, i)
                if back:
                    diagonal_sums(GRAV)
                    eng.scalar_tensor_tensor(out=tiles(half_dist[:, :]), in0=bcast_last(sq[:, 0, :], P), scalar=-1.0,
                                             in1=tiles(gram[:, GRAV, :]), op0=ALU.mult,
                                             op1=ALU.add).then_inc(half_ready, 1)
                    yt_rest(LANG, 3)
                if tail:
                    variance(3, c)
                if back:
                    u_rest(i, 1)
                if tail:
                    norm(3, i)
                if back:
                    eng.wait_ge(pe_bc, 2 * g + 1)
                    eng.wait_ge(half_ready, g + 1)
                    link(eng.tensor_tensor(dist[:, :], BC_BANK[:, :], half_dist[:, :], ALU.add))
                    eng.tensor_scalar(dist[:, :], dist[:, :], 0.0, None, ALU.max).then_inc(dist_done, 1)
                if front:
                    add_up(2, 0)
                    add_up(2, 1)
                if back:
                    diagonal_sums(LANG)
                    eng.tensor_scalar(sq_h[:, :], sq[:, 1, :], NORM_EPS * NORM_EPS / 2, -1.0, ALU.max,
                                      ALU.mult).then_inc(var_ready, 1)
                if front:
                    measure(2, 0)
                    measure(2, 1)
                if back:
                    eng.wait_ge(gram_turned, g + 1)
                    eng.tensor_tensor(diag[:, :], GRAM_BANK[:, :], gram[:, LANG, :],
                                      ALU.add).then_inc(sum_ready, 1)
                if front:
                    add_up(2, 2)
                    add_up(2, 3)
                if back:
                    link(refine(4, i, "lang", sq_h[:, :]))
                    eng.tensor_copy(r_t[:, 4, 0:1], rstd[:, 4, 0:1]).then_inc(norm_ready, 1)
                want = LINKS[0] * front + LINKS[1] * back + LINKS[2] * tail
                assert k[0] == want, (k[0], want, front, back, tail)

            iteration(0, 0, back=False, tail=False)
            iteration(1, 1, tail=False)
            iteration(2, 0)
            iteration(3, 1)
            with eng.Fori(2, NG // 2) as pair:
                iteration(2 * pair, 0)
                iteration(2 * pair + 1, 1)
            iteration(NG, 0, front=False)
            iteration(NG + 1, 1, front=False, back=False)

        @block.gpsimd
        def _(eng):
            eng.memset(zeros[:, :], 0.0).then_inc(const_set, 1)
            eng.memset(ones[:, :], 1.0).then_inc(const_set, 1)
            eng.wait_ge(const_set, 2)
            eng.affine_select(out=ident[:, :], in_=zeros[:, :], compare_op=ALU.not_equal, fill=1.0, base=0,
                              pattern=[[-1, P]], channel_multiplier=1).then_inc(const_set, 1)
            eng.affine_select(out=not_eye[:, :], in_=ones[:, :], compare_op=ALU.not_equal, fill=0.0, base=0,
                              pattern=[[-1, P]], channel_multiplier=1).then_inc(const_set, 1)
            eng.memset(w1_f[:, :], 0.0).then_inc(const_set, 1)

            eng.wait_ge(small_in, 96)
            eng.wait_ge(const_set, 5)
            k = [0]

            def made(ins):
                k[0] += 1
                ins.then_inc(pool_link, 1)
                eng.wait_ge(pool_link, k[0])

            made(eng.tensor_tensor(adj_off[:, :], adj_sb[:, :], not_eye[:, :], ALU.mult))
            made(eng.tensor_scalar(adj_s[:, :], adj_sb[:, :], ADJ_SCALE, 0.0, ALU.mult, ALU.add))
            made(eng.tensor_copy(adj_hi[:, :], adj_s[:, :]))
            eng.tensor_tensor(adj_lo[:, :], adj_s[:, :], adj_hi[:, :], ALU.subtract).then_inc(adj_made, 1)
            made(eng.tensor_tensor(w1_f[:, :], adj_sb[:, :], adj_sb[:, :], ALU.mult))
            made(eng.tensor_tensor(w1_f[:, :], w1_f[:, :], ident[:, :], ALU.add))
            made(eng.tensor_scalar(w1_f[:, :], w1_f[:, :], W1_SCALE, 0.0, ALU.mult, ALU.add))
            made(eng.tensor_copy(w1_hi[:, :], w1_f[:, :]))
            eng.tensor_tensor(w1_lo[:, :], w1_f[:, :], w1_hi[:, :], ALU.subtract).then_inc(adj_made, 1)

            def split_lo(q, b):
                eng.wait_ge(xnhi_done, q * G + b + 1)
                eng.tensor_tensor(xn_part(q, LO, b), xn_f[:, b, :], xn_part(q, HI, b),
                                  ALU.subtract).then_inc(xnlo_done, 1)

            with eng.Fori(0, NG) as q:
                for b in range(G):
                    split_lo(q, b)

            for t in range(T):
                eng.wait_ge(s_copied, t + 1)
                if t >= 1:
                    eng.wait_ge(s_mirrored, t)
                eng.affine_select(out=work[:, t, :], in_=s_sb[:, t, :], compare_op=ALU.not_equal, fill=NEG, base=t * P,
                                  pattern=[[-1, N]], channel_multiplier=1).then_inc(s_diag, 1)
                eng.wait_ge(s_diag, 2 * t + 1)
                c = slice(t * P, (t + 1) * P)
                eng.affine_select(out=s_sb[:, t, c], in_=s_sb[:, t, c], compare_op=ALU.not_equal, fill=0.0, base=0,
                                  pattern=[[-1, P]], channel_multiplier=1).then_inc(s_diag, 1)
            k2 = 0
            for hi, lo in ((pg_hi, pg_lo), (pl_hi, pl_lo), (m_hi, m_lo)):
                for d in range(T):
                    eng.wait_ge(prod_hi, k2 + 1)
                    r = slice(0 if hi is m_hi else d * P, N)
                    eng.tensor_tensor(lo[:, d, r], prod_f[:, k2 % T, r], hi[:, d, r],
                                      ALU.subtract).then_inc(prod_lo, 1)
                    k2 += 1

            def x_rest(g, b, first=False):
                if not first:
                    eng.wait_ge(mix_used, mix_of(0, g - 1, b) + 1)
                eng.wait_ge(xhi_done, G * g + b + 1)
                eng.tensor_tensor(x_lo[:, b, :], x_in[:, b, :], x_hi[:, b, :],
                                  ALU.subtract).then_inc(xlo_done, 1)
                eng.tensor_scalar(xb[:, b, :], x_in[:, b, :], 1.0, bias0_col[:, :], ALU.mult,
                                  ALU.add).then_inc(xb_done, 1)

            def hold(root):
                eng.wait_ge(norm_ready, root + 1)
                eng.tensor_tensor(pool_held[:, :], ones[:, 0:1], ones[:, 0:1], ALU.mult)

            def y_rest(layer, i, first=False):
                hold(r_of(i, f"ln{layer}"))
                for b in range(G):
                    n = 2 * G * i + G * layer + b
                    eng.tensor_scalar(y_f[:, b, :], t_sb[:, b, :], rstd[:, layer, b:b + 1], nmr[:, layer, b:b + 1],
                                      ALU.mult, ALU.add).then_inc(yf_done, 1)
                    if not first:
                        eng.wait_ge(yf_done, n + 1)
                        eng.wait_ge(yhi_done, n + 1)
                        eng.tensor_tensor(y_lo[:, b, :], y_f[:, b, :], y_hi[:, b, :],
                                          ALU.subtract).then_inc(ylo_done, 1)

            def h_rows(i, par):
                hold(r_of(i, "ln2"))
                for b in range(2, G):
                    eng.tensor_scalar(h_two[par][:, b, :], t_sb[:, b, :], rstd[:, 2, b:b + 1], nmr[:, 2, b:b + 1],
                                      ALU.mult, ALU.add).then_inc(h_rest, 1)

            def iteration(i, par, front=True, back=True, tail=True, prep=True):
                g, c = i - 1, i - 2
                if back:
                    h_rows(g, 1 - par)
                if tail:
                    eng.wait_ge(cg_ready, c + 1)
                    eng.tensor_tensor(tiles(k_g[:, :]), tiles(a_g[:, :]), bcast_last(coef[:, 0, :], P),
                                      ALU.mult).then_inc(kg_done, 1)
                    eng.wait_ge(kg_done, c + 1)
                    eng.wait_ge(kl_done, c + 1)
                    eng.tensor_tensor(k_sb[:, :], k_l[:, :], k_g[:, :], ALU.add).then_inc(k_done, 1)
                if front:
                    y_rest(0, i, first=not back)
                if front and prep:
                    for b in range(G):
                        x_rest(i + 1, b)
                if front:
                    y_rest(1, i, first=not back)
                if back:
                    eng.wait_ge(exp_done, g + 1)
                    eng.tensor_tensor(tiles(a_g[:, :]), tiles(expo[:, :]), bcast_mid(adj_off[:, :], G),
                                      ALU.mult).then_inc(ag_done, 1)
                    eng.wait_ge(relu_done, g + 1)
                    eng.tensor_tensor(tiles(a_l[:, :]), tiles(diag[:, :]), bcast_mid(adj_off[:, :], G),
                                      ALU.mult).then_inc(al_ready, 1)

            for b in range(G):
                x_rest(0, b, first=True)
            for t in range(T // 2):
                eng.wait_ge(anhi_done, t + 1)
                eng.tensor_tensor(an_lo[:, t, :], an_f[:, t, :], an_hi[:, t, :],
                                  ALU.subtract).then_inc(an_done_pool, 1)
            iteration(0, 0, back=False, tail=False)
            iteration(1, 1, tail=False)
            iteration(2, 0)
            iteration(3, 1)
            with eng.Fori(2, NG // 2 - 1) as pair:
                iteration(2 * pair, 0)
                iteration(2 * pair + 1, 1)
            iteration(NG - 2, 0)
            iteration(NG - 1, 1, prep=False)
            iteration(NG, 0, front=False)
            iteration(NG + 1, 1, front=False, back=False)


_INS = ['x', 'adj', 'L0_gnn_bias', 'L1_gnn_bias', 'L2_gnn_bias', 'L3_gnn_W_lang', 'L3_gnn_W_grav', 'L3_gnn_W_V',
        'L3_gnn_W_O', 'L3_gnn_gate_logit', 'L3_gnn_log_sigma']
_OUT = (64, 128, 512)


def kernel(**inputs):
    import numpy as np
    import concourse.bacc as bacc
    from concourse.bass_utils import run_bass_kernel_spmd as run

    nc = bacc.Bacc("TRN2", target_bir_lowering=False, num_devices=1)
    arrays, args = {}, []
    for name in _INS:
        a = np.asarray(inputs[name])
        if a.ndim == 0:
            a = a.reshape(1, 1)
        a = np.ascontiguousarray(a)
        arrays[f"in_{name}"] = a
        args.append(nc.dram_tensor(f"in_{name}", a.shape, mybir.dt.from_np(a.dtype), kind="ExternalInput").ap())
    args.append(nc.dram_tensor("out_0", _OUT, F32, kind="ExternalOutput").ap())
    gnn_kernel(nc, *args)
    r = run(nc, [arrays], core_ids=[0])
    return r.results[0]["out_0"]
```
